# Optimizing a Trainium2 kernel written in Bass

```python
import numpy as np
import jax
import jax.numpy as jnp

def _softmax(x, axis=-1):
    return jax.nn.softmax(x, axis=axis)

def _gelu(x):
    return jax.nn.gelu(x, approximate=True)

def _silu(x):
    return jax.nn.silu(x)

def _sigmoid(x):
    return jax.nn.sigmoid(x)

def _layernorm(x, axis=-1, eps=1e-05):
    m = jnp.mean(x, axis=axis, keepdims=True)
    v = jnp.var(x, axis=axis, keepdims=True)
    return (x - m) / jnp.sqrt(v + eps)

def _scatter_add(tgt, idx, src, axis=0):
    return tgt.at[idx].add(src)

def _segment_sum(src, seg, n):
    return jax.ops.segment_sum(src, seg, n)
kernel_name = 'mk_xattn_ffn_d4_seqx_r8_6013e8'

def setup_inputs(seed: int=0):
    np.random.seed(seed)
    _w = jnp.asarray

    def _rec_inputs():
        import jax
        import jax.numpy as jnp
        _rk = jax.random.key(seed)
        x = 7.22e-05 + 1 * jax.random.normal(jax.random.fold_in(_rk, 1), (8, 256, 128), jnp.float32)
        _lenS = 256 - jax.random.randint(jax.random.fold_in(_rk, 7), (8,), 0, max(1, 256 // 4) + 1, jnp.int32)
        _lenS2 = 256 - jax.random.randint(jax.random.fold_in(_rk, 8), (8,), 0, max(1, 256 // 4) + 1, jnp.int32)
        _ctx_768P = jax.random.normal(jax.random.fold_in(_rk, 11), (8, 16, 96), jnp.float32)
        _ctx_768c = jax.random.dirichlet(jax.random.fold_in(_rk, 511), 0.3 * jnp.ones((16,), jnp.float32), (8, 256))
        _ctx_768t = jnp.einsum('bsk,bkd->bsd', _ctx_768c, _ctx_768P)
        _ctx_768t = _ctx_768t * jax.lax.rsqrt(jnp.mean(jnp.square(_ctx_768t)) + 1e-12) * 0.953939
        ctx_768 = -0.000191848 + 0.999787 * (_ctx_768t + 0.3 * jax.random.normal(jax.random.fold_in(_rk, 611), (8, 256, 96), jnp.float32))
        _validS = jnp.arange(256)[None, :] < _lenS[:, None]
        _validS2 = jnp.arange(256)[None, :] < _lenS2[:, None]
        _causal = jnp.tril(jnp.ones((256, 256), dtype=bool))
        mask_1x1xSxS2_bk0 = jnp.logical_not(jnp.broadcast_to(_validS2[0:1, None, None, :], (1, 1, 256, 256)))
        mask_BxS2_bf1 = jnp.ones((8, 256), dtype=bool)
        return (x, ctx_768, mask_1x1xSxS2_bk0, mask_BxS2_bf1)
    x, ctx_768, mask_1x1xSxS2_bk0, mask_BxS2_bf1 = _rec_inputs()

    def _L0_xattn_setup():
        import jax, jax.numpy as jnp
        import numpy as np
        B, T, Q_DIM, KV_DIM = (4, 256, 128, 96)
        HEADS, DIM_HEAD = (16, 64)
        INNER = HEADS * DIM_HEAD
        NUM_FRAMES, NUM_PATCHES = (8, 32)
        LN_EPS = 1e-05

        def diagonal_frame_mask(num_patches, num_frames):
            fid = np.repeat(np.arange(num_frames), num_patches)
            m = fid[:, None] == fid[None, :]
            return jnp.asarray(m[None, None])
        key = jax.random.key(seed)
        ks = jax.random.split(key, 6)
        s = lambda d: 1.0 / np.sqrt(d)
        return {'x': jax.random.normal(ks[0], (B, T, Q_DIM), jnp.float32), 'context': jax.random.normal(ks[1], (B, T, KV_DIM), jnp.float32), 'ln_gamma': jnp.ones((Q_DIM,), jnp.float32), 'ln_beta': jnp.zeros((Q_DIM,), jnp.float32), 'Wq': jax.random.normal(ks[2], (Q_DIM, INNER), jnp.float32) * s(Q_DIM), 'Wkv': jax.random.normal(ks[3], (KV_DIM, 2 * INNER), jnp.float32) * s(KV_DIM), 'Wo': jax.random.normal(ks[4], (INNER, Q_DIM), jnp.float32) * s(INNER), 'bo': jnp.zeros((Q_DIM,), jnp.float32), 'mask': diagonal_frame_mask(NUM_PATCHES, NUM_FRAMES)}
    _L0_xattn_all = _L0_xattn_setup()
    _L0_xattn_in = {k: v for k, v in _L0_xattn_all.items() if k in ('ln_gamma', 'ln_beta', 'Wq', 'Wkv', 'Wo', 'bo')}
    del _L0_xattn_all

    def _L0_ffn_setup():
        import jax, jax.numpy as jnp
        import numpy as np
        EXPERTS = 8
        TOP_K = 2

        def swiglu(x, w1, w2, w3):
            h = x @ w1
            return h * jax.nn.sigmoid(h) * (x @ w2) @ w3
        key = jax.random.key(seed)
        ks = jax.random.split(key, 9)
        B, S, D = (4, 256, 128)
        H = 2 * D
        s = 0.02
        x = jax.random.normal(ks[0], (B, S, D), dtype=jnp.float32)
        gate_w = jax.random.normal(ks[1], (D, EXPERTS), dtype=jnp.float32) * s
        ew1 = jax.random.normal(ks[2], (EXPERTS, D, H), dtype=jnp.float32) * s
        ew2 = jax.random.normal(ks[3], (EXPERTS, D, H), dtype=jnp.float32) * s
        ew3 = jax.random.normal(ks[4], (EXPERTS, H, D), dtype=jnp.float32) * s
        sw1 = jax.random.normal(ks[5], (D, H), dtype=jnp.float32) * s
        sw2 = jax.random.normal(ks[6], (D, H), dtype=jnp.float32) * s
        sw3 = jax.random.normal(ks[7], (H, D), dtype=jnp.float32) * s
        return {'x': x, 'gate_w': gate_w, 'ew1': ew1, 'ew2': ew2, 'ew3': ew3, 'sw1': sw1, 'sw2': sw2, 'sw3': sw3}
    _L0_ffn_all = _L0_ffn_setup()
    _L0_ffn_in = {k: v for k, v in _L0_ffn_all.items() if k in ('gate_w', 'ew1', 'ew2', 'ew3', 'sw1', 'sw2', 'sw3')}
    del _L0_ffn_all

    def _L1_xattn_setup():
        import jax, jax.numpy as jnp
        import numpy as np
        Q_DIM = 128
        KV_DIM = 96
        HEADS = 16
        DK = Q_DIM // HEADS
        key = jax.random.key(seed)
        ks = jax.random.split(key, 6)
        B, T_q, T_kv = (4, 256, 256)
        s_q = 1.0 / np.sqrt(Q_DIM)
        s_kv = 1.0 / np.sqrt(KV_DIM)
        return {'q_tokens': jax.random.normal(ks[0], (B, T_q, Q_DIM), jnp.float32), 'kv_tokens': jax.random.normal(ks[1], (B, T_kv, KV_DIM), jnp.float32), 'Wq': jax.random.normal(ks[2], (Q_DIM, Q_DIM), jnp.float32) * s_q, 'Wk': jax.random.normal(ks[3], (Q_DIM, KV_DIM), jnp.float32) * s_kv, 'Wv': jax.random.normal(ks[4], (Q_DIM, KV_DIM), jnp.float32) * s_kv, 'Wo': jax.random.normal(ks[5], (Q_DIM, Q_DIM), jnp.float32) * s_q}
    _L1_xattn_all = _L1_xattn_setup()
    _L1_xattn_in = {k: v for k, v in _L1_xattn_all.items() if k in ('Wq', 'Wk', 'Wv', 'Wo')}
    del _L1_xattn_all

    def _L1_ffn_setup():
        import jax, jax.numpy as jnp
        import numpy as np
        B, S, D = (4, 256, 128)
        E, F = (8, 512)
        key = jax.random.key(seed)
        ks = jax.random.split(key, 5)
        x = jax.random.normal(ks[0], (B, S, D), dtype=jnp.float32)
        switch_w = jax.random.normal(ks[1], (D, E), dtype=jnp.float32) * D ** (-0.5)
        switch_b = jnp.zeros((E,), dtype=jnp.float32)
        w1 = jax.random.normal(ks[2], (E, D, F), dtype=jnp.float32) * D ** (-0.5)
        b1 = jnp.zeros((E, F), dtype=jnp.float32)
        w2 = jax.random.normal(ks[3], (E, F, D), dtype=jnp.float32) * F ** (-0.5)
        b2 = jnp.zeros((E, D), dtype=jnp.float32)
        return {'x': x, 'switch_w': switch_w, 'switch_b': switch_b, 'w1': w1, 'b1': b1, 'w2': w2, 'b2': b2}
    _L1_ffn_all = _L1_ffn_setup()
    _L1_ffn_in = {k: v for k, v in _L1_ffn_all.items() if k in ('switch_w', 'switch_b', 'w1', 'b1', 'w2', 'b2')}
    del _L1_ffn_all

    def _L2_xattn_setup():
        import jax, jax.numpy as jnp
        import numpy as np
        IMG_DIM, TXT_DIM, HID = (128, 96, 128)
        B, LQ, LK = (8, 256, 256)
        key = jax.random.key(seed)
        ks = jax.random.split(key, 8)
        s_img = 1.0 / np.sqrt(IMG_DIM)
        s_txt = 1.0 / np.sqrt(TXT_DIM)
        return {'image_features': jax.random.normal(ks[0], (B, LQ, IMG_DIM), jnp.float32), 'text_features': jax.random.normal(ks[1], (B, LK, TXT_DIM), jnp.float32), 'Wq': jax.random.uniform(ks[2], (IMG_DIM, HID), jnp.float32, -s_img, s_img), 'bq': jax.random.uniform(ks[3], (HID,), jnp.float32, -s_img, s_img), 'Wk': jax.random.uniform(ks[4], (TXT_DIM, HID), jnp.float32, -s_txt, s_txt), 'bk': jax.random.uniform(ks[5], (HID,), jnp.float32, -s_txt, s_txt), 'Wv': jax.random.uniform(ks[6], (TXT_DIM, HID), jnp.float32, -s_txt, s_txt), 'bv': jax.random.uniform(ks[7], (HID,), jnp.float32, -s_txt, s_txt)}
    _L2_xattn_all = _L2_xattn_setup()
    _L2_xattn_in = {k: v for k, v in _L2_xattn_all.items() if k in ('Wq', 'bq', 'Wk', 'bk', 'Wv', 'bv')}
    del _L2_xattn_all

    def _L2_ffn_setup():
        import jax, jax.numpy as jnp
        import numpy as np
        DIM = 128
        HIDDEN = 352
        NUM_EXPERTS = 8
        TOP_K = 2
        BATCH, SEQ = (4, 256)
        key = jax.random.key(seed)
        ks = jax.random.split(key, 5)
        x = jax.random.normal(ks[0], (BATCH, SEQ, DIM), dtype=jnp.float32)
        gate_w = jax.random.normal(ks[1], (NUM_EXPERTS, DIM), dtype=jnp.float32) * 0.02
        w1 = jax.random.normal(ks[2], (NUM_EXPERTS, HIDDEN, DIM), dtype=jnp.float32) * 0.02
        w3 = jax.random.normal(ks[3], (NUM_EXPERTS, HIDDEN, DIM), dtype=jnp.float32) * 0.02
        w2 = jax.random.normal(ks[4], (NUM_EXPERTS, DIM, HIDDEN), dtype=jnp.float32) * 0.02
        return {'x': x, 'gate_w': gate_w, 'w1': w1, 'w3': w3, 'w2': w2}
    _L2_ffn_all = _L2_ffn_setup()
    _L2_ffn_in = {k: v for k, v in _L2_ffn_all.items() if k in ('gate_w', 'w1', 'w3', 'w2')}
    del _L2_ffn_all

    def _L3_xattn_setup():
        import jax, jax.numpy as jnp
        import numpy as np
        import math
        B, N, M = (4, 128, 128)
        DIM, CTX_DIM = (128, 96)
        HEADS, DIM_HEAD = (16, 64)
        INNER = HEADS * DIM_HEAD

        def layer_norm(t, g, eps=1e-05):
            mean = jnp.mean(t, axis=-1, keepdims=True)
            var = jnp.mean((t - mean) ** 2, axis=-1, keepdims=True)
            return (t - mean) * jax.lax.rsqrt(var + eps) * g
        key = jax.random.key(seed)
        ks = jax.random.split(key, 8)
        return {'x': jax.random.normal(ks[0], (B, N, DIM), jnp.float32), 'context': jax.random.normal(ks[1], (B, M, CTX_DIM), jnp.float32), 'mask': jnp.ones((B, M), dtype=bool), 'g_norm': jnp.ones((DIM,), jnp.float32), 'null_kv': jax.random.normal(ks[2], (2, DIM_HEAD), jnp.float32), 'Wq': jax.random.normal(ks[3], (DIM, INNER), jnp.float32) * DIM ** (-0.5), 'Wkv': jax.random.normal(ks[4], (CTX_DIM, 2 * INNER), jnp.float32) * CTX_DIM ** (-0.5), 'Wout': jax.random.normal(ks[5], (INNER, DIM), jnp.float32) * INNER ** (-0.5), 'g_out': jnp.ones((DIM,), jnp.float32)}
    _L3_xattn_all = _L3_xattn_setup()
    _L3_xattn_in = {k: v for k, v in _L3_xattn_all.items() if k in ('g_norm', 'null_kv', 'Wq', 'Wkv', 'Wout', 'g_out')}
    del _L3_xattn_all

    def _L3_ffn_setup():
        import jax, jax.numpy as jnp
        import numpy as np
        BITS = 8
        LORA_RANK = 16
        LORA_ALPHA = 32
        SCALING = LORA_ALPHA / LORA_RANK

        def fake_quant_weight(w, bits=BITS):
            qmax = 2.0 ** (bits - 1) - 1
            scale = jnp.max(jnp.abs(w)) / qmax
            wq = jnp.clip(jnp.round(w / scale), -qmax - 1, qmax) * scale
            return w + jax.lax.stop_gradient(wq - w)

        def qat_lora_linear(x, W, b, A, B):
            Wq = fake_quant_weight(W)
            base = jnp.einsum('bsi,oi->bso', x, Wq) + b
            lora = jnp.einsum('bsr,or->bso', jnp.einsum('bsi,ri->bsr', x, A), B)
            return base + SCALING * lora
        key = jax.random.key(seed)
        ks = jax.random.split(key, 9)
        d, f = (128, 512)
        s_in = 1.0 / np.sqrt(d)
        s_ff = 1.0 / np.sqrt(f)
        return {'hidden_states': jax.random.normal(ks[0], (4, 256, d), jnp.float32), 'W_fc': jax.random.normal(ks[1], (f, d), jnp.float32) * s_in, 'b_fc': jnp.zeros((f,), jnp.float32), 'A_fc': jax.random.normal(ks[2], (LORA_RANK, d), jnp.float32) * s_in, 'B_fc': jnp.zeros((f, LORA_RANK), jnp.float32), 'W_proj': jax.random.normal(ks[3], (d, f), jnp.float32) * s_ff, 'b_proj': jnp.zeros((d,), jnp.float32), 'A_proj': jax.random.normal(ks[4], (LORA_RANK, f), jnp.float32) * s_ff, 'B_proj': jnp.zeros((d, LORA_RANK), jnp.float32)}
    _L3_ffn_all = _L3_ffn_setup()
    _L3_ffn_in = {k: v for k, v in _L3_ffn_all.items() if k in ('W_fc', 'b_fc', 'A_fc', 'B_fc', 'W_proj', 'b_proj', 'A_proj', 'B_proj')}
    del _L3_ffn_all
    return {'x': x, 'ctx_768': ctx_768, 'mask_1x1xSxS2_bk0': mask_1x1xSxS2_bk0, 'mask_BxS2_bf1': mask_BxS2_bf1, 'L0_xattn_ln_gamma': _L0_xattn_in['ln_gamma'], 'L0_xattn_ln_beta': _L0_xattn_in['ln_beta'], 'L0_xattn_Wq': _L0_xattn_in['Wq'], 'L0_xattn_Wkv': _L0_xattn_in['Wkv'], 'L0_xattn_Wo': _L0_xattn_in['Wo'], 'L0_xattn_bo': _L0_xattn_in['bo'], 'L0_ffn_gate_w': _L0_ffn_in['gate_w'], 'L0_ffn_ew1': _L0_ffn_in['ew1'], 'L0_ffn_ew2': _L0_ffn_in['ew2'], 'L0_ffn_ew3': _L0_ffn_in['ew3'], 'L0_ffn_sw1': _L0_ffn_in['sw1'], 'L0_ffn_sw2': _L0_ffn_in['sw2'], 'L0_ffn_sw3': _L0_ffn_in['sw3'], 'L1_xattn_Wq': _L1_xattn_in['Wq'], 'L1_xattn_Wk': _L1_xattn_in['Wk'], 'L1_xattn_Wv': _L1_xattn_in['Wv'], 'L1_xattn_Wo': _L1_xattn_in['Wo'], 'L1_ffn_switch_w': _L1_ffn_in['switch_w'], 'L1_ffn_switch_b': _L1_ffn_in['switch_b'], 'L1_ffn_w1': _L1_ffn_in['w1'], 'L1_ffn_b1': _L1_ffn_in['b1'], 'L1_ffn_w2': _L1_ffn_in['w2'], 'L1_ffn_b2': _L1_ffn_in['b2'], 'L2_xattn_Wq': _L2_xattn_in['Wq'], 'L2_xattn_bq': _L2_xattn_in['bq'], 'L2_xattn_Wk': _L2_xattn_in['Wk'], 'L2_xattn_bk': _L2_xattn_in['bk'], 'L2_xattn_Wv': _L2_xattn_in['Wv'], 'L2_xattn_bv': _L2_xattn_in['bv'], 'L2_ffn_gate_w': _L2_ffn_in['gate_w'], 'L2_ffn_w1': _L2_ffn_in['w1'], 'L2_ffn_w3': _L2_ffn_in['w3'], 'L2_ffn_w2': _L2_ffn_in['w2'], 'L3_xattn_g_norm': _L3_xattn_in['g_norm'], 'L3_xattn_null_kv': _L3_xattn_in['null_kv'], 'L3_xattn_Wq': _L3_xattn_in['Wq'], 'L3_xattn_Wkv': _L3_xattn_in['Wkv'], 'L3_xattn_Wout': _L3_xattn_in['Wout'], 'L3_xattn_g_out': _L3_xattn_in['g_out'], 'L3_ffn_W_fc': _L3_ffn_in['W_fc'], 'L3_ffn_b_fc': _L3_ffn_in['b_fc'], 'L3_ffn_A_fc': _L3_ffn_in['A_fc'], 'L3_ffn_B_fc': _L3_ffn_in['B_fc'], 'L3_ffn_W_proj': _L3_ffn_in['W_proj'], 'L3_ffn_b_proj': _L3_ffn_in['b_proj'], 'L3_ffn_A_proj': _L3_ffn_in['A_proj'], 'L3_ffn_B_proj': _L3_ffn_in['B_proj']}

def reference(x, ctx_768, mask_1x1xSxS2_bk0, mask_BxS2_bf1, L0_xattn_ln_gamma, L0_xattn_ln_beta, L0_xattn_Wq, L0_xattn_Wkv, L0_xattn_Wo, L0_xattn_bo, L0_ffn_gate_w, L0_ffn_ew1, L0_ffn_ew2, L0_ffn_ew3, L0_ffn_sw1, L0_ffn_sw2, L0_ffn_sw3, L1_xattn_Wq, L1_xattn_Wk, L1_xattn_Wv, L1_xattn_Wo, L1_ffn_switch_w, L1_ffn_switch_b, L1_ffn_w1, L1_ffn_b1, L1_ffn_w2, L1_ffn_b2, L2_xattn_Wq, L2_xattn_bq, L2_xattn_Wk, L2_xattn_bk, L2_xattn_Wv, L2_xattn_bv, L2_ffn_gate_w, L2_ffn_w1, L2_ffn_w3, L2_ffn_w2, L3_xattn_g_norm, L3_xattn_null_kv, L3_xattn_Wq, L3_xattn_Wkv, L3_xattn_Wout, L3_xattn_g_out, L3_ffn_W_fc, L3_ffn_b_fc, L3_ffn_A_fc, L3_ffn_B_fc, L3_ffn_W_proj, L3_ffn_b_proj, L3_ffn_A_proj, L3_ffn_B_proj):
    import jax
    import jax.numpy as jnp

    def _L0_xattn_ref(x, context, ln_gamma, ln_beta, Wq, Wkv, Wo, bo, mask):
        import jax, jax.numpy as jnp
        import numpy as np
        B, T, Q_DIM, KV_DIM = (4, 256, 128, 96)
        HEADS, DIM_HEAD = (16, 64)
        INNER = HEADS * DIM_HEAD
        NUM_FRAMES, NUM_PATCHES = (8, 32)
        LN_EPS = 1e-05

        def diagonal_frame_mask(num_patches, num_frames):
            fid = np.repeat(np.arange(num_frames), num_patches)
            m = fid[:, None] == fid[None, :]
            return jnp.asarray(m[None, None])
        mu = jnp.mean(x, axis=-1, keepdims=True)
        var = jnp.mean(jnp.square(x - mu), axis=-1, keepdims=True)
        xn = (x - mu) * jax.lax.rsqrt(var + LN_EPS) * ln_gamma + ln_beta
        scale = DIM_HEAD ** (-0.5)
        q = xn @ Wq
        kv = context @ Wkv
        k, v = jnp.split(kv, 2, axis=-1)
        split_heads = lambda t: t.reshape(t.shape[0], t.shape[1], HEADS, DIM_HEAD).transpose(0, 2, 1, 3)
        q, k, v = (split_heads(q), split_heads(k), split_heads(v))
        dots = jnp.einsum('bhnd,bhmd->bhnm', q, k) * scale
        dots = jnp.where(mask, dots, -jnp.inf)
        attn = jax.nn.softmax(dots, axis=-1)
        out = jnp.einsum('bhnm,bhmd->bhnd', attn, v)
        out = out.transpose(0, 2, 1, 3).reshape(x.shape[0], x.shape[1], INNER)
        return out @ Wo + bo

    def _L0_ffn_ref(x, gate_w, ew1, ew2, ew3, sw1, sw2, sw3):
        import jax, jax.numpy as jnp
        import numpy as np
        EXPERTS = 8
        TOP_K = 2

        def swiglu(x, w1, w2, w3):
            h = x @ w1
            return h * jax.nn.sigmoid(h) * (x @ w2) @ w3
        B, S, D = x.shape
        gate_out = x @ gate_w
        top_v, top_i = jax.lax.top_k(gate_out, TOP_K)
        masked = jnp.full_like(gate_out, -1e+20)
        bi = jnp.arange(B)[:, None, None]
        si = jnp.arange(S)[None, :, None]
        masked = masked.at[bi, si, top_i].set(top_v)
        probs = jax.nn.softmax(masked, axis=-1)
        chosen = jnp.zeros_like(gate_out, dtype=bool).at[bi, si, top_i].set(True)
        w = jnp.where(chosen, probs, 0.0)

        def one_expert(w1, w2, w3, we):
            return swiglu(x, w1, w2, w3) * we[..., None]
        out = jax.vmap(one_expert, in_axes=(0, 0, 0, 2))(ew1, ew2, ew3, w).sum(0)
        out = out + swiglu(x, sw1, sw2, sw3)
        return out

    def _L1_xattn_ref(q_tokens, kv_tokens, Wq, Wk, Wv, Wo):
        import jax, jax.numpy as jnp
        import numpy as np
        Q_DIM = 128
        KV_DIM = 96
        HEADS = 16
        DK = Q_DIM // HEADS
        B, T_q, _ = q_tokens.shape
        T_kv = kv_tokens.shape[1]
        q = q_tokens @ Wq.T
        k = kv_tokens @ Wk.T
        v = kv_tokens @ Wv.T
        q = q.reshape(B, T_q, HEADS, DK).transpose(0, 2, 1, 3)
        k = k.reshape(B, T_kv, HEADS, DK).transpose(0, 2, 1, 3)
        v = v.reshape(B, T_kv, HEADS, DK).transpose(0, 2, 1, 3)
        scale = 1.0 / jnp.sqrt(jnp.asarray(DK, q.dtype))
        attn = jnp.einsum('bhqd,bhkd->bhqk', q, k) * scale
        attn = jax.nn.softmax(attn, axis=-1)
        out = jnp.einsum('bhqk,bhkd->bhqd', attn, v)
        out = out.transpose(0, 2, 1, 3).reshape(B, T_q, Q_DIM)
        return out @ Wo.T

    def _L1_ffn_ref(x, switch_w, switch_b, w1, b1, w2, b2):
        import jax, jax.numpy as jnp
        import numpy as np
        B, S, D = (4, 256, 128)
        E, F = (8, 512)
        b, s, d = x.shape
        t = x.reshape(-1, d)
        logits = t @ switch_w + switch_b
        route_prob = jax.nn.softmax(logits, axis=-1)
        route_prob_max = jnp.max(route_prob, axis=-1)
        routes = jnp.argmax(route_prob, axis=-1)
        out = jnp.zeros_like(t)
        n_experts = w1.shape[0]
        for e in range(n_experts):
            h = jax.nn.gelu(t @ w1[e] + b1[e])
            y = h @ w2[e] + b2[e]
            mask = (routes == e)[:, None]
            out = jnp.where(mask, y, out)
        out = out * route_prob_max[:, None]
        return out.reshape(b, s, d)

    def _L2_xattn_ref(image_features, text_features, Wq, bq, Wk, bk, Wv, bv):
        import jax, jax.numpy as jnp
        import numpy as np
        IMG_DIM, TXT_DIM, HID = (128, 96, 128)
        B, LQ, LK = (8, 256, 256)
        query = jnp.einsum('bqi,ih->bqh', image_features, Wq) + bq
        key = jnp.einsum('bkt,th->bkh', text_features, Wk) + bk
        value = jnp.einsum('bkt,th->bkh', text_features, Wv) + bv
        scale = 1.0 / jnp.sqrt(jnp.asarray(HID, query.dtype))
        scores = jnp.einsum('bqh,bkh->bqk', query, key) * scale
        weights = jax.nn.softmax(scores, axis=-1)
        attended = jnp.einsum('bqk,bkh->bqh', weights, value)
        return attended

    def _L2_ffn_ref(x, gate_w, w1, w3, w2):
        import jax, jax.numpy as jnp
        import numpy as np
        DIM = 128
        HIDDEN = 352
        NUM_EXPERTS = 8
        TOP_K = 2
        BATCH, SEQ = (4, 256)
        orig_shape = x.shape
        xf = x.reshape(-1, x.shape[-1])
        T = xf.shape[0]
        E, K = (gate_w.shape[0], TOP_K)
        scores = jax.nn.softmax(xf @ gate_w.T, axis=-1)
        expert_weights, expert_indices = jax.lax.top_k(scores, K)
        expert_weights = expert_weights / jnp.sum(expert_weights, axis=-1, keepdims=True)
        x_rep = jnp.repeat(xf, K, axis=0)
        flat_idx = expert_indices.reshape(-1)
        y = jnp.zeros_like(x_rep)
        for e in range(E):
            m = (flat_idx == e)[:, None]
            xe = jnp.where(m, x_rep, 0.0)
            h = jax.nn.silu(xe @ w1[e].T) * (xe @ w3[e].T)
            out = h @ w2[e].T
            y = y + jnp.where(m, out, 0.0)
        y = jnp.sum(y.reshape(T, K, -1) * expert_weights[..., None], axis=1)
        return y.reshape(orig_shape)

    def _L3_xattn_ref(x, context, mask, g_norm, null_kv, Wq, Wkv, Wout, g_out):
        import jax, jax.numpy as jnp
        import numpy as np
        import math
        B, N, M = (4, 128, 128)
        DIM, CTX_DIM = (128, 96)
        HEADS, DIM_HEAD = (16, 64)
        INNER = HEADS * DIM_HEAD

        def layer_norm(t, g, eps=1e-05):
            mean = jnp.mean(t, axis=-1, keepdims=True)
            var = jnp.mean((t - mean) ** 2, axis=-1, keepdims=True)
            return (t - mean) * jax.lax.rsqrt(var + eps) * g
        b = x.shape[0]
        scale = DIM_HEAD ** (-0.5)
        sqrt_scale = math.sqrt(scale)
        x = layer_norm(x, g_norm)
        q = x @ Wq
        kv = context @ Wkv
        k, v = jnp.split(kv, 2, axis=-1)

        def to_heads(t):
            return t.reshape(b, t.shape[1], HEADS, DIM_HEAD).transpose(0, 2, 1, 3)
        q, k, v = (to_heads(q), to_heads(k), to_heads(v))
        nk = jnp.broadcast_to(null_kv[0], (b, HEADS, 1, DIM_HEAD))
        nv = jnp.broadcast_to(null_kv[1], (b, HEADS, 1, DIM_HEAD))
        k = jnp.concatenate([nk, k], axis=2)
        v = jnp.concatenate([nv, v], axis=2)
        q = q * sqrt_scale
        k = k * sqrt_scale
        sim = jnp.einsum('bhid,bhjd->bhij', q, k)
        max_neg = -jnp.finfo(sim.dtype).max
        full_mask = jnp.pad(mask, ((0, 0), (1, 0)), constant_values=True)
        sim = jnp.where(full_mask[:, None, None, :], sim, max_neg)
        attn = jax.nn.softmax(sim.astype(jnp.float32), axis=-1).astype(sim.dtype)
        out = jnp.einsum('bhij,bhjd->bhid', attn, v)
        out = out.transpose(0, 2, 1, 3).reshape(b, -1, INNER)
        out = out @ Wout
        return layer_norm(out, g_out)

    def _L3_ffn_ref(hidden_states, W_fc, b_fc, A_fc, B_fc, W_proj, b_proj, A_proj, B_proj):
        import jax, jax.numpy as jnp
        import numpy as np
        BITS = 8
        LORA_RANK = 16
        LORA_ALPHA = 32
        SCALING = LORA_ALPHA / LORA_RANK

        def fake_quant_weight(w, bits=BITS):
            qmax = 2.0 ** (bits - 1) - 1
            scale = jnp.max(jnp.abs(w)) / qmax
            wq = jnp.clip(jnp.round(w / scale), -qmax - 1, qmax) * scale
            return w + jax.lax.stop_gradient(wq - w)

        def qat_lora_linear(x, W, b, A, B):
            Wq = fake_quant_weight(W)
            base = jnp.einsum('bsi,oi->bso', x, Wq) + b
            lora = jnp.einsum('bsr,or->bso', jnp.einsum('bsi,ri->bsr', x, A), B)
            return base + SCALING * lora
        h = qat_lora_linear(hidden_states, W_fc, b_fc, A_fc, B_fc)
        h = jax.nn.gelu(h, approximate=False)
        h = qat_lora_linear(h, W_proj, b_proj, A_proj, B_proj)
        return h
    x = x + _L0_xattn_ref(_layernorm(x, axis=-1), ctx_768, L0_xattn_ln_gamma, L0_xattn_ln_beta, L0_xattn_Wq, L0_xattn_Wkv, L0_xattn_Wo, L0_xattn_bo, mask_1x1xSxS2_bk0)
    x = x + _L0_ffn_ref(_layernorm(x, axis=-1), L0_ffn_gate_w, L0_ffn_ew1, L0_ffn_ew2, L0_ffn_ew3, L0_ffn_sw1, L0_ffn_sw2, L0_ffn_sw3)
    x = x + _L1_xattn_ref(_layernorm(x, axis=-1), ctx_768, L1_xattn_Wq, L1_xattn_Wk, L1_xattn_Wv, L1_xattn_Wo)
    x = x + _L1_ffn_ref(_layernorm(x, axis=-1), L1_ffn_switch_w, L1_ffn_switch_b, L1_ffn_w1, L1_ffn_b1, L1_ffn_w2, L1_ffn_b2)
    x = x + _L2_xattn_ref(_layernorm(x, axis=-1), ctx_768, L2_xattn_Wq, L2_xattn_bq, L2_xattn_Wk, L2_xattn_bk, L2_xattn_Wv, L2_xattn_bv)
    x = x + _L2_ffn_ref(_layernorm(x, axis=-1), L2_ffn_gate_w, L2_ffn_w1, L2_ffn_w3, L2_ffn_w2)
    x = x + _L3_xattn_ref(_layernorm(x, axis=-1), ctx_768, mask_BxS2_bf1, L3_xattn_g_norm, L3_xattn_null_kv, L3_xattn_Wq, L3_xattn_Wkv, L3_xattn_Wout, L3_xattn_g_out)
    x = x + _L3_ffn_ref(_layernorm(x, axis=-1), L3_ffn_W_fc, L3_ffn_b_fc, L3_ffn_A_fc, L3_ffn_B_fc, L3_ffn_W_proj, L3_ffn_b_proj, L3_ffn_A_proj, L3_ffn_B_proj)
    return x

_drawn_inputs = setup_inputs


def setup_inputs(seed=0):
    import zlib

    import numpy as np

    out = dict(_drawn_inputs(seed))
    spreads = {'L0_xattn_ln_gamma': (1.0, 0.2),
     'L0_xattn_ln_beta': (0.0, 0.287),
     'L0_xattn_bo': (0.0, 0.1),
     'L1_ffn_switch_b': (0.0, 0.1),
     'L1_ffn_b1': (0.0, 0.478),
     'L1_ffn_b2': (0.0, 0.32),
     'L3_xattn_g_norm': (1.0, 0.2),
     'L3_xattn_g_out': (1.0, 0.2),
     'L3_ffn_b_fc': (0.0, 0.615),
     'L3_ffn_B_fc': (0.0, 0.1),
     'L3_ffn_b_proj': (0.0, 0.535),
     'L3_ffn_B_proj': (0.0, 0.1)}
    factors = {'L0_ffn_gate_w': 7.838,
     'L0_ffn_ew1': 6.551,
     'L0_ffn_ew2': 6.934,
     'L0_ffn_ew3': 6.459,
     'L0_ffn_sw1': 5.705,
     'L0_ffn_sw2': 5.852,
     'L0_ffn_sw3': 6.205,
     'L2_xattn_bq': 8.0,
     'L2_xattn_bk': 64.0,
     'L2_ffn_gate_w': 8.0,
     'L2_ffn_w1': 8.0,
     'L2_ffn_w3': 8.0,
     'L2_ffn_w2': 8.0,
     'L3_xattn_null_kv': 5.494}
    for name, (base, spread) in spreads.items():
        noise = np.random.default_rng([zlib.crc32(name.encode()), seed]).standard_normal(out[name].shape)
        drawn = base * np.exp(spread * noise) if base else spread * noise
        out[name] = jnp.asarray(drawn.astype(out[name].dtype))
    for name, factor in factors.items():
        out[name] = (out[name] * factor).astype(out[name].dtype)
    return out
```

```python
from contextlib import ExitStack

import numpy as np

import concourse.bass as bass
from concourse import mybir

F32 = mybir.dt.float32
BF16 = mybir.dt.bfloat16
U32 = mybir.dt.uint32
U8 = mybir.dt.uint8
ALU = mybir.AluOpType
ACT = mybir.ActivationFunctionType
AX = mybir.AxisListType
RMAX = bass.bass_isa.ReduceOp.max

P = 128
B, S, D = 8, 256, 128
T = B * S
NT = T // P
DC = 96
EPS = 1e-5
MASKED = -3e38
CH = 512
NCH = T // CH
ROUND = 12582912.0

V_B1, V_BFC, V_GAMMA, V_BETA, V_GNORM, V_BQ, V_BK, V_GATE2, V_N = 0, 32, 36, 37, 38, 39, 40, 41, 49

class Attention:
    def __init__(self, n, nh, dh, scale, pieces, mask, null):
        self.n, self.nh, self.dh, self.scale = n, nh, dh, scale
        self.pieces, self.mask, self.null = pieces, mask, null


class FeedForward:
    def __init__(self, n, E, routed, FT, last, gated, k):
        self.n, self.E, self.routed, self.FT, self.last, self.gated, self.k = n, E, routed, FT, last, gated, k
        self.U = (8 if n == 1 else E) * FT


class Counted:

    def __init__(self, sem, base):
        self.sem, self.base = sem, base


class Ring:

    def __init__(self, filled, act, dve):
        self.filled, self.act, self.dve = filled, act, dve


class AttentionSems:
    def __init__(self, c):
        self.ring = Ring(c["filled"], c["act"], c["dve"])
        self.scores, self.negmax, self.exp, self.turn = c["scores"], c["negmax"], c["exp"], c["turn"]
        self.pt = [c["pt0"], c["pt1"]]
        self.av, self.norm, self.stats, self.yn = c["av"], c["norm"], c["stats"], c["yn"]
        self.ctxb, self.qm, self.ostats, self.onorm = c["ctxb"], c["qm"], c["ostats"], c["onorm"]


class FeedForwardSems:
    def __init__(self, c):
        self.h, self.silu, self.g, self.y, self.acc = c["h"], c["silu"], c["g"], c["y"], c["acc"]
        self.stats, self.yn, self.lnf, self.lne = c["stats"], c["yn"], c["lnf"], c["lne"]
        self.gt, self.gte, self.gl, self.gle = c["gt"], c["gte"], c["gl"], c["gle"]
        self.gd, self.gx, self.w, self.wt, self.wte = c["gd"], c["gx"], c["w"], c["wt"], c["wte"]


ATT = [
    Attention(n=0, nh=16, dh=64, scale=0.125, pieces=8, mask="full", null=False),
    Attention(n=1, nh=16, dh=8, scale=8.0 ** -0.5, pieces=1, mask=None, null=False),
    Attention(n=2, nh=8, dh=128, scale=128.0 ** -0.5, pieces=0, mask=None, null=False),
    Attention(n=3, nh=16, dh=64, scale=0.125, pieces=9, mask="key", null=True),
]
FFN = [
    FeedForward(n=0, E=9, routed=8, FT=2, last=128, gated=True, k=2),
    FeedForward(n=1, E=9, routed=8, FT=4, last=128, gated=False, k=1),
    FeedForward(n=2, E=8, routed=8, FT=3, last=96, gated=True, k=2),
    FeedForward(n=3, E=1, routed=0, FT=4, last=128, gated=False, k=0),
]

BATCH_FILLS = {0: 18, 1: 6, 3: 22}


def att_schedule(A, first, last):
    st = []
    for i in range(A.nh):
        st += [("scores", i), ("softmax", i)]
        if i >= 1:
            st.append(("turn", i - 1))
        if i >= 3:
            st.append(("av", i - 3))
            if (i - 3) % 2:
                st.append(("norm", (i - 3) // 2))
        if i == 4 and not first and A.null:
            st.append(("resid2", 0))
        if i == 7 and not first:
            st.append(("ln", 0))
        if A.pieces >= 8 and i in (8, 12):
            st.append(("outT", i // 4 - 2))
    wide = A.pieces >= 8
    q = [] if last else [("q", j) for j in range(4 if wide else 1)]
    k = [] if last else [("k", j) for j in range(4 if wide else 1)]
    v = [] if last else [("v", j) for j in range(4 if wide else 1)]
    sn = [] if last or not A.null else [("sn", 0), ("snt", 0)]
    st += [("av", 13), ("norm", 6)] + q[:2] + [("turn", 15)] + q[2:]
    if wide:
        st.append(("outT", 2))
    st += [("av", 14)] + k[:2] + [("av", 15), ("norm", 7)] + k[2:] + sn
    st += [("outT", 3), ("outT", 4)] if A.null else [("outT", 3 if wide else 0)]
    if A.null:
        return st + [("wo", 0), ("resid", 0), ("wo", 1)] + v
    return st + (v[:1] or [("wo", 1)]) + [("wo", 0), ("resid", 0)] + v[1:]


def att_prologue(A):
    wide = A.pieces >= 8
    n = 4 if wide else 1
    st = [("q", j) for j in range(n)] + [("k", j) for j in range(n)]
    st += [("sn", 0), ("snt", 0)] if A.null else []
    return st + [("v", j) for j in range(n)]


def single_schedule(A):
    st = [("q", j) for j in range(4)] + [("k", j) for j in range(4)] + [("v", j) for j in range(4)]
    for i in range(A.nh + 4):
        if i < A.nh:
            st += [("scores", i), ("softmax", i)]
        if 1 <= i <= A.nh:
            st.append(("turn", i - 1))
        if 2 <= i <= A.nh + 1:
            st += [("av", i - 2), ("norm", i - 2)]
        if 4 <= i:
            st.append(("ln", i - 4))
    return st


def kind_steps(A, kinds):
    if kinds == "single":
        return single_schedule(A)
    if kinds == "prologue":
        return att_prologue(A)
    if kinds == "epilogue":
        return ([("resid2", 0)] if A.null else []) + [("ln", 0)]
    return att_schedule(A, kinds == "first", kinds == "last")


FILLS = ("q", "k", "v", "sn", "snt", "outT", "wo", "ln")


def ffn_schedule(F, first):
    st = []
    if F.k:
        st.append(("gate", 0))
    for e in range(F.E):
        if e * F.FT < F.U:
            for ft in range(F.FT):
                st.append(("up", (e, ft)))
                if F.k and e == 0 and ft == 0:
                    st.append(("gate", 1))
                if F.k and e == 1 and ft == 0:
                    st.append(("gate", 2))
        if e == 1 and F.n == 1:
            st.append(("gate", 3))
        if e >= 1:
            st.append(("down", e - 1))
        if e == 2 and not first:
            st.append(("ln", 0))
    return st + [("down", F.E - 1), ("fin", 0)]


def build(nc, a, out):
    ctx = ExitStack()
    with ctx:
        def sb(name, shape, dt=F32):
            return ctx.enter_context(nc.sbuf_tensor(name, shape, dt))

        def sem(name):
            return ctx.enter_context(nc.semaphore(name))

        bank = [ctx.enter_context(nc.psum_tensor(f"bank{i}", [P, 512], F32)) for i in range(8)]

        x = sb("x", [P, NT, D])
        xnT = sb("xnT", [P, T])
        ctxT = sb("ctxT", [DC, T])
        R0 = sb("R0", [P, 11008])
        R1 = sb("R1", [P, 8704])
        ident = sb("ident", [P, P])
        identb = sb("identb", [P, P], BF16)
        onesb = sb("onesb", [P, P], BF16)
        iota = sb("iota", [P, 8])
        vecs = sb("vecs", [V_N, P])
        vecT = sb("vecT", [P, V_N])
        w1T = sb("w1T", [P, 512])
        headmask = sb("headmask", [P, 16])
        w2a = sb("w2a", [P, 384])
        bqs = sb("bqs", [P, 1])
        bo_bc = sb("bo_bc", [P, D])
        bv_bc = sb("bv_bc", [P, D])
        gout_bc = sb("gout_bc", [P, D])
        bproj_bc = sb("bproj_bc", [P, D])
        swb_bc = sb("swb_bc", [P, 8])
        nk_bc = sb("nk_bc", [P, 64])
        nv_col = sb("nv_col", [P, 1])
        gw0 = sb("gw0", [P, 8])
        gw1 = sb("gw1", [P, 8])
        b2pad = sb("b2pad", [P, D])
        mask0 = sb("mask0", [P, 2, S], U8)
        mask3 = sb("mask3", [1, B * S], U8)
        mb0 = sb("mb0", [P, 2, S], BF16)
        mb3 = sb("mb3", [P, B * S], BF16)
        bopen = sb("bopen", [P, 2, D])
        seen = sb("seen", [P, 2])
        pen = sb("pen", [P, 2])
        neghalf = sb("neghalf", [P, 4])

        Qz = sb("Qz", [P, 16, S])
        kT = sb("kT", [P, 8, S])
        VxF = sb("VxF", [P, 2208])
        Pm = sb("Pm", [P, 2, 512])
        PTs = sb("PTs", [P, 4, 512])
        On = sb("On", [P, 2, 9 * P])
        OT = sb("OT", [P, 9, S])
        ctxb = sb("ctxb", [DC, S])
        QTs = sb("QTs", [P, S])
        negm = sb("negm", [P, 4, 2])
        rden = sb("rden", [P, 2, 2, 2])
        den = sb("den", [P, 2, 2, 2])
        sn16 = sb("sn16", [16, S])
        nsn = sb("nsn", [P, 2, 16])
        dn = sb("dn", [P, 4, 2])
        pn = sb("pn", [P, 2, 16])
        xnew = sb("xnew", [P, 4, D])
        rtmp = sb("rtmp", [P, 4, D])
        st6 = sb("st6", [P, 4, 6])
        mv = sb("mv", [P, 4, 2])
        ve = sb("ve", [P, 4])
        rstd = sb("rstd", [P, 4])
        yn = sb("yn", [P, 4, D])
        scrap = sb("scrap", [P, 1])
        osb = sb("osb", [P, 2, D])
        mvo = sb("mvo", [P, 2, 2])
        on1 = sb("on1", [P, 2, D])
        on2 = sb("on2", [P, 2, D])

        G = Qz[:, :, :].rearrange("p h s -> p (h s)").rearrange("p (g s) -> p g s", s=CH)
        sg = Pm
        OTf = OT[:, :, :].rearrange("p c s -> p (c s)")
        acc = OTf[:, 0:512].rearrange("p (t d) -> p t d", d=D)
        gTs = OTf[0:8, 512:1024]
        wTs = OTf[:, 1024:1536]
        ctok = PTs[:, :, :].rearrange("p u s -> p (u s)")[:, 0:NT * DC].rearrange("p (t c) -> p t c", c=DC)
        w1nat = OTf[:, 0:448]
        lg = sb("lg", [P, 4, 8])
        mx = sb("mx", [P, 4, 8])
        mi = sb("mi", [P, 4, 8], U32)
        mif = sb("mif", [P, 4, 8])
        oh0 = sb("oh0", [P, 4, 8])
        oh1 = sb("oh1", [P, 4, 8])
        gd = sb("gd", [P, 4, 8])
        ge = sb("ge", [P, 4, 8])
        gs = sb("gs", [P, 4])
        gr = sb("gr", [P, 4])
        gp = sb("gp", [P, 4])
        wpad = sb("wpad", [P, 4, P])

        def cols(t, lo, n):
            return t[:, lo:lo + n]

        L0Wq = cols(R0, 0, 1024)
        L0Wkv = R0[0:DC, 1024:3072]
        L0Wo = cols(R0, 3072, 1024).rearrange("p (c d) -> p c d", d=D)
        L0w1 = cols(R0, 4096, 2048)
        L0w2 = cols(R0, 6144, 2048)
        L0w3 = cols(R0, 8192, 2048).rearrange("p (e f d) -> p e f d", f=2, d=D)
        L0s1 = cols(R0, 10240, 256)
        L0s2 = cols(R0, 10496, 256)
        L0s3 = cols(R0, 10752, 256).rearrange("p (f d) -> p f d", d=D)
        n1 = cols(R0, 0, 2816)
        n3 = cols(R0, 2816, 2816)
        n2 = cols(R0, 5632, 2816).rearrange("p (e f) -> p e f", f=352)
        L3Wq = cols(R0, 0, 1024)
        L3Wkv = R0[0:DC, 1024:3072]
        L3Wo = cols(R0, 3072, 1152).rearrange("p (c d) -> p c d", d=D)
        fcn = cols(R0, 4224, 512)
        prn = cols(R0, 4736, 512)
        fcT = cols(R0, 5248, 512)
        prT = cols(R0, 5760, 512).rearrange("p (c d) -> p c d", d=D)
        Afc = R0[0:16, 6272:6400]
        Apr = R0[0:16, 6400:6912]
        Bfc = cols(R0, 6912, 64).rearrange("p (c r) -> p c r", r=16)
        Bpr = cols(R0, 6976, 16)
        BT = R0[0:16, 6992:7632]
        qtmp = cols(R0, 7632, 1024)
        Wn = cols(R0, 8656, 16)
        NVsel = cols(R0, 8672, 128).rearrange("p (c h) -> p c h", h=16)
        NVflat = cols(R0, 8672, 128)
        am = cols(R0, 8800, 2)
        amx = cols(R0, 8802, 2)
        qsc = cols(R0, 8804, 2)
        rqs = cols(R0, 8806, 2)
        L1w1 = cols(R1, 0, 4096)
        L1w2 = cols(R1, 4096, 4096).rearrange("p (e f d) -> p e f d", f=4, d=D)
        L2w1 = cols(R1, 0, 2816)
        L2w3 = cols(R1, 2816, 2816)
        L2w2 = cols(R1, 5632, 3072).rearrange("p (e f d) -> p e f d", f=3, d=D)

        loads = {n: sem(f"loaded_{n}") for n in
                 ("x", "ctx", "small", "l1a", "l0a", "mask", "l0f", "l1f", "l2a", "l2f", "l3")}
        LOADED = dict(x=1, ctx=1, small=19, l1a=4, l0a=3, mask=2, l0f=6, l1f=3, l2a=3, l2f=3, l3=9)
        engines_done = {n: sem(f"{n}_phase_done") for n in ("pe", "act", "dve", "pool")}
        consts_ready = sem("consts_ready")
        consts_ready_dve = sem("mask_bias_ready")
        waits_met = {e.engine: sem(n + "_waits_met")
                     for n, e in (("pe", nc.tensor), ("dve", nc.vector), ("pool", nc.gpsimd))}
        pool_chain = sem("pool_chain")
        dve_chain = sem("dve_chain")
        out_written = sem("out_written")

        def ring(tag):
            return Ring(sem(f"{tag}_filled"), sem(f"{tag}_read_by_act"), sem(f"{tag}_read_by_dve"))

        setup = ring("setup")
        prep = {2: ring("prep2"), 3: ring("prep3")}
        setup_stats = sem("setup_stats")
        setup_normed = sem("setup_normed")
        prep3_rows = sem("prep3_rows")
        prep3_max = sem("prep3_max")
        prep3_done = sem("prep3_operands")
        prep3_zero = sem("prep3_zero")
        zeroed = sem("ones_columns_set")

        def counted(names, tag, layers):
            sems = {n: sem(tag + n) for n in names}
            total = dict.fromkeys(names, 0)
            out = []
            for counts in layers:
                out.append({n: Counted(sems[n], total[n]) for n in names})
                for n, c in counts.items():
                    total[n] += c
            return out

        def att_counts(A):
            nh, nb = (A.nh, 1) if A.n == 2 else (A.nh * B, B)
            kinds = ["single"] if A.n == 2 else ["prologue", "first"] + ["mid"] * (B - 2) + ["last", "epilogue"]
            fills = sum(s[0] in FILLS for k in kinds for s in kind_steps(A, k))
            return dict(filled=fills, act=(fills + 1) // 2, dve=fills // 2, scores=nh, negmax=nh, exp=nh,
                        turn=nh, pt0=nh // 2, pt1=nh // 2, av=nh, norm=nh if A.n == 2 else nh // 2, stats=B,
                        yn=B, ctxb=0 if A.n == 2 else B, qm=nh if A.n == 1 else 0,
                        ostats=B if A.null else 0, onorm=B if A.null else 0)

        def ffn_counts(F):
            routed = NCH if F.k else 0
            return dict(h=F.U * NCH, silu=F.U * NCH if F.gated else 0, g=F.U * NCH, y=F.E * NCH, acc=F.E * NCH,
                        stats=NCH, yn=NCH if F.n < 3 else 0, lnf=NCH if F.n < 3 else 0,
                        lne=NCH if F.n < 3 else 0, gt=routed, gte=routed, gl=routed, gle=routed, gd=routed,
                        gx=routed, w=NCH if F.k == 1 else 0, wt=NCH if F.k == 1 else 0,
                        wte=NCH if F.k == 1 else 0)

        att_s = [AttentionSems(c) for c in
                 counted(list(att_counts(ATT[0])), "att_", [att_counts(A) for A in ATT])]
        ffn_s = [FeedForwardSems(c) for c in
                 counted(list(ffn_counts(FFN[0])), "ffn_", [ffn_counts(F) for F in FFN])]

        def need(eng, s, value):
            if not isinstance(value, int) or value > 0:
                if isinstance(s, Counted):
                    eng.wait_ge(s.sem, s.base + value)
                else:
                    eng.wait_ge(s, value)

        def plain(eng):
            eng.sem_inc(waits_met[eng.engine], 1)

        def loaded(eng, name):
            eng.wait_ge(loads[name], 16 * LOADED[name])

        def boundary(eng, name, phase):
            eng.drain().then_inc(engines_done[name], 1)
            for other in engines_done:
                if other != name:
                    eng.wait_ge(engines_done[other], phase)

        def ring_base(A, b, kinds):
            per = BATCH_FILLS[A.n]
            n0 = sum(s[0] in FILLS for s in att_prologue(A))
            if kinds == "first":
                return n0
            f0 = sum(s[0] in FILLS for s in att_schedule(A, True, False))
            assert f0 + 1 == per, (A.n, f0)
            return n0 + f0 - per

        def steps(A, b, kinds):
            st = kind_steps(A, kinds)
            if kinds in ("single", "prologue"):
                base = 0
            elif kinds == "epilogue":
                base = ring_base(A, b, "last") + sum(s[0] in FILLS for s in kind_steps(A, "last"))
            else:
                base = ring_base(A, b, kinds)
                if kinds == "mid":
                    assert sum(s[0] in FILLS for s in st) == BATCH_FILLS[A.n], (A.n, st)
            n = base
            for kind, k in st:
                if kind == "wo" and k == 0:
                    assert n % 2 == 1, (A.n, kinds, n)
                yield kind, k, n, base
                n += kind in FILLS

        def batches(eng, A, body):
            if A.n == 2:
                body(0, "single")
                return
            body(0, "prologue")
            body(0, "first")
            with eng.Fori(1, B - 1) as b:
                body(b, "mid")
            body(B - 1, "last")
            body(B - 1, "epilogue")

        def chunks(eng, F, body):
            body(0, True)
            with eng.Fori(1, NCH) as c:
                body(c, False)
            body(NCH, None)

        def Vx(A):
            if A.n == 2:
                return VxF[:, 0:16 * 129].rearrange("p (t e) -> p t e", e=129)
            return VxF[:, 0:2 * 1104].rearrange("p (t e) -> p t e", e=1104)

        def Vheads(A, kt):
            e = A.dh + 1
            return Vx(A)[:, kt, 0:16 * e].rearrange("p (h e) -> p h e", e=e)

        AWq = {0: L0Wq, 1: w1T[:, 0:128], 2: w2a[:, 0:128], 3: L3Wq}
        AWk = {0: L0Wkv[:, 0:1024], 1: w1T[0:DC, 128:256], 2: w2a[0:DC, 128:256], 3: L3Wkv[:, 0:1024]}
        AWv = {0: L0Wkv[:, 1024:2048], 1: w1T[0:DC, 256:384], 2: w2a[0:DC, 256:384],
               3: L3Wkv[:, 1024:2048]}
        AWo = {0: L0Wo, 1: w1T[:, 384:512].rearrange("p (c d) -> p c d", d=D), 3: L3Wo}

        def keys_of(A, h):
            return kT[:, h // 2, :] if A.dh == 64 else kT[:, 0, :] if A.n == 1 else kT[:, h, :]

        def bank_of(n):
            return bank[6 + n % 2]

        SETUP = [("ctx", j) for j in range(4)] + [("vec", 0), ("l1w", 0)] + [("ln", j) for j in range(4)]
        PREP2 = [("n1", j) for j in range(6)] + [("n3", j) for j in range(6)] + [("n2", e) for e in range(8)]
        PREP3 = [("bfc", 0), ("bpr", 0), ("nv", 0), ("fc", 0), ("pr", 0)]

        def setup_evac(move, kind, k, src):
            if kind == "ctx":
                return move(ctxT[:, k * 512:(k + 1) * 512], src[0:DC, :])
            if kind == "vec":
                return move(vecT[:, :], src[:, 0:V_N])
            if kind == "l1w":
                move(w1T[:, 0:128], src[:, 0:128])
                move(w1T[0:DC, 128:384], src[0:DC, 128:384])
                return move(w1T[:, 384:512], src[:, 384:512])
            return move(xnT[:, k * CH:(k + 1) * CH], src[:, :], vecT[:, V_GAMMA:V_GAMMA + 1],
                        vecT[:, V_BETA:V_BETA + 1])

        def prep_evac(move, kind, k, src):
            if kind in ("n1", "n3"):
                n = 4 if k < 5 else 2
                dst = L2w1 if kind == "n1" else L2w3
                return move(dst[:, k * 512:k * 512 + n * 128], src[:, 0:n * 128])
            if kind == "n2":
                move(L2w2[:, k, 0:2, :], src[:, 0:256].rearrange("p (f d) -> p f d", d=D))
                return move(L2w2[0:96, k, 2, :], src[0:96, 256:384])
            if kind == "bfc":
                return move(BT[:, 0:512], src[0:16, :], 2.0)
            if kind == "bpr":
                return move(BT[:, 512:640], src[0:16, 0:128], 2.0)
            if kind == "nv":
                return move(L3Wo[0:16, 8, :], src[0:16, 0:128])
            if kind == "fc":
                return move(fcT, src[:, :])
            return move(prT, src[:, :].rearrange("p (c d) -> p c d", d=D))

        def att_evac(A, move, kind, k, b, kinds, src):
            if kind == "q" and A.dh == 64:
                Q4 = Qz[:, :, :].rearrange("p (g u) s -> p g u s", u=2)
                v = src[:, :].rearrange("p (g s) -> p g s", s=S)
                move(Q4[0:64, 2 * k:2 * k + 2, 0, :], v[0:64], A.scale)
                return move(Q4[64:128, 2 * k:2 * k + 2, 1, :], v[64:128], A.scale)
            if kind == "q" and A.n == 1:
                return move(QTs[:, :], src[:, 0:S], A.scale)
            if kind == "q":
                return move(Qz[:, 2 * k:2 * k + 2, :].rearrange("p h s -> p (h s)"), src[:, :], A.scale,
                            bqs[:, 0:1])
            if kind == "k" and A.dh == 64:
                return move(kT[:, 2 * k:2 * k + 2, :].rearrange("p h s -> p (h s)"), src[:, :])
            if kind == "k" and A.n == 1:
                return move(kT[:, 0, :], src[:, 0:S])
            if kind == "k":
                return move(kT[:, 2 * k:2 * k + 2, :].rearrange("p h s -> p (h s)"), src[:, :], None,
                            vecT[:, V_BK:V_BK + 1])
            if kind == "v" and A.dh == 64:
                return move(Vheads(A, k // 2)[:, 8 * (k % 2):8 * (k % 2) + 8, 0:64],
                            src[:, :].rearrange("p (h e) -> p h e", e=64))
            if kind == "v" and A.n == 1:
                move(Vheads(A, 0)[:, :, 0:8], src[:, 0:128].rearrange("p (h e) -> p h e", e=8))
                return move(Vheads(A, 1)[:, :, 0:8], src[:, 128:256].rearrange("p (h e) -> p h e", e=8))
            if kind == "v":
                return move(Vx(A)[:, 4 * k:4 * k + 4, 0:128], src[:, :].rearrange("p (t e) -> p t e", e=128))
            if kind == "sn":
                return move(sn16[:, :], src[0:16, 0:S], -A.scale)
            if kind == "snt":
                return move(nsn[:, :, :].rearrange("p q h -> p (q h)"), src[:, 0:32])
            if kind == "outT" and A.dh == 64 and k < 4:
                return move(OT[:, 2 * k:2 * k + 2, :].rearrange("p c s -> p (c s)"), src[:, :])
            if kind == "outT":
                return move(OT[:, 8 if A.null else 0, :], src[:, 0:S])
            if kind == "wo":
                assert k == 1
                return move(scrap[:, :], src[:, 0:1])
            assert kind == "ln"
            bl = k if A.n == 2 else b if kinds == "epilogue" else b - 1
            return move(xnT[:, bass.ts(bl, S)], src[:, 0:S])

        def ffn_ln_evac(F, move, c):
            gain = vecT[:, V_GNORM:V_GNORM + 1] if F.n == 2 else None
            return move(xnT[:, bass.ts(c, CH)], bank[6][:, :], gain)

        block = ctx.enter_context(nc.Block())

        @block.sync
        def _(sp):
            def load(name, dst, src):
                sp.dma_start(dst, src).then_inc(loads[name], 16)

            def row(v):
                return v.rearrange("(a n) -> a n", a=1)

            def spread(v, n=D):
                return row(v).to_broadcast([P, n])

            load("ctx", ctok[:, :, :], a["ctx_768"].rearrange("b (h p) c -> p (b h) c", p=P))
            load("x", x[:, :, :], a["x"].rearrange("b (h p) c -> p (b h) c", p=P))
            load("small", vecs[V_B1:V_B1 + 32, :], a["L1_ffn_b1"].rearrange("e (f p) -> (e f) p", p=P))
            load("small", vecs[V_BFC:V_BFC + 4, :], a["L3_ffn_b_fc"].rearrange("(f p) -> f p", p=P))
            for at, name in ((V_GAMMA, "L0_xattn_ln_gamma"), (V_BETA, "L0_xattn_ln_beta"),
                             (V_GNORM, "L3_xattn_g_norm"), (V_BQ, "L2_xattn_bq"), (V_BK, "L2_xattn_bk")):
                load("small", vecs[at:at + 1, :], row(a[name]))
            load("small", vecs[V_GATE2:V_GATE2 + 8, :], a["L2_ffn_gate_w"])
            load("l1a", w1nat[:, 0:128], a["L1_xattn_Wq"])
            load("l1a", w1nat[:, 128:224], a["L1_xattn_Wk"])
            load("l1a", w1nat[:, 224:320], a["L1_xattn_Wv"])
            load("l1a", w1nat[:, 320:448], a["L1_xattn_Wo"])
            load("l0a", L0Wq, a["L0_xattn_Wq"])
            load("l0a", L0Wkv, a["L0_xattn_Wkv"])
            load("l0a", L0Wo, a["L0_xattn_Wo"].rearrange("(c p) d -> p c d", p=P))
            load("mask", mask0[:, :, :], a["mask_1x1xSxS2_bk0"].rearrange("a b (t p) k -> p (a b t) k", p=P))
            load("mask", mask3[:, :], a["mask_BxS2_bf1"].rearrange("(o b) k -> o (b k)", o=1))
            for dst, name, n in ((bo_bc, "L0_xattn_bo", D), (bv_bc, "L2_xattn_bv", D),
                                 (gout_bc, "L3_xattn_g_out", D), (bproj_bc, "L3_ffn_b_proj", D),
                                 (swb_bc, "L1_ffn_switch_b", 8)):
                load("small", dst[:, :], spread(a[name], n))
            load("small", nk_bc[:, :], a["L3_xattn_null_kv"][0:1, :].to_broadcast([P, 64]))
            for half in range(2):
                load("small", nv_col[64 * half:64 * half + 64, :],
                     a["L3_xattn_null_kv"][1:2, :].rearrange("a p -> p a"))
            load("small", gw0[:, :], a["L0_ffn_gate_w"])
            load("small", gw1[:, :], a["L1_ffn_switch_w"])
            sp.wait_ge(consts_ready, 1)
            load("small", b2pad[0:8, :], a["L1_ffn_b2"])
            load("l0f", L0w1.rearrange("p (e f) -> p e f", e=8), a["L0_ffn_ew1"].rearrange("e p f -> p e f"))
            load("l0f", L0w2.rearrange("p (e f) -> p e f", e=8), a["L0_ffn_ew2"].rearrange("e p f -> p e f"))
            load("l0f", L0w3.rearrange("p e f d -> p (e f) d"),
                 a["L0_ffn_ew3"].rearrange("e (f p) d -> p (e f) d", p=P))
            load("l0f", L0s1, a["L0_ffn_sw1"])
            load("l0f", L0s2, a["L0_ffn_sw2"])
            load("l0f", L0s3, a["L0_ffn_sw3"].rearrange("(f p) d -> p f d", p=P))
            load("l1f", L1w1.rearrange("p (e f) -> p e f", e=8), a["L1_ffn_w1"].rearrange("e p f -> p e f"))
            for e in (0, 4):
                load("l1f", L1w2[:, e:e + 4, :, :].rearrange("p e f d -> p (e f) d"),
                     a["L1_ffn_w2"][e:e + 4].rearrange("e (f p) d -> p (e f) d", p=P))
            load("l2a", w2a[:, 0:128], a["L2_xattn_Wq"])
            load("l2a", w2a[0:DC, 128:256], a["L2_xattn_Wk"])
            load("l2a", w2a[0:DC, 256:384], a["L2_xattn_Wv"])
            sp.wait_ge(engines_done["pe"], 3)
            load("l2f", n1.rearrange("p (t d) -> p t d", d=D),
                 a["L2_ffn_w1"].rearrange("e f d -> (e f) d").rearrange("(t p) d -> p t d", p=P))
            load("l2f", n3.rearrange("p (t d) -> p t d", d=D),
                 a["L2_ffn_w3"].rearrange("e f d -> (e f) d").rearrange("(t p) d -> p t d", p=P))
            load("l2f", n2, a["L2_ffn_w2"].rearrange("e d f -> d e f"))
            sp.wait_ge(prep[2].filled, len(PREP2))
            load("l3", L3Wq, a["L3_xattn_Wq"])
            load("l3", L3Wkv, a["L3_xattn_Wkv"])
            load("l3", L3Wo[:, 0:8, :], a["L3_xattn_Wout"].rearrange("(c p) d -> p c d", p=P))
            load("l3", fcn.rearrange("p (c d) -> p c d", d=D), a["L3_ffn_W_fc"].rearrange("(c p) d -> p c d", p=P))
            load("l3", prn, a["L3_ffn_W_proj"])
            load("l3", Afc, a["L3_ffn_A_fc"])
            load("l3", Apr, a["L3_ffn_A_proj"])
            load("l3", Bfc, a["L3_ffn_B_fc"].rearrange("(c p) r -> p c r", p=P))
            load("l3", Bpr, a["L3_ffn_B_proj"])
            for c in range(NCH):
                need(sp, ffn_s[3].stats, c + 1)
                sp.dma_start(out.rearrange("b (h p) c -> p (b h) c", p=P)[:, 4 * c:4 * c + 4, :],
                             x[:, 4 * c:4 * c + 4, :]).then_inc(out_written, 16)
            sp.wait_ge(out_written, 16 * NCH)

        @block.gpsimd
        def _(pool):
            count = [0]

            def link(ins):
                count[0] += 1
                ins.then_inc(pool_chain, 1)
                pool.wait_ge(pool_chain, count[0])

            pool.memset(b2pad[:, :], 0.0).then_inc(consts_ready, 1)
            link(pool.memset(ident[:, :], 0.0))
            link(pool.affine_select(out=ident[:, :], in_=ident[:, :], compare_op=ALU.not_equal, fill=1.0,
                                    base=0, pattern=[[-1, P]], channel_multiplier=1))
            link(pool.tensor_copy(identb[:, :], ident[:, :]))
            pool.memset(onesb[:, :], 1.0)
            pool.memset(neghalf[:, :], -0.5)
            pool.memset(mb3[:, :], 0.0)
            pool.memset(wpad[:, :, :], 0.0)
            for e in range(8):
                pool.memset(iota[:, e:e + 1], float(e))
            link(pool.memset(headmask[:, :], 1.0))
            link(pool.affine_select(out=headmask[:, :], in_=headmask[:, :], compare_op=ALU.is_ge, fill=0.0,
                                    base=0, pattern=[[-8, 16]], channel_multiplier=1))
            link(pool.affine_select(out=headmask[:, :], in_=headmask[:, :], compare_op=ALU.is_ge, fill=0.0,
                                    base=7, pattern=[[8, 16]], channel_multiplier=-1))
            pool.memset(Qz[:, :, :], 0.0)
            pool.memset(VxF[:, :], 0.0)
            pool.memset(On[:, :, 1024:1152], 0.0).then_inc(consts_ready, 1)
            count0 = [0]

            def normalise(n, stats_sem, value, yn_sem, scale, offset, turned, chain, at=0):
                need(pool, stats_sem, value)
                plain(pool)
                chain(pool.tensor_scalar(ve[:, 0:n], mv[:, 0:n, 1], scale, offset, ALU.mult, ALU.add))
                chain(pool.tensor_tensor(rstd[:, 0:n], ve[:, 0:n], neghalf[:, 0:n], ALU.pow))
                plain(pool)
                for t in range(n):
                    src = xnew[:, t, :]
                    last = pool.tensor_scalar(yn[:, at + t, :], src, mv[:, t, 0:1], rstd[:, t:t + 1],
                                              ALU.subtract, ALU.mult)
                last.then_inc(yn_sem.sem, 1)

            for j in range(4):
                need(pool, setup.filled, 0 if j == 0 else 6 + j)
                pool.wait_ge(setup_stats, j + 1)
                link(pool.tensor_scalar(ve[:, 0:4], mv[:, 0:4, 1], 1.0 + EPS, EPS * EPS, ALU.mult, ALU.add))
                link(pool.tensor_tensor(rstd[:, 0:4], ve[:, 0:4], neghalf[:, 0:4], ALU.pow))
                for t in range(4):
                    last = pool.tensor_scalar(yn[:, t, :], x[:, 4 * j + t, :], mv[:, t, 0:1],
                                              rstd[:, t:t + 1], ALU.subtract, ALU.mult)
                last.then_inc(setup_normed, 1)
            boundary(pool, "pool", 1)

            def chain_for(base_per, b, start):
                n = [0]

                def chain(ins):
                    n[0] += 1
                    ins.then_inc(pool_chain, 1)
                    pool.wait_ge(pool_chain, b * base_per + (start + n[0]))
                return chain, n

            def attention(A):
                s = att_s[A.n]
                links = {0: 2, 1: 2, 2: 2, 3: 5}[A.n]
                start = count[0]
                if A.n == 3:
                    loaded(pool, "l3")
                    pool.memset(Qz[:, :, :], 0.0)
                    pool.memset(NVflat, 0.0)
                    pool.memset(L3Wo[:, 8, :], 0.0)
                    pool.memset(On[:, :, 1024:1152], 0.0).then_inc(prep3_zero, 1)
                if A.n:
                    link(pool.memset(VxF[:, :], 0.0))
                if A.n == 2:
                    pool.memset(Vx(A)[:, :, 128], 1.0).then_inc(zeroed, 1)
                else:
                    pool.memset(Vheads(A, 0)[:, :, A.dh], 1.0)
                    pool.memset(Vheads(A, 1)[:, :, A.dh], 1.0).then_inc(zeroed, 1)
                if A.n == 3:
                    pool.wait_ge(prep3_rows, 1)
                    pool.partition_all_reduce(amx, am, P, RMAX).then_inc(prep3_max, 1)
                start = count[0]
                a_, c_ = (1.0 + EPS, EPS * EPS) if A.n == 3 and False else (1.0, EPS)

                def masks(bw):
                    plain(pool)
                    for h in range(16):
                        pool.tensor_scalar(Qz[:, h, :], QTs[:, :], headmask[:, h:h + 1], None,
                                           ALU.mult).then_inc(s.qm.sem, 1)

                def body(b, kinds):
                    if A.n == 2:
                        for h in range(A.nh):
                            need(pool, s.stats, h + 1)
                            pool.tensor_copy(x[:, 2 * h:2 * h + 2, :], xnew[:, 0:2, :])
                            need(pool, s.ring.filled, 12 + h - 1)
                            normalise(2, s.stats, h + 1, s.yn, 1.0, EPS, None, link, 2 * (h % 2))
                        return
                    if kinds == "prologue":
                        pool.tensor_copy(ctxb[:, :], ctxT[:, 0:S]).then_inc(s.ctxb.sem, 1)
                        if A.n == 1:
                            need(pool, s.ring.act, 1)
                            masks(0)
                        return
                    if kinds == "epilogue":
                        if A.null:
                            tail(b, kinds)
                        return
                    at = {n: (k, m, base) for n, (k, m, base) in (
                        (kind, (k, m, base)) for kind, k, m, base in steps(A, b, kinds))}
                    base = at["scores"][2]
                    if kinds != "last":
                        need(pool, s.ring.filled, b * BATCH_FILLS[A.n] + base if A.n != 2 else base)
                        pool.tensor_copy(ctxb[:, :], ctxT[:, bass.ts(b + 1, S)]).then_inc(s.ctxb.sem, 1)
                    if A.null:
                        if kinds != "first":
                            tail(b - 1, kinds)
                        own_norm(b, kinds)
                        return
                    if A.n == 1 and kinds != "last":
                        m = [m for kind, k, m, _ in steps(A, b, kinds) if kind == "q"][0]
                        reader = s.ring.dve if m % 2 else s.ring.act
                        need(pool, reader, b * (BATCH_FILLS[1] // 2) + m // 2 + 1)
                        masks(b + 1)
                    tail(b, kinds)

                def chain_at(b, kinds, off):
                    n = [0]

                    def chain(ins):
                        n[0] += 1
                        ins.then_inc(pool_chain, 1)
                        pool.wait_ge(pool_chain, b * links + (start + off + n[0]))
                    return chain

                def own_norm(b, kinds):
                    chain = chain_at(b, kinds, 0)
                    need(pool, s.ostats, b + 1)
                    plain(pool)
                    chain(pool.tensor_scalar(ve[:, 2:4], mvo[:, :, 1], 1.0, EPS, ALU.mult, ALU.add))
                    chain(pool.tensor_tensor(rstd[:, 2:4], ve[:, 2:4], neghalf[:, 0:2], ALU.pow))
                    plain(pool)
                    pool.tensor_scalar(on1[:, 0, :], osb[:, 0, :], mvo[:, 0, 0:1], rstd[:, 2:3],
                                       ALU.subtract, ALU.mult)
                    chain(pool.tensor_scalar(on1[:, 1, :], osb[:, 1, :], mvo[:, 1, 0:1], rstd[:, 3:4],
                                             ALU.subtract, ALU.mult))
                    pool.tensor_tensor(on2[:, 0, :], on1[:, 0, :], gout_bc[:, :], ALU.mult)
                    pool.tensor_tensor(on2[:, 1, :], on1[:, 1, :], gout_bc[:, :],
                                       ALU.mult).then_inc(s.onorm.sem, 1)

                def tail(b, kinds):
                    chain = chain_at(b, kinds, links - 2 if A.null else 0)
                    need(pool, s.stats, b + 1)
                    pool.tensor_copy(x[:, bass.ds(b * 2, 2), :], xnew[:, 0:2, :])
                    normalise(2, s.stats, b + 1, s.yn, 1.0, EPS, None, chain)

                batches(pool, A, body)
                if A.n == 2:
                    return
                count[0] = start + B * links

            def feed_forward(F):
                s = ffn_s[F.n]
                start = count[0]

                def body(c, first):
                    if first is None:
                        return
                    n = [0]

                    def chain(ins):
                        n[0] += 1
                        ins.then_inc(pool_chain, 1)
                        pool.wait_ge(pool_chain, c * 2 + (start + n[0]))
                    need(pool, s.stats, c + 1)
                    pool.tensor_copy(x[:, bass.ds(c * 4, 4), :], xnew[:, :, :])
                    twice = F.n == 2
                    normalise(4, s.stats, c + 1, s.yn, 1.0 + EPS if twice else 1.0,
                              EPS * EPS if twice else EPS, None, chain)
                if F.n < 3:
                    chunks(pool, F, body)
                    count[0] = start + 2 * NCH

            for n in range(4):
                attention(ATT[n])
                boundary(pool, "pool", 2 * n + 2)
                feed_forward(FFN[n])
                if n < 3:
                    boundary(pool, "pool", 2 * n + 3)

        @block.scalar
        def _(act):
            def move(dst, src, gain=None, bias=None):
                if bias is not None:
                    return act.activation(dst, src, ACT.Identity, bias=bias, scale=1.0 if gain is None else gain)
                if gain is None or isinstance(gain, float):
                    return act.activation(dst, src, ACT.Copy, scale=1.0 if gain is None else gain)
                return act.activation(dst, src, ACT.Identity, scale=gain)

            for n, (kind, k) in enumerate(SETUP):
                if n % 2 == 0:
                    act.wait_ge(setup.filled, n + 1)
                    setup_evac(move, kind, k, bank_of(n)).then_inc(setup.act, 1)
            boundary(act, "act", 1)

            def attention(A):
                s = att_s[A.n]
                if A.n in prep:
                    r = prep[A.n]
                    for n, (kind, k) in enumerate(PREP2 if A.n == 2 else PREP3):
                        if n % 2 == 0:
                            act.wait_ge(r.filled, n + 1)
                            prep_evac(move, kind, k, bank_of(n)).then_inc(r.act, 1)
                act.wait_ge(zeroed, A.n + 1)

                def body(b, kinds):
                    nh = A.nh
                    for kind, k, m, base in steps(A, b, kinds):
                        if kind == "softmax":
                            need(act, s.negmax, b * nh + (k + 1))
                            need(act, s.turn, b * nh + (k - 1))
                            if A.null:
                                act.activation(pn[:, :, k], dn[:, k % 4, :], ACT.Exp)
                            for qt in range(2):
                                last = act.activation(Pm[:, k % 2, qt * S:(qt + 1) * S],
                                                      bank[k % 2][:, qt * S:(qt + 1) * S], ACT.Exp,
                                                      bias=negm[:, k % 4, qt:qt + 1])
                            last.then_inc(s.exp.sem, 1)
                        elif kind == "turn" and k % 2 == 0:
                            need(act, s.turn, b * nh + (k + 1))
                            need(act, s.av, b * nh + (k - 3))
                            move(PTs[:, k % 4, :], bank[2][:, :]).then_inc(s.pt[0].sem, 1)
                        elif kind in FILLS and m % 2 == 0:
                            need(act, s.ring.filled, b * BATCH_FILLS.get(A.n, 0) + (m + 1))
                            att_evac(A, move, kind, k, b, kinds, bank_of(m)).then_inc(s.ring.act.sem, 1)
                batches(act, A, body)

            def feed_forward(F):
                s = ffn_s[F.n]

                def body(c, first):
                    if first is None:
                        if F.n < 3:
                            need(act, s.lnf, NCH)
                            ffn_ln_evac(F, move, NCH - 1).then_inc(s.lne.sem, 1)
                        return
                    for kind, k in ffn_schedule(F, first):
                        if kind == "gate" and k == 0:
                            need(act, s.gt, c + 1)
                            need(act, s.gl, c)
                            move(gTs[:, :], bank[6][0:8, :]).then_inc(s.gte.sem, 1)
                        elif kind == "gate" and k == 2:
                            need(act, s.gd, c + 1)
                            if F.k == 1:
                                act.activation(ge[:, :, :], gd[:, :, :], ACT.Exp).then_inc(s.gx.sem, 1)
                            else:
                                act.activation(ge[:, :, 0], gd[:, :, 0], ACT.Exp).then_inc(s.gx.sem, 1)
                        elif kind == "up":
                            e, ft = k
                            u = e * F.FT + ft
                            M = F.last if ft == F.FT - 1 else P
                            need(act, s.h, c * F.U + (u + 1))
                            if F.gated:
                                need(act, s.g, c * F.U + (u - 1))
                                act.activation(sg[0:M, u % 2, :], bank[u % 2][0:M, :],
                                               ACT.Silu).then_inc(s.silu.sem, 1)
                            else:
                                need(act, s.y, c * F.E + (e - 1 if e >= 2 else 0))
                                bias = (vecT[:, V_B1 + u:V_B1 + u + 1] if F.n == 1
                                        else vecT[:, V_BFC + u:V_BFC + u + 1])
                                act.activation(G[:, u % (2 * F.FT), :], bank[u % 4][:, :],
                                               ACT.Gelu_apprx_tanh if F.n == 1 else ACT.Gelu,
                                               bias=bias).then_inc(s.g.sem, 1)
                        elif kind == "ln":
                            need(act, s.lnf, c)
                            ffn_ln_evac(F, move, c - 1).then_inc(s.lne.sem, 1)
                chunks(act, F, body)

            for n in range(4):
                attention(ATT[n])
                boundary(act, "act", 2 * n + 2)
                feed_forward(FFN[n])
                if n < 3:
                    boundary(act, "act", 2 * n + 3)

        @block.tensor
        def _(pe):
            def mm(o, l, r, start=True, stop=True):
                return pe.matmul(o, l, r, start=start, stop=stop)

            def turn(o, i):
                n = i.shape[0]
                return pe.transpose(o, i, ident[0:n, 0:n])

            pe.wait_ge(consts_ready, 2)
            for n, (kind, k) in enumerate(SETUP):
                ps = bank_of(n)
                if n >= 2:
                    pe.wait_ge(setup.dve if n % 2 else setup.act, n // 2)
                if kind == "ctx":
                    if k == 0:
                        loaded(pe, "ctx")
                    for t in range(4):
                        last = turn(ps[0:DC, t * P:(t + 1) * P], ctok[:, 4 * k + t, :])
                elif kind == "vec":
                    loaded(pe, "small")
                    last = turn(ps[:, 0:V_N], vecs[:, :])
                elif kind == "l1w":
                    loaded(pe, "l1a")
                    turn(ps[:, 0:128], w1nat[:, 0:128])
                    turn(ps[0:DC, 128:256], w1nat[:, 128:224])
                    turn(ps[0:DC, 256:384], w1nat[:, 224:320])
                    last = turn(ps[:, 384:512], w1nat[:, 320:448])
                else:
                    pe.wait_ge(setup_normed, k + 1)
                    for t in range(4):
                        last = turn(ps[:, t * P:(t + 1) * P], yn[:, t, :])
                last.then_inc(setup.filled, 1)
            boundary(pe, "pe", 1)

            def prep_fill(kind, k, ps):
                if kind in ("n1", "n3"):
                    src = n1 if kind == "n1" else n3
                    for t in range(4 if k < 5 else 2):
                        last = turn(ps[:, t * P:(t + 1) * P], src[:, (4 * k + t) * P:(4 * k + t + 1) * P])
                elif kind == "n2":
                    for f in range(3):
                        w = 128 if f < 2 else 96
                        last = turn(ps[0:w, f * P:f * P + P], n2[:, k, f * P:f * P + w])
                elif kind == "bfc":
                    for t in range(4):
                        last = turn(ps[0:16, t * P:(t + 1) * P], Bfc[:, t, :])
                elif kind == "bpr":
                    last = turn(ps[0:16, 0:P], Bpr)
                elif kind == "nv":
                    pe.wait_ge(prep3_done, 1)
                    for c in range(8):
                        last = mm(ps[0:16, 0:P], NVsel[:, c, :], L3Wo[:, c, :], c == 0, c == 7)
                elif kind == "fc":
                    pe.wait_ge(prep[3].act, 1)
                    pe.wait_ge(prep3_done, 2)
                    for t in range(4):
                        o = ps[:, t * P:(t + 1) * P]
                        mm(o, fcn[:, t * P:(t + 1) * P], ident[:, :], True, False)
                        last = mm(o, Afc, BT[:, t * P:(t + 1) * P], False, True)
                else:
                    pe.wait_ge(prep[3].dve, 1)
                    pe.wait_ge(prep3_done, 3)
                    for t in range(4):
                        o = ps[:, t * P:(t + 1) * P]
                        mm(o, prn[:, t * P:(t + 1) * P], ident[:, :], True, False)
                        last = mm(o, Apr[:, t * P:(t + 1) * P], BT[:, 512:640], False, True)
                return last

            def attention(A):
                s = att_s[A.n]
                Wq, Wk, Wv = AWq[A.n], AWk[A.n], AWv[A.n]
                if A.n in prep:
                    r = prep[A.n]
                    loaded(pe, "l2f" if A.n == 2 else "l3")
                    for n, (kind, k) in enumerate(PREP2 if A.n == 2 else PREP3):
                        if n >= 2:
                            pe.wait_ge(r.dve if n % 2 else r.act, n // 2)
                        prep_fill(kind, k, bank_of(n)).then_inc(r.filled, 1)
                    n = len(PREP2 if A.n == 2 else PREP3)
                    pe.wait_ge(r.act, (n + 1) // 2)
                    pe.wait_ge(r.dve, n // 2)
                if A.n in (0, 2):
                    loaded(pe, "l0a" if A.n == 0 else "l2a")
                pe.wait_ge(zeroed, A.n + 1)
                if A.n in (0, 3):
                    pe.wait_ge(consts_ready_dve, 1)
                per = BATCH_FILLS.get(A.n, 0)

                def fills_read(b, m):
                    need(pe, s.ring.act, b * (per // 2) + (m + 1) // 2)
                    need(pe, s.ring.dve, b * (per // 2) + m // 2)

                def fill(kind, k, b, kinds, m, ps):
                    bw = 0 if kinds in ("prologue", "single") else b + 1
                    need(pe, s.ring.dve if m % 2 else s.ring.act, b * (per // 2) + m // 2)
                    if kind == "q" and A.dh == 64:
                        for g in range(2):
                            hp = 2 * k + g
                            last = mm(ps[:, g * S:(g + 1) * S], Wq[:, hp * P:(hp + 1) * P], xnT[:, bass.ts(bw, S)])
                    elif kind == "q" and A.n == 1:
                        last = mm(ps[:, 0:S], Wq, xnT[:, bass.ts(bw, S)])
                    elif kind == "q":
                        last = mm(ps[:, :], Wq, xnT[:, k * 512:(k + 1) * 512])
                    elif kind == "k" and A.dh == 64:
                        for g in range(2):
                            hp = 2 * k + g
                            last = mm(ps[:, g * S:(g + 1) * S], Wk[:, hp * P:(hp + 1) * P], ctxT[:, bass.ts(bw, S)])
                    elif kind == "k" and A.n == 1:
                        last = mm(ps[:, 0:S], Wk, ctxT[:, bass.ts(bw, S)])
                    elif kind == "k":
                        last = mm(ps[:, :], Wk, ctxT[:, k * 512:(k + 1) * 512])
                    elif kind == "v" and A.dh == 64:
                        need(pe, s.ctxb, bw + 1)
                        last = mm(ps[:, :], ctxb[:, (k // 2) * P:(k // 2 + 1) * P],
                                  Wv[:, (k % 2) * 512:(k % 2 + 1) * 512])
                    elif kind == "v" and A.n == 1:
                        need(pe, s.ctxb, bw + 1)
                        for kt in range(2):
                            last = mm(ps[:, kt * P:(kt + 1) * P], ctxb[:, kt * P:(kt + 1) * P], Wv)
                    elif kind == "v":
                        for t in range(4):
                            last = mm(ps[:, t * P:(t + 1) * P], ctxT[:, (4 * k + t) * P:(4 * k + t + 1) * P], Wv)
                    elif kind == "sn":
                        plain(pe)
                        last = mm(ps[0:16, 0:S], Wn, xnT[:, bass.ts(bw, S)])
                    elif kind == "snt":
                        fills_read(b, m)
                        plain(pe)
                        for qt in range(2):
                            last = turn(ps[:, qt * 16:(qt + 1) * 16], sn16[:, qt * P:(qt + 1) * P])
                    elif kind == "outT" and A.dh == 64 and k < 4:
                        need(pe, s.norm, b * 8 + (2 * k + 2))
                        for c in range(2):
                            for qt in range(2):
                                last = turn(ps[:, c * S + qt * P:c * S + (qt + 1) * P],
                                            On[:, qt, (2 * k + c) * P:(2 * k + c + 1) * P])
                    elif kind == "outT":
                        need(pe, s.norm, b * 8 + 8)
                        c = 8 if A.null else 0
                        for qt in range(2):
                            last = turn(ps[:, qt * P:(qt + 1) * P], On[:, qt, c * P:(c + 1) * P])
                    elif kind == "wo" and k == 0:
                        fills_read(b, m)
                        for qt in range(2):
                            for c in range(A.pieces):
                                last = mm(ps[:, qt * P:(qt + 1) * P], OT[:, c, qt * P:(qt + 1) * P],
                                          AWo[A.n][:, c, :], c == 0, c == A.pieces - 1)
                    elif kind == "wo":
                        last = turn(ps[:, 0:P], ident[:, :])
                    else:
                        bl = (k if A.n == 2 else b if kinds == "epilogue" else b - 1)
                        need(pe, s.yn, bl + 1)
                        at = 2 * (k % 2) if A.n == 2 else 0
                        for t in range(2):
                            last = turn(ps[:, t * P:(t + 1) * P], yn[:, at + t, :])
                    last.then_inc(s.ring.filled.sem, 1)

                def body(b, kinds):
                    nh = A.nh
                    for kind, k, m, base in steps(A, b, kinds):
                        if kind == "scores":
                            if k == 0:
                                fills_read(b, m if A.n == 2 else base - 1 if A.n == 1 else base - 2)
                            if A.n == 1:
                                need(pe, s.qm, b * nh + (k + 1))
                            need(pe, s.exp, b * nh + (k - 1))
                            for qt in range(2):
                                o = bank[k % 2][:, qt * S:(qt + 1) * S]
                                if A.mask == "full":
                                    mm(o, identb[:, :], mb0[:, qt, :], True, False)
                                elif A.mask == "key":
                                    mm(o, onesb[:, :], mb3[:, bass.ts(b, S)], True, False)
                                last = mm(o, Qz[:, k, qt * P:(qt + 1) * P], keys_of(A, k), A.mask is None, True)
                            last.then_inc(s.scores.sem, 1)
                        elif kind == "turn":
                            need(pe, s.exp, b * nh + (k + 1))
                            need(pe, s.pt[k % 2], b * (nh // 2) + k // 2)
                            for kt in range(2):
                                for qt in range(2):
                                    last = turn(bank[2 + k % 2][:, kt * S + qt * P:kt * S + (qt + 1) * P],
                                                Pm[:, k % 2, qt * S + kt * P:qt * S + (kt + 1) * P])
                            last.then_inc(s.turn.sem, 1)
                        elif kind == "av":
                            need(pe, s.pt[k % 2], b * (nh // 2) + k // 2 + 1)
                            if A.n == 2:
                                need(pe, s.norm, k - 1)
                                for qt in range(2):
                                    for kt in range(2):
                                        last = mm(bank[4 + k % 2][:, qt * S:qt * S + 129],
                                                  PTs[:, k % 4, kt * S + qt * P:kt * S + (qt + 1) * P],
                                                  Vx(A)[:, 2 * k + kt, :], kt == 0, kt == 1)
                            else:
                                p = k // 2
                                if k == 0:
                                    fills_read(b, base)
                                if k % 2 == 0:
                                    need(pe, s.norm, b * 8 + (p - 1))
                                at = k * (A.dh + 1)
                                for qt in range(2):
                                    r = (k % 2) * 2 + qt
                                    for kt in range(2):
                                        last = mm(bank[4 + p % 2][:, r * P:(r + 1) * P],
                                                  PTs[:, k % 4, kt * S + qt * P:kt * S + (qt + 1) * P],
                                                  Vx(A)[:, kt, at:at + P], kt == 0, kt == 1)
                            last.then_inc(s.av.sem, 1)
                        elif kind in FILLS:
                            fill(kind, k, b, kinds, m, bank_of(m))
                batches(pe, A, body)

            def feed_forward(F):
                s = ffn_s[F.n]
                if F.n in (0, 1):
                    loaded(pe, f"l{F.n}f")
                gw = {0: gw0[:, :], 1: gw1[:, :], 2: vecT[:, V_GATE2:V_GATE2 + 8], 3: None}[F.n]

                def w_up(e, ft):
                    if F.n == 0:
                        sl = slice(ft * P, (ft + 1) * P) if e == 8 else slice(e * 256 + ft * P, e * 256 + (ft + 1) * P)
                        return (L0s1[:, sl], L0s2[:, sl]) if e == 8 else (L0w1[:, sl], L0w2[:, sl])
                    if F.n == 1:
                        return (L1w1[:, e * 512 + ft * P:e * 512 + (ft + 1) * P],)
                    if F.n == 2:
                        lo = e * 352 + ft * P
                        hi = lo + (96 if ft == 2 else P)
                        return L2w1[:, lo:hi], L2w3[:, lo:hi]
                    return (fcT[:, ft * P:(ft + 1) * P],)

                def w_down(e, ft):
                    if F.n == 0:
                        return L0s3[:, ft, :] if e == 8 else L0w3[:, e, ft, :]
                    if F.n == 1:
                        return L1w2[:, e, ft, :]
                    if F.n == 2:
                        return L2w2[0:96 if ft == 2 else P, e, ft, :]
                    return prT[:, ft, :]

                def ln(c):
                    need(pe, s.yn, c + 1)
                    for t in range(4):
                        last = turn(bank[6][:, t * P:(t + 1) * P], yn[:, t, :])
                    last.then_inc(s.lnf.sem, 1)

                def body(c, first):
                    if first is None:
                        if F.n < 3:
                            need(pe, s.lne, NCH - 1)
                            ln(NCH - 1)
                        return
                    xc = xnT[:, bass.ts(c, CH)]
                    for kind, k in ffn_schedule(F, first):
                        if kind == "gate" and k == 0:
                            need(pe, s.lne, 0 if first else c - 1)
                            plain(pe)
                            mm(bank[6][0:8, :], gw, xc).then_inc(s.gt.sem, 1)
                        elif kind == "gate" and k == 1:
                            need(pe, s.gte, c + 1)
                            need(pe, s.gle, c)
                            if F.n == 1:
                                need(pe, s.wte, c)
                            plain(pe)
                            for t in range(4):
                                last = turn(bank[7][:, t * 8:(t + 1) * 8], gTs[:, t * P:(t + 1) * P])
                            last.then_inc(s.gl.sem, 1)
                        elif kind == "gate" and k == 3:
                            need(pe, s.w, c + 1)
                            need(pe, s.gle, c + 1)
                            for t in range(4):
                                last = turn(bank[7][:, t * P:(t + 1) * P], wpad[:, t, :])
                            last.then_inc(s.wt.sem, 1)
                        elif kind == "up":
                            e, ft = k
                            u = e * F.FT + ft
                            ws = w_up(e, ft)
                            M = F.last if ft == F.FT - 1 else P
                            need(pe, s.g, c * F.U + (u - 1 if F.gated else u - 3))
                            if F.gated:
                                mm(bank[u % 2][0:M, :], ws[0], xc)
                                last = mm(bank[2 + u % 2][0:M, :], ws[1], xc)
                            else:
                                last = mm(bank[u % 4][:, :], ws[0], xc)
                            last.then_inc(s.h.sem, 1)
                        elif kind == "down":
                            e = k
                            need(pe, s.acc, c * F.E + (e - 1 if e >= 2 else 0))
                            if F.n == 1 and e == 8:
                                need(pe, s.wte, c + 1)
                                for t in range(4):
                                    last = mm(bank[4 + e % 2][:, t * P:(t + 1) * P], wTs[:, t * P:(t + 1) * P],
                                              b2pad[:, :])
                            else:
                                need(pe, s.g, c * F.U + (e + 1) * F.FT)
                                for t in range(4):
                                    for ft in range(F.FT):
                                        K = F.last if ft == F.FT - 1 else P
                                        slot = (e * F.FT + ft) % (2 * F.FT)
                                        last = mm(bank[4 + e % 2][:, t * P:(t + 1) * P],
                                                  G[0:K, slot, t * P:(t + 1) * P], w_down(e, ft),
                                                  ft == 0, ft == F.FT - 1)
                            last.then_inc(s.y.sem, 1)
                        elif kind == "ln":
                            need(pe, s.gte, c + 1)
                            ln(c - 1)
                chunks(pe, F, body)

            for n in range(4):
                attention(ATT[n])
                boundary(pe, "pe", 2 * n + 2)
                feed_forward(FFN[n])
                if n < 3:
                    boundary(pe, "pe", 2 * n + 3)

        @block.vector
        def _(dve):
            count = [0]

            def link(ins):
                count[0] += 1
                ins.then_inc(dve_chain, 1)
                dve.wait_ge(dve_chain, count[0])

            def move(dst, src, gain=None, bias=None):
                if gain is None and bias is None:
                    return dve.tensor_copy(dst, src)
                if bias is None:
                    return dve.tensor_scalar(dst, src, gain, None, ALU.mult)
                if gain is None:
                    return dve.tensor_scalar(dst, src, bias, None, ALU.add)
                return dve.tensor_scalar(dst, src, gain, bias, ALU.mult, ALU.add)

            def stats(src, n, chain, done, to=None):
                for t in range(n):
                    last = dve.bn_stats(st6[:, t, :], src[:, t, :])
                chain(last)
                plain(dve)
                to = mv if to is None else to
                for t in range(n):
                    last = dve.bn_aggr(to[:, t, :], st6[:, t, :])
                last.then_inc(done, 1)

            loaded(dve, "x")
            for n, (kind, k) in enumerate(SETUP):
                if kind == "ln":
                    need(dve, setup_normed, k)
                    stats(x[:, 4 * k:4 * k + 4, :], 4, link, setup_stats)
                if n % 2:
                    dve.wait_ge(setup.filled, n + 1)
                    setup_evac(move, kind, k, bank_of(n)).then_inc(setup.dve, 1)
            loaded(dve, "mask")
            loaded(dve, "small")
            dve.wait_ge(consts_ready, 2)
            dve.tensor_scalar(mb0[:, :, :], mask0[:, :, :], -1.0, -MASKED, ALU.add, ALU.mult)
            dve.tensor_reduce(seen[:, :], mask0[:, :, :], AX.X, ALU.max)
            link(dve.tensor_scalar(mb3[0:1, :], mask3[:, :], -1.0, -MASKED, ALU.add, ALU.mult))
            link(dve.tensor_scalar(pen[:, :], seen[:, :], -1.0, -MASKED, ALU.add, ALU.mult))
            link(dve.tensor_scalar(pen[:, :], pen[:, :], 10.0, None, ALU.mult))
            link(dve.tensor_tensor(pen[:, :], pen[:, :], pen[:, :], ALU.subtract))
            for qt in range(2):
                dve.tensor_scalar(bopen[:, qt, :], bo_bc[:, :], pen[:, qt:qt + 1], None, ALU.add)
            dve.wait_ge(setup.act, 3)
            dve.tensor_scalar(bqs[:, :], vecT[:, V_BQ:V_BQ + 1], ATT[2].scale, None,
                              ALU.mult).then_inc(consts_ready_dve, 1)
            boundary(dve, "dve", 1)

            def prep3_operands():
                loaded(dve, "l3")
                dve.wait_ge(prep3_zero, 1)
                dve.tensor_reduce(am[:, 0:1], fcn, AX.X, ALU.max, apply_absolute_value=True)
                dve.tensor_reduce(am[:, 1:2], prn, AX.X, ALU.max,
                                  apply_absolute_value=True).then_inc(prep3_rows, 1)
                dve.tensor_copy(NVflat[0:64, 0:128:18], nv_col[0:64, 0:1].to_broadcast([64, 8]))
                dve.tensor_copy(NVflat[64:128, 1:128:18],
                                nv_col[64:128, 0:1].to_broadcast([64, 8])).then_inc(prep3_done, 1)
                q3 = qtmp.rearrange("p (h e) -> p h e", e=64)
                link(dve.tensor_tensor(q3, L3Wq.rearrange("p (h e) -> p h e", e=64),
                                       nk_bc[:, :].unsqueeze(1).to_broadcast([P, 16, 64]), ALU.mult))
                link(dve.tensor_reduce(Wn, q3, AX.X, ALU.add))
                dve.wait_ge(prep3_max, 1)
                link(dve.tensor_scalar(qsc, amx, 1.0 / 127.0, None, ALU.mult))
                link(dve.reciprocal(rqs, qsc))
                for i, w in enumerate((fcn, prn)):
                    link(dve.tensor_scalar(w, w, rqs[:, i:i + 1], ROUND, ALU.mult, ALU.add))
                    link(dve.tensor_scalar(w, w, -ROUND, 127.0, ALU.add, ALU.min))
                    dve.tensor_scalar(w, w, -128.0, qsc[:, i:i + 1], ALU.max, ALU.mult).then_inc(prep3_done, 1)

            def attention(A):
                s = att_s[A.n]
                if A.n == 3:
                    prep3_operands()
                if A.n in prep:
                    r = prep[A.n]
                    for n, (kind, k) in enumerate(PREP2 if A.n == 2 else PREP3):
                        if n % 2:
                            dve.wait_ge(r.filled, n + 1)
                            prep_evac(move, kind, k, bank_of(n)).then_inc(r.dve, 1)
                dve.wait_ge(zeroed, A.n + 1)
                per_links = {0: 10, 1: 9, 2: 0, 3: 51}[A.n]
                start = count[0]
                nh = A.nh

                def body(b, kinds):
                    n = [0]

                    def chain(ins):
                        if A.n == 2:
                            return link(ins)
                        n[0] += 1
                        ins.then_inc(dve_chain, 1)
                        dve.wait_ge(dve_chain, b * per_links + (first_off(kinds) + n[0]))

                    for kind, k, m, base in steps(A, b, kinds):
                        if kind == "softmax":
                            need(dve, s.scores, b * nh + (k + 1))
                            v = bank[k % 2][:, :].rearrange("p (q s) -> p q s", s=S)
                            nm = negm[:, k % 4, :]
                            if A.null:
                                chain(dve.tensor_reduce(nm, v, AX.X, ALU.max, negate=True))
                                chain(dve.tensor_tensor(nm, nm, nsn[:, :, k], ALU.min))
                                dve.tensor_tensor(dn[:, k % 4, :], nm, nsn[:, :, k],
                                                  ALU.subtract).then_inc(s.negmax.sem, 1)
                            else:
                                dve.tensor_reduce(nm, v, AX.X, ALU.max, negate=True).then_inc(s.negmax.sem, 1)
                        elif kind == "turn" and k % 2:
                            need(dve, s.turn, b * nh + (k + 1))
                            need(dve, s.av, b * nh + (k - 3))
                            move(PTs[:, k % 4, :], bank[3][:, :]).then_inc(s.pt[1].sem, 1)
                        elif kind == "norm" and A.n == 2:
                            need(dve, s.av, k + 1)
                            o = bank[4 + k % 2][:, :].rearrange("p (q s) -> p q s", s=S)
                            chain(dve.reciprocal(rden[:, 0, 0, :], o[:, :, 128]))
                            need(dve, s.yn, k)
                            for qt in range(2):
                                last = dve.scalar_tensor_tensor(rtmp[:, qt, :], o[:, qt, 0:128],
                                                                rden[:, 0, 0, qt:qt + 1], bv_bc[:, :],
                                                                ALU.mult, ALU.add)
                            last.then_inc(s.norm.sem, 1)
                            need(dve, s.norm, k + 1)
                            chain(dve.tensor_tensor(xnew[:, 0:2, :], rtmp[:, 0:2, :], x[:, 2 * k:2 * k + 2, :],
                                                    ALU.add))
                            stats(xnew, 2, chain, s.stats.sem)
                        elif kind == "norm":
                            p = k
                            need(dve, s.av, b * nh + (2 * p + 2))
                            o = bank[4 + p % 2][:, :].rearrange("p (h q e) -> p h q e", h=2, q=2)
                            rd = rden[:, p % 2, :, :]
                            if A.null:
                                pnv = pn[:, :, 2 * p:2 * p + 2].rearrange("p q h -> p h q")
                                chain(dve.tensor_tensor(den[:, p % 2, :, :], o[:, :, :, A.dh], pnv, ALU.add))
                                chain(dve.reciprocal(rd, den[:, p % 2, :, :]))
                                dve.tensor_tensor(
                                    On[:, :, 1024 + 2 * p:1026 + 2 * p].rearrange("p q h -> p h q"), pnv, rd,
                                    ALU.mult)
                            else:
                                chain(dve.reciprocal(rd, o[:, :, :, A.dh]))
                            dst = On[:, :, 2 * p * A.dh:(2 * p + 2) * A.dh]
                            dve.tensor_tensor(dst.rearrange("p q (h e) -> p h q e", h=2), o[:, :, :, 0:A.dh],
                                              rd.unsqueeze(3).to_broadcast([P, 2, 2, A.dh]),
                                              ALU.mult).then_inc(s.norm.sem, 1)
                        elif kind == "resid":
                            mw = m - 1
                            need(dve, s.ring.filled, b * BATCH_FILLS[A.n] + (mw + 1))
                            ps = bank_of(mw)[:, 0:S].rearrange("p (t d) -> p t d", d=D)
                            need(dve, s.yn if not A.null else s.onorm, b)
                            if A.null:
                                dve.tensor_copy(osb[:, :, :], ps).then_inc(s.ring.dve.sem, 1)
                                need(dve, s.ring.dve, b * (BATCH_FILLS[A.n] // 2) + mw // 2 + 1)
                                stats(osb, 2, chain, s.ostats.sem, mvo)
                            else:
                                if A.n == 0:
                                    dve.tensor_tensor(rtmp[:, 0:2, :], ps, bopen[:, :, :],
                                                      ALU.add).then_inc(s.ring.dve.sem, 1)
                                    need(dve, s.ring.dve, b * (BATCH_FILLS[A.n] // 2) + mw // 2 + 1)
                                    chain(dve.tensor_tensor(xnew[:, 0:2, :], rtmp[:, 0:2, :],
                                                            x[:, bass.ds(b * 2, 2), :], ALU.add))
                                else:
                                    dve.tensor_tensor(xnew[:, 0:2, :], ps, x[:, bass.ds(b * 2, 2), :],
                                                      ALU.add).then_inc(s.ring.dve.sem, 1)
                                    need(dve, s.ring.dve, b * (BATCH_FILLS[A.n] // 2) + mw // 2 + 1)
                                stats(xnew, 2, chain, s.stats.sem)
                        elif kind == "resid2":
                            bl = b if kinds == "epilogue" else b - 1
                            need(dve, s.onorm, bl + 1)
                            need(dve, s.yn, bl)
                            chain(dve.tensor_tensor(xnew[:, 0:2, :], on2[:, :, :], x[:, bass.ds(bl * 2, 2), :],
                                                    ALU.add))
                            stats(xnew, 2, chain, s.stats.sem)
                        elif kind in FILLS and m % 2 and not (kind == "wo" and k == 0):
                            need(dve, s.ring.filled, b * BATCH_FILLS.get(A.n, 0) + (m + 1))
                            att_evac(A, move, kind, k, b, kinds, bank_of(m)).then_inc(s.ring.dve.sem, 1)
                    used[kinds] = n[0]

                used = {}

                def first_off(kinds):
                    if kinds in ("prologue", "first"):
                        return start
                    if kinds == "epilogue":
                        return start + used["first"] - per_links + used["last"]
                    return start + used["first"] - per_links
                batches(dve, A, body)
                if A.n != 2:
                    assert used["mid"] == per_links, (A.n, used, per_links)
                    count[0] = start + used["first"] + (B - 2) * used["mid"] + used["last"] + used["epilogue"]

            def feed_forward(F):
                s = ffn_s[F.n]
                per_links = {0: 11, 1: 8, 2: 11, 3: 0}[F.n]
                start = count[0]
                used = []

                def body(c, first):
                    if first is None:
                        return
                    n = [0]

                    def chain(ins):
                        n[0] += 1
                        ins.then_inc(dve_chain, 1)
                        dve.wait_ge(dve_chain, c * per_links + (start + n[0]))

                    for kind, k in ffn_schedule(F, first):
                        if kind == "gate" and k == 1:
                            need(dve, s.gl, c + 1)
                            src = bank[7][:, 0:32].rearrange("p (t e) -> p t e", e=8)
                            if F.n == 1:
                                ins = dve.tensor_tensor(lg[:, :, :], src,
                                                        swb_bc[:, :].unsqueeze(1).to_broadcast([P, 4, 8]), ALU.add)
                            else:
                                ins = dve.tensor_copy(lg[:, :, :], src)
                            ins.then_inc(s.gle.sem, 1)
                            need(dve, s.gle, c + 1)
                            plain(dve)
                            for t in range(4):
                                last = dve.max(mx[:, t, :], lg[:, t, :])
                            chain(last)
                            if F.k == 1:
                                dve.tensor_tensor(gd[:, :, :], lg[:, :, :],
                                                  mx[:, :, 0:1].to_broadcast([P, 4, 8]),
                                                  ALU.subtract).then_inc(s.gd.sem, 1)
                            else:
                                dve.tensor_tensor(gd[:, :, 0], mx[:, :, 1], mx[:, :, 0],
                                                  ALU.subtract).then_inc(s.gd.sem, 1)
                            plain(dve)
                            for t in range(4):
                                last = dve.max_index(mi[:, t, :], mx[:, t, :], lg[:, t, :])
                            chain(last)
                            chain(dve.tensor_copy(mif[:, :, :], mi[:, :, :]))
                            io = iota[:, :].unsqueeze(1).to_broadcast([P, 4, 8])
                            dve.tensor_tensor(oh1[:, :, :], io, mif[:, :, 1:2].to_broadcast([P, 4, 8]),
                                              ALU.is_equal)
                            chain(dve.tensor_tensor(oh0[:, :, :], io, mif[:, :, 0:1].to_broadcast([P, 4, 8]),
                                                    ALU.is_equal))
                        elif kind == "gate" and k == 2:
                            need(dve, s.gx, c + 1)
                            if F.k == 1:
                                chain(dve.tensor_reduce(gs[:, :], ge[:, :, :], AX.X, ALU.add))
                                chain(dve.reciprocal(gr[:, :], gs[:, :]))
                                dve.tensor_tensor(wpad[:, :, 0:8], oh0[:, :, :],
                                                  gr[:, :].unsqueeze(2).to_broadcast([P, 4, 8]),
                                                  ALU.mult).then_inc(s.w.sem, 1)
                                need(dve, s.w, c + 1)
                            else:
                                chain(dve.tensor_scalar(gs[:, :], ge[:, :, 0], 1.0, None, ALU.add))
                                chain(dve.reciprocal(gr[:, :], gs[:, :]))
                                chain(dve.tensor_tensor(gp[:, :], ge[:, :, 0], gr[:, :], ALU.mult))
                                dve.tensor_tensor(oh0[:, :, :], oh0[:, :, :],
                                                  gr[:, :].unsqueeze(2).to_broadcast([P, 4, 8]), ALU.mult)
                                chain(dve.tensor_tensor(oh1[:, :, :], oh1[:, :, :],
                                                        gp[:, :].unsqueeze(2).to_broadcast([P, 4, 8]), ALU.mult))
                                chain(dve.tensor_tensor(wpad[:, :, 0:8], oh0[:, :, :], oh1[:, :, :], ALU.add))
                        elif kind == "gate" and k == 3:
                            need(dve, s.wt, c + 1)
                            dve.tensor_copy(wTs[:, :], bank[7][:, :]).then_inc(s.wte.sem, 1)
                        elif kind == "up" and F.gated:
                            e, ft = k
                            u = e * F.FT + ft
                            M = F.last if ft == F.FT - 1 else P
                            need(dve, s.silu, c * F.U + (u + 1))
                            need(dve, s.y, c * F.E + (e - 1 if e >= 2 else 0))
                            dve.tensor_tensor(G[0:M, u % (2 * F.FT), :], sg[0:M, u % 2, :],
                                              bank[2 + u % 2][0:M, :], ALU.mult).then_inc(s.g.sem, 1)
                        elif kind == "down":
                            e = k
                            need(dve, s.y, c * F.E + (e + 1))
                            Y = bank[4 + e % 2][:, :].rearrange("p (t d) -> p t d", d=D)
                            need(dve, s.acc, c * F.E + e)
                            if F.n == 3:
                                need(dve, s.stats, c)
                                last = dve.tensor_tensor(acc[:, :, :], Y,
                                                         bproj_bc[:, :].unsqueeze(1).to_broadcast([P, 4, D]), ALU.add)
                            elif e >= F.routed:
                                last = dve.tensor_tensor(acc[:, :, :], Y, acc[:, :, :], ALU.add)
                            else:
                                for t in range(4):
                                    w = wpad[:, t, e:e + 1]
                                    if e == 0:
                                        last = dve.tensor_scalar(acc[:, t, :], Y[:, t, :], w, None, ALU.mult)
                                    else:
                                        last = dve.scalar_tensor_tensor(acc[:, t, :], Y[:, t, :], w, acc[:, t, :],
                                                                        ALU.mult, ALU.add)
                            last.then_inc(s.acc.sem, 1)
                        elif kind == "fin":
                            need(dve, s.acc, c * F.E + F.E)
                            if F.n == 3:
                                dve.tensor_tensor(x[:, bass.ds(c * 4, 4), :], acc[:, :, :],
                                                  x[:, bass.ds(c * 4, 4), :], ALU.add).then_inc(s.stats.sem, 1)
                            else:
                                need(dve, s.yn, c)
                                chain(dve.tensor_tensor(xnew[:, :, :], acc[:, :, :], x[:, bass.ds(c * 4, 4), :],
                                                        ALU.add))
                                stats(xnew, 4, chain, s.stats.sem)
                    used.append(n[0])
                    assert F.n == 3 or n[0] == per_links, (F.n, n[0])
                chunks(dve, F, body)
                count[0] = start + used[0] * NCH

            for n in range(4):
                attention(ATT[n])
                boundary(dve, "dve", 2 * n + 2)
                feed_forward(FFN[n])
                if n < 3:
                    boundary(dve, "dve", 2 * n + 3)


def kernel(**inputs):
    import concourse.bacc as _bacc
    from concourse.bass_utils import run_bass_kernel_spmd as _run

    nc = _bacc.Bacc("TRN2", target_bir_lowering=False, num_devices=1)
    arrays, args = {}, {}
    for name in inputs:
        v = np.ascontiguousarray(inputs[name])
        arrays[f"in_{name}"] = v
        args[name] = nc.dram_tensor(f"in_{name}", v.shape, mybir.dt.from_np(v.dtype), kind="ExternalInput").ap()
    out = nc.dram_tensor("out", (B, S, D), F32, kind="ExternalOutput").ap()
    build(nc, args, out)
    r = _run(nc, [arrays], core_ids=[0])
    return r.results[0]["out"]
```

```python
from contextlib import ExitStack

import numpy as np

import concourse.bass as bass
from concourse import mybir

F32 = mybir.dt.float32
BF16 = mybir.dt.bfloat16
F16 = mybir.dt.float16
U32 = mybir.dt.uint32
U8 = mybir.dt.uint8
ALU = mybir.AluOpType
ACT = mybir.ActivationFunctionType
AX = mybir.AxisListType
RMAX = bass.bass_isa.ReduceOp.max

P = 128
B, S, D = 8, 256, 128
T = B * S
NT = T // P
DC = 96
EPS = 1e-5
MASKED = -3e38
CH = 512
NCH = T // CH
ROUND = 12582912.0

V_B1, V_BFC, V_GAMMA, V_BETA, V_GNORM, V_BQ, V_BK, V_GATE2, V_N = 0, 32, 36, 37, 38, 39, 40, 41, 49

class Attention:
    def __init__(self, n, nh, dh, scale, pieces, mask, null):
        self.n, self.nh, self.dh, self.scale = n, nh, dh, scale
        self.pieces, self.mask, self.null = pieces, mask, null


class FeedForward:
    def __init__(self, n, E, routed, FT, last, gated, k):
        self.n, self.E, self.routed, self.FT, self.last, self.gated, self.k = n, E, routed, FT, last, gated, k
        self.U = (8 if n == 1 else E) * FT


class Counted:

    def __init__(self, sem, base):
        self.sem, self.base = sem, base


class Ring:

    def __init__(self, filled, act, dve):
        self.filled, self.act, self.dve = filled, act, dve


class AttentionSems:
    def __init__(self, c):
        self.ring = Ring(c["filled"], c["act"], c["dve"])
        self.scores, self.negmax, self.exp, self.turn = c["scores"], c["negmax"], c["exp"], c["turn"]
        self.pt = [c["pt0"], c["pt1"]]
        self.av, self.norm, self.stats, self.yn = c["av"], c["norm"], c["stats"], c["yn"]
        self.vhigh, self.vlow = c["vhigh"], c["vlow"]
        self.ctxb, self.qm, self.ostats, self.onorm = c["ctxb"], c["qm"], c["ostats"], c["onorm"]


class FeedForwardSems:
    def __init__(self, c):
        self.h, self.silu, self.g, self.y, self.acc = c["h"], c["silu"], c["g"], c["y"], c["acc"]
        self.stats, self.yn, self.lnf, self.lne = c["stats"], c["yn"], c["lnf"], c["lne"]
        self.gt, self.gte, self.gl, self.gle = c["gt"], c["gte"], c["gl"], c["gle"]
        self.gd, self.gx, self.w, self.wt, self.wte = c["gd"], c["gx"], c["w"], c["wt"], c["wte"]


ATT = [
    Attention(n=0, nh=16, dh=64, scale=0.125, pieces=8, mask="full", null=False),
    Attention(n=1, nh=16, dh=8, scale=8.0 ** -0.5, pieces=1, mask=None, null=False),
    Attention(n=2, nh=8, dh=128, scale=128.0 ** -0.5, pieces=0, mask=None, null=False),
    Attention(n=3, nh=16, dh=64, scale=0.125, pieces=9, mask="key", null=True),
]
FFN = [
    FeedForward(n=0, E=9, routed=8, FT=2, last=128, gated=True, k=2),
    FeedForward(n=1, E=9, routed=8, FT=4, last=128, gated=False, k=1),
    FeedForward(n=2, E=8, routed=8, FT=3, last=96, gated=True, k=2),
    FeedForward(n=3, E=1, routed=0, FT=4, last=128, gated=False, k=0),
]

BATCH_FILLS = {0: 18, 1: 4, 3: 22}

WIDE = {1: [("k", 3)], 2: [("outT", -2)], 3: [("v", 1)], 4: [("q", 3)], 5: [("v", 3), ("outT", -1)],
        7: [("wo", 0), ("resid", 0), ("q", 0), ("k", 0)], 8: [("outT", 0)], 9: [("q", 1)],
        10: [("k", 1)], 11: [("v", 0)], 12: [("outT", 1), ("v", 2)], 13: [("q", 2), ("ln", 0)],
        14: [("k", 2)]}
WIDE_NULL = {0: [("q", 3)], 1: [("k", 3)], 2: [("outT", -2)], 3: [("v", 1)], 4: [("outN", 0), ("v", 3)],
             5: [("outT", -1)], 7: [("wo", 0), ("resid", 0), ("turns", 0), ("q", 0), ("k", 0)],
             8: [("outT", 0)], 9: [("q", 1)], 11: [("v", 0), ("k", 1)],
             12: [("v", 2), ("outT", 1), ("resid2", 0)], 13: [("q", 2), ("sn", 0)], 14: [("k", 2)],
             15: [("ln", 0), ("snt", 0)]}
NARROW = {4: [("outT", -1)], 7: [("wo", 0), ("resid", 0)], 13: [("ln", 0), ("turns", 0)]}
PREVIOUS = [("outT", -2), ("outT", -1), ("outN", 0), ("wo", 0), ("resid", 0), ("resid2", 0), ("ln", 0)]
OWN = [("q", 3), ("k", 3), ("v", 1), ("v", 3)]


def head_steps(i):
    st = [("scores", i), ("softmax", i)] if i < 16 else []
    st += [("turn", i - 2)] if i < 18 else []
    st += [("low", i - 3)] if i < 19 else []
    st.append(("av", i - 4))
    if i % 2:
        st.append(("norm", (i - 4) // 2))
    return st


def att_schedule(A, first, last):
    table = WIDE_NULL if A.null else WIDE if A.pieces >= 8 else NARROW
    st = []
    for i in range(A.nh):
        st += [(kind, k) for kind, k in head_steps(i) if k >= 0 or not first]
        for step in table.get(i, []):
            if step in PREVIOUS:
                if not first:
                    st.append(step)
            elif step in OWN or step[0] in ("outT", "turns") or not last:
                st.append(step)
    return st


def att_early(A):
    if A.dh != 64:
        return [(kind, j) for kind in "kv" for j in range(4)]
    return [("k", 0), ("k", 1), ("k", 2), ("v", 0), ("v", 2)]


def att_prologue(A):
    if A.n == 1:
        return [("q", j) for j in range(4)] + [("turns", 0)]
    return [("q", 0), ("q", 1), ("q", 2)] + ([("sn", 0), ("snt", 0)] if A.null else []) + [("turns", 0)]


def att_epilogue(A):
    st = []
    for i in range(16, 20):
        st += [(kind, k - 16 if kind != "norm" else k - 8) for kind, k in head_steps(i)]
        if i == 17 and A.dh == 64:
            st.append(("outT", -2))
    st.append(("outT", -1))
    return st + ([("outN", 0)] if A.null else []) + PREVIOUS[3:5] + (
        [("resid2", 0)] if A.null else [])


def single_schedule(A):
    st = [("q", j) for j in range(4)]
    for i in range(A.nh + 3):
        if i < A.nh:
            st += [("scores", i), ("softmax", i)]
        if 1 <= i <= A.nh:
            st.append(("turn", i - 1))
        if 2 <= i <= A.nh + 1:
            st += [("av", i - 2), ("norm", i - 2)]
        if 4 <= i:
            st.append(("ln", i - 4))
    return st


def kind_steps(A, kinds):
    if kinds == "single":
        return single_schedule(A)
    if kinds == "early":
        return att_early(A)
    if kinds == "prologue":
        return att_prologue(A)
    if kinds == "epilogue":
        return att_epilogue(A)
    return att_schedule(A, kinds == "first", kinds == "last")


FILLS = ("q", "k", "v", "sn", "snt", "outT", "outN", "wo", "ln", "turns")


def ffn_schedule(F, first):
    st = []
    if F.k:
        st.append(("gate", 0))
    for e in range(F.E):
        if e * F.FT < F.U:
            for ft in range(F.FT):
                st.append(("up", (e, ft)))
                if F.k and e == 0 and ft == 1:
                    st.append(("gate", 1))
                if F.k and e == 1 and ft == 1:
                    st.append(("gate", 2))
        if e == 1 and F.n == 1:
            st.append(("gate", 3))
        if e >= 1:
            st.append(("down", e - 1))
        if e == 2:
            st += [("attln", 0)] if first else [("ln", 0)]
    st.append(("down", F.E - 1))
    if F.n == 3 and first:
        st.append(("attln", 0))
    return st + [("fin", 0)]


def build(nc, a, out):
    ctx = ExitStack()
    with ctx:
        def sb(name, shape, dt=F32):
            return ctx.enter_context(nc.sbuf_tensor(name, shape, dt))

        def sem(name):
            return ctx.enter_context(nc.semaphore(name))

        bank = [ctx.enter_context(nc.psum_tensor(f"bank{i}", [P, 512], F32)) for i in range(8)]

        x = sb("x", [P, NT, D])
        xnT = sb("xnT", [P, T])
        ctxT = sb("ctxT", [DC, T])
        R0 = sb("R0", [P, 11520])
        R1 = sb("R1", [P, 8704])
        ident = sb("ident", [P, P])
        identb = sb("identb", [P, P], BF16)
        onesb = sb("onesb", [P, P], BF16)
        iota = sb("iota", [P, 8])
        vecs = sb("vecs", [V_N, P])
        vecT = sb("vecT", [P, V_N])
        w1T = sb("w1T", [P, 512])
        headmask = sb("headmask", [P, 16])
        w2a = sb("w2a", [P, 384])
        bqs = sb("bqs", [P, 1])
        bo_bc = sb("bo_bc", [P, D])
        bv_bc = sb("bv_bc", [P, D])
        gout_bc = sb("gout_bc", [P, D])
        bproj_bc = sb("bproj_bc", [P, D])
        swb_bc = sb("swb_bc", [P, 8])
        nk_bc = sb("nk_bc", [P, 64])
        nv_col = sb("nv_col", [P, 1])
        gw0 = sb("gw0", [P, 8])
        gw1 = sb("gw1", [P, 8])
        b2pad = sb("b2pad", [P, D])
        mask0 = sb("mask0", [P, 2, S], U8)
        mask3 = sb("mask3", [1, B * S], U8)
        xH = sb("xH", [P, T], F16)
        xL = sb("xL", [P, T], F16)
        upscale = sb("upscale", [P, 3])
        upback = sb("upback", [P, 3])
        upmax = sb("upmax", [P, 3, 16])
        uprow = sb("uprow", [P, 3])
        uprowall = sb("uprowall", [P, 3])
        mb0 = sb("mb0", [P, 2, S], BF16)
        mb3 = sb("mb3", [P, B * S], BF16)
        bopen = sb("bopen", [P, 2, D])
        seen = sb("seen", [P, 2])
        pen = sb("pen", [P, 2])
        neghalf = sb("neghalf", [P, NT])

        Qz = sb("Qz", [P, 16, S])
        kT = sb("kT", [P, 8, S])
        VxF = sb("VxF", [P, 2304])
        VxH = VxF[:, 0:1152].bitcast(F16)
        VxL = VxF[:, 1152:2304].bitcast(F16)
        vscale = sb("vscale", [P, 4])
        vmax = sb("vmax", [P, 4])
        vmaxall = sb("vmaxall", [P, 4])
        Pm = sb("Pm", [P, 4, 512])
        PTs = sb("PTs", [P, 4, 512])
        PTf = PTs[:, :, :].rearrange("p u s -> p (u s)")
        PTh = PTf[:, 0:1024].bitcast(F16).rearrange("p (u s) -> p u s", s=512)
        PTl = PTf[:, 1024:2048].bitcast(F16).rearrange("p (u s) -> p u s", s=512)
        On = sb("On", [P, 2, 9 * P])
        OT = sb("OT", [P, 9, S])
        ctxb = sb("ctxb", [DC, S])
        negm = sb("negm", [P, 4, 2])
        rden = sb("rden", [P, 2, 2, 2])
        den = sb("den", [P, 2, 2, 2])
        nsn = sb("nsn", [P, 2, 16])
        dn = sb("dn", [P, 4, 2])
        pn = sb("pn", [P, 2, 16])
        xnew = sb("xnew", [P, 4, D])
        rtmp = sb("rtmp", [P, 4, D])
        st6 = sb("st6", [P, 4, 6])
        mv = sb("mv", [P, 4, 2])
        ve = sb("ve", [P, 4])
        rstd = sb("rstd", [P, 4])
        yn = sb("yn", [P, 4, D])
        scrap = sb("scrap", [P, 1])
        mvo = sb("mvo", [P, 2, 2])

        G = Qz[:, :, :].rearrange("p h s -> p (h s)").rearrange("p (g s) -> p g s", s=CH)
        sg = Pm
        OTf = OT[:, :, :].rearrange("p c s -> p (c s)")
        acc = OTf[:, 0:512].rearrange("p (t d) -> p t d", d=D)
        gTs = OTf[0:8, 512:1024]
        wTs = OTf[:, 1024:1536]
        ctok = PTs[:, :, :].rearrange("p u s -> p (u s)")[:, 0:NT * DC].rearrange("p (t c) -> p t c", c=DC)
        w1nat = OTf[:, 0:448]
        rtmpf = rtmp[:, :, :].rearrange("p t d -> p (t d)")
        st0 = rtmpf[:, 0:96].rearrange("p (t k) -> p t k", k=6)
        mv0 = rtmpf[:, 96:128].rearrange("p (t k) -> p t k", k=2)
        ve0 = rtmpf[:, 128:144]
        rstd0 = rtmpf[:, 144:160]
        normed0 = (yn, xnew)
        lg = sb("lg", [P, 4, 8])
        mx = sb("mx", [P, 4, 8])
        mi = sb("mi", [P, 4, 8], U32)
        mif = sb("mif", [P, 4, 8])
        oh0 = sb("oh0", [P, 4, 8])
        oh1 = sb("oh1", [P, 4, 8])
        gd = sb("gd", [P, 4, 8])
        ge = sb("ge", [P, 4, 8])
        gs = sb("gs", [P, 4])
        gr = sb("gr", [P, 4])
        gp = sb("gp", [P, 4])
        wpad = sb("wpad", [P, 4, P])

        def cols(t, lo, n):
            return t[:, lo:lo + n]

        L0Wq = cols(R0, 0, 1024)
        L0Wkv = R0[0:DC, 1024:3072]
        L0Wo = cols(R0, 3072, 1024).rearrange("p (c d) -> p c d", d=D)
        L0w1 = cols(R0, 4608, 2048)
        L0w2 = cols(R0, 6656, 2048)
        L0s1 = cols(R0, 8704, 256)
        L0s2 = cols(R0, 8960, 256)
        L0w3 = cols(R0, 9216, 2048).rearrange("p (e f d) -> p e f d", f=2, d=D)
        L0s3 = cols(R0, 11264, 256).rearrange("p (f d) -> p f d", d=D)
        n1 = cols(R0, 0, 2816)
        n3 = cols(R0, 2816, 2816)
        n2 = cols(R0, 5632, 2816).rearrange("p (e f) -> p e f", f=352)
        L3Wq = cols(R0, 0, 1024)
        L3Wkv = R0[0:DC, 1024:3072]
        L3Wo = cols(R0, 3072, 1152).rearrange("p (c d) -> p c d", d=D)
        fcn = cols(R0, 4224, 512)
        prn = cols(R0, 4736, 512)
        fcT = cols(R0, 5248, 512)
        prT = cols(R0, 5760, 512).rearrange("p (c d) -> p c d", d=D)
        Afc = R0[0:16, 6272:6400]
        Apr = R0[0:16, 6400:6912]
        Bfc = cols(R0, 6912, 64).rearrange("p (c r) -> p c r", r=16)
        Bpr = cols(R0, 6976, 16)
        BT = R0[0:16, 6992:7632]
        qtmp = cols(R0, 7632, 1024)
        Wn = cols(R0, 8656, 16)
        NVsel = cols(R0, 8672, 128).rearrange("p (c h) -> p c h", h=16)
        NVflat = cols(R0, 8672, 128)
        am = cols(R0, 8800, 2)
        amx = cols(R0, 8802, 2)
        qsc = cols(R0, 8804, 2)
        rqs = cols(R0, 8806, 2)
        sn16 = R0[0:16, 8832:8832 + S]
        osb = cols(R0, 9088, 2 * D).rearrange("p (t d) -> p t d", d=D)
        on1 = cols(R0, 9344, 2 * D).rearrange("p (t d) -> p t d", d=D)
        L1w1 = cols(R1, 512, 4096)
        L1w2 = cols(R1, 4608, 4096).rearrange("p (e f d) -> p e f d", f=4, d=D)
        L2w2 = cols(R1, 5632, 3072).rearrange("p (e f d) -> p e f d", f=3, d=D)

        def part(t, lo, n, at=0, m=None):
            v = t[:, lo:lo + n].bitcast(F16)
            return v[:, at:at + (2 * n if m is None else m)]

        UP = {0: (R0, 4096, 9), 1: (R1, 0, 8)}

        def block_parts(n, i, at=0, m=None):
            t, lo, _ = UP[n]
            return tuple(part(t, lo + 512 * i + 256 * j, 256, at, m) for j in range(2))

        def blocks_before(n):
            return 0 if n == 0 else UP[0][2]

        def l2_parts(which, at, m):
            lo = 0 if which == "n1" else 2816
            return tuple(part(R1, lo + 1408 * j, 1408, at, m) for j in range(2))

        loads = {n: sem(f"loaded_{n}") for n in
                 ("x", "ctx", "vecs", "small", "l1a", "l0a", "mask", "l0f", "l1f", "l2a", "l2f", "l3")}
        LOADED = dict(x=1, ctx=1, vecs=8, small=11, l1a=4, l0a=3, mask=2, l0f=6, l1f=3, l2a=3, l2f=3, l3=9)
        engines_done = {n: sem(f"{n}_phase_done") for n in ("pe", "act", "dve", "pool")}
        consts_ready = sem("consts_ready")
        consts_ready_dve = sem("mask_bias_ready")
        waits_met = {e.engine: sem(n + "_waits_met")
                     for n, e in (("pe", nc.tensor), ("dve", nc.vector), ("pool", nc.gpsimd))}
        pool_chain = sem("pool_chain")
        dve_chain = sem("dve_chain")
        out_written = sem("out_written")

        def ring(tag):
            return Ring(sem(f"{tag}_filled"), sem(f"{tag}_read_by_act"), sem(f"{tag}_read_by_dve"))

        setup = ring("setup")
        prep = {2: ring("prep2"), 3: ring("prep3")}
        setup_stats = sem("setup_stats")
        setup_rstd = sem("setup_rstd")
        split_chain = sem("split_chain")
        up_rows = sem("up_rows")
        up_max = sem("up_max")
        up_scale = sem("up_scale")
        up_high = sem("up_high")
        up_low = sem("up_low")
        x_split = sem("x_split")
        prep2_high = sem("prep2_high")
        prep2_low = sem("prep2_low")
        setup_normed = sem("setup_normed")
        prep3_rows = sem("prep3_rows")
        vmax3_rows = sem("vmax3_rows")
        vmax3_max = sem("vmax3_max")
        prep3_max = sem("prep3_max")
        prep3_done = sem("prep3_operands")
        prep3_zero = sem("prep3_zero")
        zeroed = sem("layer2_ones_set")
        ones_set = sem("scaled_ones_set")
        setup_vmax = sem("setup_vmax")
        setup_vmaxall = sem("setup_vmaxall")

        def counted(names, tag, layers):
            sems = {n: sem(tag + n) for n in names}
            total = dict.fromkeys(names, 0)
            out = []
            for counts in layers:
                out.append({n: Counted(sems[n], total[n]) for n in names})
                for n, c in counts.items():
                    total[n] += c
            return out

        def att_counts(A):
            nh, nb = (A.nh, 1) if A.n == 2 else (A.nh * B, B)
            kinds = ["early", "single"] if A.n == 2 else ["early", "prologue", "first"] + ["mid"] * (B - 2) + ["last", "epilogue"]
            fills = sum(s[0] in FILLS for k in kinds for s in kind_steps(A, k))
            vfills = [m % 2 for k in kinds if A.n != 2 for kind, j, m, _ in steps(A, 0, k) if kind == "v"]
            return dict(vhigh=sum(vfills), vlow=len(vfills) - sum(vfills), filled=fills, act=(fills + 1) // 2, dve=fills // 2, scores=nh, negmax=nh, exp=nh,
                        turn=nh, pt0=nh // 2 if A.n == 2 else nh, pt1=nh // 2 if A.n == 2 else nh, av=nh, norm=nh if A.n == 2 else nh // 2, stats=B,
                        yn=B, ctxb=B if A.dh == 64 else 0, qm=4 * B if A.n == 1 else 0,
                        ostats=B if A.null else 0, onorm=B if A.null else 0)

        def ffn_counts(F):
            routed = NCH if F.k else 0
            return dict(h=F.U * NCH, silu=F.U * NCH if F.gated else 0, g=F.U * NCH, y=F.E * NCH, acc=F.E * NCH,
                        stats=NCH, yn=NCH if F.n < 3 else 0, lnf=NCH + 1 if F.n < 3 else 1,
                        lne=NCH + 1 if F.n < 3 else 1, gt=routed, gte=routed, gl=routed, gle=routed, gd=routed,
                        gx=routed, w=NCH if F.k == 1 else 0, wt=NCH if F.k == 1 else 0,
                        wte=NCH if F.k == 1 else 0)

        def need(eng, s, value):
            if not isinstance(value, int) or value > 0:
                if isinstance(s, Counted):
                    eng.wait_ge(s.sem, s.base + value)
                else:
                    eng.wait_ge(s, value)

        def plain(eng):
            eng.sem_inc(waits_met[eng.engine], 1)

        def loaded(eng, name):
            eng.wait_ge(loads[name], 16 * LOADED[name])

        def boundary(eng, name, phase):
            eng.drain().then_inc(engines_done[name], 1)
            for other in engines_done:
                if other != name:
                    eng.wait_ge(engines_done[other], phase)

        def ring_base(A, b, kinds):
            per = BATCH_FILLS[A.n]
            n0 = sum(s[0] in FILLS for s in att_early(A) + att_prologue(A))
            if kinds == "first":
                return n0
            f0 = sum(s[0] in FILLS for s in att_schedule(A, True, False))
            return n0 + f0 - per

        def steps(A, b, kinds):
            st = kind_steps(A, kinds)
            if kinds == "early":
                base = 0
            elif kinds in ("single", "prologue"):
                base = len(att_early(A))
            elif kinds == "epilogue":
                base = ring_base(A, b, "last") + sum(s[0] in FILLS for s in kind_steps(A, "last")) - BATCH_FILLS[A.n]
            else:
                base = ring_base(A, b, kinds)
                if kinds == "mid":
                    assert sum(s[0] in FILLS for s in st) == BATCH_FILLS[A.n], (A.n, st)
            n = base
            for kind, k in st:
                if kind in ("wo", "snt"):
                    assert n % 2 == 1, (A.n, kinds, n)
                yield kind, k, n, base
                n += kind in FILLS

        def v_of(A, kinds, parity):
            return [m for kind, k, m, _ in steps(A, 0, kinds) if kind == "v" and m % 2 == parity]

        def v_count(A, parity):
            return len(v_of(A, "mid", parity))

        def v_done(A, b, kinds, m, parity):
            before = 0 if kinds == "early" else len(v_of(A, "early", parity))
            if kinds not in ("early", "first"):
                before += len(v_of(A, "first", parity)) - v_count(A, parity)
            return before + v_of(A, kinds, parity).index(m) + 1

        def all_fills(A):
            parts = (["early", "single"] if A.n == 2 else
                     ["early", "prologue", "first"] + ["mid"] * (B - 2) + ["last", "epilogue"])
            return sum(step[0] in FILLS for k in parts for step in kind_steps(A, k))

        def batches(eng, A, body):
            if A.n == 2:
                body(0, "single")
                return
            body(0, "prologue")
            body(0, "first")
            with eng.Fori(1, B - 1) as b:
                body(b, "mid")
            body(B - 1, "last")
            body(B, "epilogue")

        def chunks(eng, F, body):
            body(0, True)
            with eng.Fori(1, NCH) as c:
                body(c, False)

        att_s = [AttentionSems(c) for c in
                 counted(list(att_counts(ATT[0])), "att_", [att_counts(A) for A in ATT])]
        ffn_s = [FeedForwardSems(c) for c in
                 counted(list(ffn_counts(FFN[0])), "ffn_", [ffn_counts(F) for F in FFN])]

        Vx2 = VxF[:, 0:16 * 129].rearrange("p (t e) -> p t e", e=129)

        def Vheads(A, kt, part):
            e = A.dh + 1
            at = 1152 if A.dh == 64 else 16 * e
            return part[:, kt * at:kt * at + 16 * e].rearrange("p (h e) -> p h e", e=e)

        def Vhead(A, b, kt, h, part):
            if A.dh == 64:
                return Vheads(A, kt, part)[:, h, :]
            return part[:, bass.ds(b * 288 + (kt * 144 + 9 * h), 9)]

        def v_parts(A, k, src):
            if A.dh == 64:
                return [((k // 2, slice(8 * (k % 2), 8 * (k % 2) + 8)), src[:, :].rearrange("p (h e) -> p h e", e=64))]
            return [((4 * k + t, slice(0, 16)), src[:, t * 128:t * 128 + 128].rearrange("p (h e) -> p h e", e=8))
                    for t in range(4)]

        def v_high(A, move, k, src):
            for (kt, hs), v in v_parts(A, k, src):
                last = move(Vheads(A, kt, VxH)[:, hs, 0:A.dh], v, vscale[:, A.n:A.n + 1])
            return last

        def v_low(A, dve, k, src):
            for (kt, hs), v in v_parts(A, k, src):
                last = dve.scalar_tensor_tensor(Vheads(A, kt, VxL)[:, hs, 0:A.dh], v, vscale[:, A.n:A.n + 1],
                                                Vheads(A, kt, VxH)[:, hs, 0:A.dh], ALU.mult, ALU.subtract)
            return last

        AWq = {0: L0Wq, 1: w1T[:, 0:128], 2: w2a[:, 0:128], 3: L3Wq}
        AWk = {0: L0Wkv[:, 0:1024], 1: w1T[0:DC, 128:256], 2: w2a[0:DC, 128:256], 3: L3Wkv[:, 0:1024]}
        AWv = {0: L0Wkv[:, 1024:2048], 1: w1T[0:DC, 256:384], 2: w2a[0:DC, 256:384],
               3: L3Wkv[:, 1024:2048]}
        AWo = {0: L0Wo, 1: w1T[:, 384:512].rearrange("p (c d) -> p c d", d=D), 3: L3Wo}

        kTall = kT[:, :, :].rearrange("p h s -> p (h s)")

        def keys_of(A, b, h):
            return kT[:, h // 2, :] if A.dh == 64 else kTall[:, bass.ts(b, S)] if A.n == 1 else kT[:, h, :]

        def bank_of(n):
            return bank[6 + n % 2]

        SETUP = [("ctx", j) for j in range(4)] + [("vec", 0), ("l1w", 0)] + [("ln", j) for j in range(4)]
        PREP2_UP = [("n1", j) for j in range(6)] + [("n3", j) for j in range(6)]
        PREP2 = [("n2", e) for e in range(8)]
        PREP3 = [("bfc", 0), ("bpr", 0), ("nv", 0), ("fc", 0), ("pr", 0)]

        def setup_evac(move, kind, k, src):
            if kind == "ctx":
                return move(ctxT[:, k * 512:(k + 1) * 512], src[0:DC, :])
            if kind == "vec":
                return move(vecT[:, :], src[:, 0:V_N])
            if kind == "l1w":
                move(w1T[:, 0:128], src[:, 0:128])
                move(w1T[0:DC, 128:384], src[0:DC, 128:384])
                return move(w1T[:, 384:512], src[:, 384:512])
            return move(xnT[:, k * CH:(k + 1) * CH], src[:, :], vecT[:, V_GAMMA:V_GAMMA + 1],
                        vecT[:, V_BETA:V_BETA + 1])

        def prep_evac(move, kind, k, src):
            if kind == "n2":
                move(L2w2[:, k, 0:2, :], src[:, 0:256].rearrange("p (f d) -> p f d", d=D))
                return move(L2w2[0:96, k, 2, :], src[0:96, 256:384])
            if kind == "bfc":
                return move(BT[:, 0:512], src[0:16, :], 2.0)
            if kind == "bpr":
                return move(BT[:, 512:640], src[0:16, 0:128], 2.0)
            if kind == "nv":
                return move(L3Wo[0:16, 8, :], src[0:16, 0:128])
            if kind == "fc":
                return move(fcT, src[:, :])
            return move(prT, src[:, :].rearrange("p (c d) -> p c d", d=D))

        def att_evac(A, move, kind, k, b, kinds, src):
            if kind == "q" and A.dh == 64:
                Q4 = Qz[:, :, :].rearrange("p (g u) s -> p g u s", u=2)
                v = src[:, :].rearrange("p (g s) -> p g s", s=S)
                move(Q4[0:64, 2 * k:2 * k + 2, 0, :], v[0:64], A.scale)
                return move(Q4[64:128, 2 * k:2 * k + 2, 1, :], v[64:128], A.scale)
            if kind == "q" and A.n == 1:
                return move(xnT[:, k * 512:(k + 1) * 512], src[:, :], A.scale)
            if kind == "q":
                return move(Qz[:, 2 * k:2 * k + 2, :].rearrange("p h s -> p (h s)"), src[:, :], A.scale,
                            bqs[:, 0:1])
            if kind == "k" and A.n != 2:
                return move(kT[:, 2 * k:2 * k + 2, :].rearrange("p h s -> p (h s)"), src[:, :])
            if kind == "k":
                return move(kT[:, 2 * k:2 * k + 2, :].rearrange("p h s -> p (h s)"), src[:, :], None,
                            vecT[:, V_BK:V_BK + 1])
            if kind == "v":
                return move(Vx2[:, 4 * k:4 * k + 4, 0:128], src[:, :].rearrange("p (t e) -> p t e", e=128))
            if kind == "sn":
                return move(sn16[:, :], src[0:16, 0:S], -A.scale)
            if kind == "snt":
                return move(nsn[:, :, :].rearrange("p q h -> p (q h)"), src[:, 0:32])
            if kind == "outT" and A.dh == 64:
                g = k % 4
                return move(OT[:, 2 * g:2 * g + 2, :].rearrange("p c s -> p (c s)"), src[:, :])
            if kind in ("outT", "outN"):
                return move(OT[:, 8 if A.null else 0, :], src[:, 0:S])
            if kind == "turns":
                return move(scrap[:, :], src[:, 0:1])
            assert kind == "ln"
            bl = k if A.n == 2 else b - 1
            return move(xnT[:, bass.ts(bl, S)], src[:, 0:S])

        def ffn_ln_evac(F, move, c):
            gain = vecT[:, V_GNORM:V_GNORM + 1] if F.n == 2 else None
            return move(xnT[:, bass.ts(c, CH)], bank[6][:, :], gain)

        block = ctx.enter_context(nc.Block())

        @block.sync
        def _(sp):
            def load(name, dst, src):
                sp.dma_start(dst, src).then_inc(loads[name], 16)

            def row(v):
                return v.rearrange("(a n) -> a n", a=1)

            def spread(v, n=D):
                return row(v).to_broadcast([P, n])

            load("x", x[:, :, :], a["x"].rearrange("b (h p) c -> p (b h) c", p=P))
            load("ctx", ctok[:, :, :], a["ctx_768"].rearrange("b (h p) c -> p (b h) c", p=P))
            load("vecs", vecs[V_B1:V_B1 + 32, :], a["L1_ffn_b1"].rearrange("e (f p) -> (e f) p", p=P))
            load("vecs", vecs[V_BFC:V_BFC + 4, :], a["L3_ffn_b_fc"].rearrange("(f p) -> f p", p=P))
            for at, name in ((V_GAMMA, "L0_xattn_ln_gamma"), (V_BETA, "L0_xattn_ln_beta"),
                             (V_GNORM, "L3_xattn_g_norm"), (V_BQ, "L2_xattn_bq"), (V_BK, "L2_xattn_bk")):
                load("vecs", vecs[at:at + 1, :], row(a[name]))
            load("vecs", vecs[V_GATE2:V_GATE2 + 8, :], a["L2_ffn_gate_w"])
            load("l1a", w1nat[:, 0:128], a["L1_xattn_Wq"])
            load("l1a", w1nat[:, 128:224], a["L1_xattn_Wk"])
            load("l1a", w1nat[:, 224:320], a["L1_xattn_Wv"])
            load("l1a", w1nat[:, 320:448], a["L1_xattn_Wo"])
            load("l0a", L0Wq, a["L0_xattn_Wq"])
            load("l0a", L0Wkv, a["L0_xattn_Wkv"])
            load("l0a", L0Wo, a["L0_xattn_Wo"].rearrange("(c p) d -> p c d", p=P))
            load("mask", mask0[:, :, :], a["mask_1x1xSxS2_bk0"].rearrange("a b (t p) k -> p (a b t) k", p=P))
            load("mask", mask3[:, :], a["mask_BxS2_bf1"].rearrange("(o b) k -> o (b k)", o=1))
            for dst, name, n in ((bo_bc, "L0_xattn_bo", D), (bv_bc, "L2_xattn_bv", D),
                                 (gout_bc, "L3_xattn_g_out", D), (bproj_bc, "L3_ffn_b_proj", D),
                                 (swb_bc, "L1_ffn_switch_b", 8)):
                load("small", dst[:, :], spread(a[name], n))
            load("small", nk_bc[:, :], a["L3_xattn_null_kv"][0:1, :].to_broadcast([P, 64]))
            for half in range(2):
                load("small", nv_col[64 * half:64 * half + 64, :],
                     a["L3_xattn_null_kv"][1:2, :].rearrange("a p -> p a"))
            load("small", gw0[:, :], a["L0_ffn_gate_w"])
            load("small", gw1[:, :], a["L1_ffn_switch_w"])
            sp.wait_ge(consts_ready, 1)
            load("small", b2pad[0:8, :], a["L1_ffn_b2"])
            load("l0f", L0w1.rearrange("p (e f) -> p e f", e=8), a["L0_ffn_ew1"].rearrange("e p f -> p e f"))
            load("l0f", L0w2.rearrange("p (e f) -> p e f", e=8), a["L0_ffn_ew2"].rearrange("e p f -> p e f"))
            load("l0f", L0w3.rearrange("p e f d -> p (e f) d"),
                 a["L0_ffn_ew3"].rearrange("e (f p) d -> p (e f) d", p=P))
            load("l0f", L0s1, a["L0_ffn_sw1"])
            load("l0f", L0s2, a["L0_ffn_sw2"])
            load("l0f", L0s3, a["L0_ffn_sw3"].rearrange("(f p) d -> p f d", p=P))
            load("l1f", L1w1.rearrange("p (e f) -> p e f", e=8), a["L1_ffn_w1"].rearrange("e p f -> p e f"))
            for e in (0, 4):
                load("l1f", L1w2[:, e:e + 4, :, :].rearrange("p e f d -> p (e f) d"),
                     a["L1_ffn_w2"][e:e + 4].rearrange("e (f p) d -> p (e f) d", p=P))
            load("l2a", w2a[:, 0:128], a["L2_xattn_Wq"])
            load("l2a", w2a[0:DC, 128:256], a["L2_xattn_Wk"])
            load("l2a", w2a[0:DC, 256:384], a["L2_xattn_Wv"])
            sp.wait_ge(engines_done["pe"], 2)
            load("l2f", n1.rearrange("p (t d) -> p t d", d=D),
                 a["L2_ffn_w1"].rearrange("e f d -> (e f) d").rearrange("(t p) d -> p t d", p=P))
            load("l2f", n3.rearrange("p (t d) -> p t d", d=D),
                 a["L2_ffn_w3"].rearrange("e f d -> (e f) d").rearrange("(t p) d -> p t d", p=P))
            load("l2f", n2, a["L2_ffn_w2"].rearrange("e d f -> d e f"))
            sp.wait_ge(prep[2].filled, len(PREP2_UP) + len(PREP2))
            load("l3", L3Wq, a["L3_xattn_Wq"])
            load("l3", L3Wkv, a["L3_xattn_Wkv"])
            load("l3", L3Wo[:, 0:8, :], a["L3_xattn_Wout"].rearrange("(c p) d -> p c d", p=P))
            load("l3", fcn.rearrange("p (c d) -> p c d", d=D), a["L3_ffn_W_fc"].rearrange("(c p) d -> p c d", p=P))
            load("l3", prn, a["L3_ffn_W_proj"])
            load("l3", Afc, a["L3_ffn_A_fc"])
            load("l3", Apr, a["L3_ffn_A_proj"])
            load("l3", Bfc, a["L3_ffn_B_fc"].rearrange("(c p) r -> p c r", p=P))
            load("l3", Bpr, a["L3_ffn_B_proj"])
            for c in range(NCH):
                need(sp, ffn_s[3].stats, c + 1)
                sp.dma_start(out.rearrange("b (h p) c -> p (b h) c", p=P)[:, 4 * c:4 * c + 4, :],
                             x[:, 4 * c:4 * c + 4, :]).then_inc(out_written, 16)
            sp.wait_ge(out_written, 16 * NCH)

        @block.gpsimd
        def _(pool):
            count = [0]

            def link(ins):
                count[0] += 1
                ins.then_inc(pool_chain, 1)
                pool.wait_ge(pool_chain, count[0])

            pool.memset(b2pad[:, :], 0.0).then_inc(consts_ready, 1)
            link(pool.memset(ident[:, :], 0.0))
            link(pool.affine_select(out=ident[:, :], in_=ident[:, :], compare_op=ALU.not_equal, fill=1.0,
                                    base=0, pattern=[[-1, P]], channel_multiplier=1))
            link(pool.tensor_copy(identb[:, :], ident[:, :]))
            pool.memset(neghalf[:, :], -0.5).then_inc(consts_ready, 1)
            pool.memset(onesb[:, :], 1.0)
            pool.memset(mb3[:, :], 0.0)
            pool.memset(wpad[:, :, :], 0.0)
            for e in range(8):
                pool.memset(iota[:, e:e + 1], float(e))
            link(pool.memset(headmask[:, :], 1.0))
            link(pool.affine_select(out=headmask[:, :], in_=headmask[:, :], compare_op=ALU.is_ge, fill=0.0,
                                    base=0, pattern=[[-8, 16]], channel_multiplier=1))
            link(pool.affine_select(out=headmask[:, :], in_=headmask[:, :], compare_op=ALU.is_ge, fill=0.0,
                                    base=7, pattern=[[8, 16]], channel_multiplier=-1))
            pool.memset(Qz[:, :, :], 0.0)
            pool.memset(On[:, :, 1024:1152], 0.0).then_inc(consts_ready, 1)

            def normalise(n, stats_sem, value, yn_sem, scale, offset, chain, at=0):
                need(pool, stats_sem, value)
                plain(pool)
                chain(pool.tensor_scalar(ve[:, 0:n], mv[:, at:at + n, 1], scale, offset, ALU.mult, ALU.add))
                chain(pool.tensor_tensor(rstd[:, 0:n], ve[:, 0:n], neghalf[:, 0:n], ALU.pow))
                plain(pool)
                for t in range(n):
                    last = pool.tensor_scalar(yn[:, at + t, :], xnew[:, at + t, :], mv[:, at + t, 0:1],
                                              rstd[:, t:t + 1], ALU.subtract, ALU.mult)
                last.then_inc(yn_sem.sem, 1)

            pool.wait_ge(setup_stats, 1)
            link(pool.tensor_scalar(ve0, mv0[:, :, 1], 1.0 + EPS, EPS * EPS, ALU.mult, ALU.add))
            pool.tensor_tensor(rstd0, ve0, neghalf[:, :], ALU.pow).then_inc(setup_rstd, 1)
            pool.wait_ge(setup_vmax, 1)
            pool.partition_all_reduce(vmaxall[:, 0:3], vmax[:, 0:3], P, RMAX).then_inc(setup_vmaxall, 1)
            boundary(pool, "pool", 1)

            split_count = [0]

            def split_link(ins):
                split_count[0] += 1
                ins.then_inc(split_chain, 1)
                pool.wait_ge(split_chain, split_count[0])

            def largest(n):
                pool.wait_ge(up_rows, n + 1)
                pool.partition_all_reduce(uprowall[:, n:n + 1], uprow[:, n:n + 1], P, RMAX).then_inc(up_max, 1)

            def split_inputs(c):
                v = slice(c * CH, (c + 1) * CH)
                split_link(pool.tensor_copy(xH[:, v], xnT[:, v]))
                pool.tensor_tensor(xL[:, v], xnT[:, v], xH[:, v], ALU.subtract).then_inc(x_split, 1)

            def first_context(A):
                pool.tensor_copy(ctxb[:, :], ctxT[:, 0:S]).then_inc(att_s[A.n].ctxb.sem, 1)

            def early(A):
                if A.n == 0:
                    first_context(A)
                if A.n == 3:
                    pool.wait_ge(vmax3_rows, 1)
                    pool.partition_all_reduce(vmaxall[:, 3:4], vmax[:, 3:4], P, RMAX).then_inc(vmax3_max, 1)
                    need(pool, ffn_s[2].stats, NCH)
                    pool.memset(Qz[:, :, :], 0.0)
                    pool.wait_ge(prep3_rows, 1)
                    pool.partition_all_reduce(amx, am, P, RMAX).then_inc(prep3_max, 1)

            def attention(A):
                s = att_s[A.n]
                links = {0: 2, 1: 2, 2: 2, 3: 5}[A.n]
                start = count[0]

                def masks(b, bw, heads=range(0, 16, 4)):
                    for h in heads:
                        if b is not None:
                            need(pool, s.scores, b * 16 + (h + 4))
                        plain(pool)
                        pool.tensor_tensor(
                            Qz[:, h:h + 4, :], xnT[:, bass.ts(bw, S)].unsqueeze(1).to_broadcast([P, 4, S]),
                            headmask[:, h:h + 4].unsqueeze(2).to_broadcast([P, 4, S]), ALU.mult).then_inc(s.qm.sem, 1)

                def body(b, kinds):
                    if A.n == 2:
                        for h in range(A.nh):
                            need(pool, s.stats, h + 1)
                            need(pool, s.ring.filled, 12 + h - 1)
                            normalise(2, s.stats, h + 1, s.yn, 1.0, EPS, link, 2 * (h % 2))
                            if h == 5:
                                split_inputs(0)
                        return
                    if A.n == 1 and kinds == "prologue":
                        need(pool, s.ring.act, 5)
                        masks(None, 0)
                        return
                    if kinds == "prologue":
                        return
                    if A.n != 1 and kinds in ("first", "mid"):
                        m = [m for kind, k, m, _ in steps(A, b, kinds) if (kind, k) == ("v", 3)][0]
                        need(pool, s.ring.filled, b * BATCH_FILLS[A.n] + (m + 1))
                        pool.tensor_copy(ctxb[:, :], ctxT[:, bass.ts(b + 1, S)]).then_inc(s.ctxb.sem, 1)
                    if A.n == 1 and kinds == "first":
                        need(pool, s.ring.act, 6)
                        need(pool, s.ring.dve, 6)
                        masks(0, 1)
                    if A.n == 1 and kinds == "mid":
                        masks(b, b + 1, (0, 4))
                    if A.n < 2 and kinds == "first":
                        largest(A.n)
                    if A.n < 2 and kinds == "last":
                        m = [m for kind, k, m, _ in steps(A, b, kinds) if kind in FILLS][0]
                        need(pool, s.ring.filled, b * BATCH_FILLS[A.n] + (m + 1))
                        split_inputs(0)
                    if kinds != "first":
                        if A.null:
                            own_norm(b - 1, kinds)
                        tail(b - 1, kinds)
                    if A.n == 1 and kinds == "mid":
                        masks(b, b + 1, (8, 12))

                def chain_at(b, kinds, off):
                    n = [0]

                    def chain(ins):
                        n[0] += 1
                        ins.then_inc(pool_chain, 1)
                        pool.wait_ge(pool_chain, b * links + (start + off + n[0]))
                    return chain

                def own_norm(b, kinds):
                    chain = chain_at(b, kinds, 0)
                    need(pool, s.ostats, b + 1)
                    plain(pool)
                    chain(pool.tensor_scalar(ve[:, 2:4], mvo[:, :, 1], 1.0, EPS, ALU.mult, ALU.add))
                    chain(pool.tensor_tensor(rstd[:, 2:4], ve[:, 2:4], neghalf[:, 0:2], ALU.pow))
                    plain(pool)
                    pool.tensor_scalar(on1[:, 0, :], osb[:, 0, :], mvo[:, 0, 0:1], rstd[:, 2:3],
                                       ALU.subtract, ALU.mult)
                    chain(pool.tensor_scalar(on1[:, 1, :], osb[:, 1, :], mvo[:, 1, 0:1], rstd[:, 3:4],
                                             ALU.subtract, ALU.mult))
                    pool.tensor_tensor(osb[:, 0, :], on1[:, 0, :], gout_bc[:, :], ALU.mult)
                    pool.tensor_tensor(osb[:, 1, :], on1[:, 1, :], gout_bc[:, :],
                                       ALU.mult).then_inc(s.onorm.sem, 1)

                def tail(b, kinds):
                    chain = chain_at(b, kinds, links - 2 if A.null else 0)
                    need(pool, s.stats, b + 1)
                    normalise(2, s.stats, b + 1, s.yn, 1.0, EPS, chain)

                batches(pool, A, body)
                if A.n == 2:
                    return
                count[0] = start + B * links

            def feed_forward(F):
                s = ffn_s[F.n]
                start = count[0]

                def body(c, first):
                    n = [0]

                    def chain(ins):
                        n[0] += 1
                        ins.then_inc(pool_chain, 1)
                        pool.wait_ge(pool_chain, c * 2 + (start + n[0]))
                    need(pool, s.stats, c + 1)
                    twice = F.n == 2
                    normalise(4, s.stats, c + 1, s.yn, 1.0 + EPS if twice else 1.0,
                              EPS * EPS if twice else EPS, chain)
                if F.n == 1:
                    pool.memset(Vx2[:, :, 128], 1.0).then_inc(zeroed, 1)
                if F.n == 1:
                    largest(2)
                if F.n < 3:
                    A = ATT[F.n]
                    need(pool, att_s[F.n].ring.act, (all_fills(A) + 1) // 2)
                    need(pool, att_s[F.n].ring.dve, all_fills(A) // 2)
                    for c in range(1, NCH):
                        if c == NCH - 1:
                            need(pool, s.lne, 1)
                        split_inputs(c)
                if F.n == 2:
                    first_context(ATT[3])
                    pool.memset(NVflat, 0.0)
                    pool.memset(L3Wo[:, 8, :], 0.0)
                    pool.memset(On[:, :, 1024:1152], 0.0).then_inc(prep3_zero, 1)
                if F.n < 3:
                    chunks(pool, F, body)
                    count[0] = start + 2 * NCH

            early(ATT[0])
            for n in range(4):
                attention(ATT[n])
                feed_forward(FFN[n])
                if n < 3:
                    early(ATT[n + 1])
                    boundary(pool, "pool", n + 2)

        @block.scalar
        def _(act):
            def move(dst, src, gain=None, bias=None):
                if bias is not None:
                    return act.activation(dst, src, ACT.Identity, bias=bias, scale=1.0 if gain is None else gain)
                if gain is None or isinstance(gain, float):
                    return act.activation(dst, src, ACT.Copy, scale=1.0 if gain is None else gain)
                return act.activation(dst, src, ACT.Identity, scale=gain)

            for n, (kind, k) in enumerate(SETUP):
                if n % 2 == 0:
                    act.wait_ge(setup.filled, n + 1)
                    setup_evac(move, kind, k, bank_of(n)).then_inc(setup.act, 1)
            boundary(act, "act", 1)

            def early(A):
                attention(A, ("early",))
                if A.n in prep:
                    r = prep[A.n]
                    before = 0
                    if A.n == 2:
                        before = len(PREP2_UP)
                        act.wait_ge(up_scale, 3)
                        for n, (kind, k) in enumerate(PREP2_UP):
                            act.wait_ge(r.filled, n + 1)
                            w = 512 if k < 5 else 256
                            move(l2_parts(kind, k * 512, w)[0], bank_of(n)[:, 0:w],
                                 upscale[:, 2:3]).then_inc(prep2_high, 1)
                    for n, (kind, k) in enumerate(PREP2 if A.n == 2 else PREP3):
                        if n % 2 == 0:
                            act.wait_ge(r.filled, before + n + 1)
                            prep_evac(move, kind, k, bank_of(n)).then_inc(r.act, 1)

            def attention(A, early=None):
                s = att_s[A.n]

                def body(b, kinds):
                    nh = A.nh
                    for kind, k, m, base in steps(A, b, kinds):
                        if kinds == "early" and A.n != 2 and (kind, k) == ("v", 0):
                            act.wait_ge(ones_set, (1, 2, 0, 3)[A.n])
                        if kind == "softmax":
                            need(act, s.negmax, b * nh + (k + 1))
                            need(act, s.turn, b * nh + (k - 3))
                            if A.null:
                                act.activation(pn[:, :, k], dn[:, k % 4, :], ACT.Exp)
                            for qt in range(2):
                                last = act.activation(Pm[:, k % 4, qt * S:(qt + 1) * S],
                                                      bank[k % 2][:, qt * S:(qt + 1) * S], ACT.Exp,
                                                      bias=negm[:, k % 4, qt:qt + 1])
                            last.then_inc(s.exp.sem, 1)
                            if A.n < 2 and kinds == "last" and 0 <= k - 4 < UP[A.n][2]:
                                t, lo, _ = UP[A.n]
                                i = k - 4
                                if i == 0:
                                    act.wait_ge(up_scale, A.n + 1)
                                else:
                                    act.wait_ge(up_low, blocks_before(A.n) + i)
                                move(block_parts(A.n, i)[0], cols(t, lo + 512 * (i + 1), 512),
                                     upscale[:, A.n:A.n + 1]).then_inc(up_high, 1)
                        elif kind == "turn" and (A.n != 2 or k % 2 == 0):
                            need(act, s.turn, b * nh + (k + 1))
                            need(act, s.av, b * nh + (k - 3))
                            move((PTs if A.n == 2 else PTh)[:, k % 4, :],
                                 bank[2 + k % 2][:, :]).then_inc(s.pt[0].sem, 1)
                        elif kind == "v" and A.n != 2 and m % 2:
                            need(act, s.ring.filled, b * BATCH_FILLS[A.n] + (m + 1))
                            v_high(A, move, k, bank_of(m)).then_inc(s.vhigh.sem, 1)
                        elif kind == "v" and A.n != 2:
                            need(act, s.vlow, b * v_count(A, 0) + v_done(A, b, kinds, m, 0))
                            act.sem_inc(s.ring.act.sem, 1)
                        elif kind in FILLS and m % 2 == 0:
                            need(act, s.ring.filled, b * BATCH_FILLS.get(A.n, 0) + (m + 1))
                            att_evac(A, move, kind, k, b, kinds, bank_of(m)).then_inc(s.ring.act.sem, 1)
                if early:
                    body(0, "early")
                else:
                    batches(act, A, body)

            def feed_forward(F):
                s = ffn_s[F.n]

                def body(c, first):
                    for kind, k in ffn_schedule(F, first):
                        if kind == "gate" and k == 0:
                            need(act, s.gt, c + 1)
                            need(act, s.gl, c)
                            move(gTs[:, :], bank[6][0:8, :]).then_inc(s.gte.sem, 1)
                        elif kind == "gate" and k == 2:
                            need(act, s.gd, c + 1)
                            if F.k == 1:
                                act.activation(ge[:, :, :], gd[:, :, :], ACT.Exp).then_inc(s.gx.sem, 1)
                            else:
                                act.activation(ge[:, :, 0], gd[:, :, 0], ACT.Exp).then_inc(s.gx.sem, 1)
                        elif kind == "up":
                            e, ft = k
                            u = e * F.FT + ft
                            M = F.last if ft == F.FT - 1 else P
                            need(act, s.h, c * F.U + (u + 1))
                            if F.gated:
                                need(act, s.g, c * F.U + (u - 1))
                                act.activation(sg[0:M, u % 2, :], bank[u % 2][0:M, :], ACT.Silu,
                                               scale=upback[0:M, F.n:F.n + 1]).then_inc(s.silu.sem, 1)
                            else:
                                need(act, s.y, c * F.E + (e - 1 if e >= 2 else 0))
                                bias = (vecT[:, V_B1 + u:V_B1 + u + 1] if F.n == 1
                                        else vecT[:, V_BFC + u:V_BFC + u + 1])
                                act.activation(G[:, u % (2 * F.FT), :], bank[u % 4][:, :],
                                               ACT.Gelu_apprx_tanh if F.n == 1 else ACT.Gelu,
                                               bias=bias, scale=upback[:, 1:2] if F.n == 1 else 1.0
                                               ).then_inc(s.g.sem, 1)
                        elif kind == "ln":
                            need(act, s.lnf, c + 1)
                            ffn_ln_evac(F, move, c - 1).then_inc(s.lne.sem, 1)
                        elif kind == "attln":
                            need(act, s.lnf, 1)
                            move(xnT[:, (B - 1) * S:B * S], bank[6][:, 0:S]).then_inc(s.lne.sem, 1)
                chunks(act, F, body)

            def ffn_end(F):
                s = ffn_s[F.n]
                need(act, s.lnf, NCH + 1)
                ffn_ln_evac(F, move, NCH - 1).then_inc(s.lne.sem, 1)

            early(ATT[0])
            for n in range(4):
                attention(ATT[n])
                feed_forward(FFN[n])
                if n < 3:
                    early(ATT[n + 1])
                    ffn_end(FFN[n])
                    boundary(act, "act", n + 2)

        @block.tensor
        def _(pe):
            def mm(o, l, r, start=True, stop=True):
                return pe.matmul(o, l, r, start=start, stop=stop)

            def turn(o, i):
                n = i.shape[0]
                return pe.transpose(o, i, ident[0:n, 0:n])

            pe.wait_ge(consts_ready, 2)
            for n, (kind, k) in enumerate(SETUP):
                ps = bank_of(n)
                if n >= 2:
                    pe.wait_ge(setup.dve if n % 2 else setup.act, n // 2)
                if kind == "ctx":
                    if k == 0:
                        loaded(pe, "ctx")
                    for t in range(4):
                        last = turn(ps[0:DC, t * P:(t + 1) * P], ctok[:, 4 * k + t, :])
                elif kind == "vec":
                    loaded(pe, "vecs")
                    last = turn(ps[:, 0:V_N], vecs[:, :])
                elif kind == "l1w":
                    loaded(pe, "l1a")
                    turn(ps[:, 0:128], w1nat[:, 0:128])
                    turn(ps[0:DC, 128:256], w1nat[:, 128:224])
                    turn(ps[0:DC, 256:384], w1nat[:, 224:320])
                    last = turn(ps[:, 384:512], w1nat[:, 320:448])
                else:
                    pe.wait_ge(setup_normed, k + 1)
                    for t in range(4):
                        last = turn(ps[:, t * P:(t + 1) * P], normed0[k % 2][:, t, :])
                last.then_inc(setup.filled, 1)
            boundary(pe, "pe", 1)

            def prep_fill(kind, k, ps):
                if kind in ("n1", "n3"):
                    src = n1 if kind == "n1" else n3
                    for t in range(4 if k < 5 else 2):
                        last = turn(ps[:, t * P:(t + 1) * P], src[:, (4 * k + t) * P:(4 * k + t + 1) * P])
                elif kind == "n2":
                    for f in range(3):
                        w = 128 if f < 2 else 96
                        last = turn(ps[0:w, f * P:f * P + P], n2[:, k, f * P:f * P + w])
                elif kind == "bfc":
                    for t in range(4):
                        last = turn(ps[0:16, t * P:(t + 1) * P], Bfc[:, t, :])
                elif kind == "bpr":
                    last = turn(ps[0:16, 0:P], Bpr)
                elif kind == "nv":
                    pe.wait_ge(prep3_done, 1)
                    for c in range(8):
                        last = mm(ps[0:16, 0:P], NVsel[:, c, :], L3Wo[:, c, :], c == 0, c == 7)
                elif kind == "fc":
                    pe.wait_ge(prep[3].act, 1)
                    pe.wait_ge(prep3_done, 2)
                    for t in range(4):
                        o = ps[:, t * P:(t + 1) * P]
                        mm(o, fcn[:, t * P:(t + 1) * P], ident[:, :], True, False)
                        last = mm(o, Afc, BT[:, t * P:(t + 1) * P], False, True)
                else:
                    pe.wait_ge(prep[3].dve, 1)
                    pe.wait_ge(prep3_done, 3)
                    for t in range(4):
                        o = ps[:, t * P:(t + 1) * P]
                        mm(o, prn[:, t * P:(t + 1) * P], ident[:, :], True, False)
                        last = mm(o, Apr[:, t * P:(t + 1) * P], BT[:, 512:640], False, True)
                return last

            def early(A):
                if A.n in (0, 2, 3):
                    loaded(pe, {0: "l0a", 2: "l2a", 3: "l3"}[A.n])
                attention(A, ("early",))
                if A.n in prep:
                    r = prep[A.n]
                    need(pe, att_s[A.n].ring.act, (len(att_early(A)) + 1) // 2)
                    need(pe, att_s[A.n].ring.dve, len(att_early(A)) // 2)
                    if A.n == 2:
                        loaded(pe, "l2f")
                    if A.n == 2:
                        for n, (kind, k) in enumerate(PREP2_UP):
                            if n >= 2:
                                pe.wait_ge(prep2_low, n - 1)
                            prep_fill(kind, k, bank_of(n)).then_inc(r.filled, 1)
                        pe.wait_ge(prep2_low, len(PREP2_UP))
                    for n, (kind, k) in enumerate(PREP2 if A.n == 2 else PREP3):
                        if n >= 2:
                            pe.wait_ge(r.dve if n % 2 else r.act, n // 2)
                        prep_fill(kind, k, bank_of(n)).then_inc(r.filled, 1)
                    n = len(PREP2 if A.n == 2 else PREP3)
                    pe.wait_ge(r.act, (n + 1) // 2)
                    pe.wait_ge(r.dve, n // 2)

            def attention(A, early=None):
                s = att_s[A.n]
                Wq, Wk, Wv = AWq[A.n], AWk[A.n], AWv[A.n]
                if not early:
                    if A.n == 2:
                        pe.wait_ge(zeroed, 1)
                    else:
                        pe.wait_ge(ones_set, (1, 2, 0, 3)[A.n])
                    if A.n in (0, 3):
                        pe.wait_ge(consts_ready_dve, 1)
                elif A.n:
                    f = ffn_s[A.n - 1]
                    need(pe, f.lne, NCH)
                    need(pe, f.gle, NCH)
                    if FFN[A.n - 1].k == 1:
                        need(pe, f.wte, NCH)
                per = BATCH_FILLS.get(A.n, 0)

                def fills_read(b, m):
                    need(pe, s.ring.act, b * (per // 2) + (m + 1) // 2)
                    need(pe, s.ring.dve, b * (per // 2) + m // 2)

                def fill(kind, k, b, kinds, m, ps):
                    bw = 0 if kinds in ("early", "prologue", "single") else b if (kind, k) in OWN else b + 1
                    need(pe, s.ring.dve if m % 2 else s.ring.act, b * (per // 2) + m // 2)
                    if kind == "q" and A.dh == 64:
                        for g in range(2):
                            hp = 2 * k + g
                            last = mm(ps[:, g * S:(g + 1) * S], Wq[:, hp * P:(hp + 1) * P], xnT[:, bass.ts(bw, S)])
                    elif kind == "q":
                        last = mm(ps[:, :], Wq, xnT[:, k * 512:(k + 1) * 512])
                    elif kind == "k" and A.dh == 64:
                        for g in range(2):
                            hp = 2 * k + g
                            last = mm(ps[:, g * S:(g + 1) * S], Wk[:, hp * P:(hp + 1) * P], ctxT[:, bass.ts(bw, S)])
                    elif kind == "k":
                        last = mm(ps[:, :], Wk, ctxT[:, k * 512:(k + 1) * 512])
                    elif kind == "v" and A.dh == 64:
                        need(pe, s.ctxb, bw + 1)
                        last = mm(ps[:, :], ctxb[:, (k // 2) * P:(k // 2 + 1) * P],
                                  Wv[:, (k % 2) * 512:(k % 2 + 1) * 512])
                    elif kind == "v":
                        for t in range(4):
                            last = mm(ps[:, t * P:(t + 1) * P], ctxT[:, (4 * k + t) * P:(4 * k + t + 1) * P], Wv)
                    elif kind == "sn":
                        plain(pe)
                        last = mm(ps[0:16, 0:S], Wn, xnT[:, bass.ts(bw, S)])
                    elif kind == "snt":
                        ms = [m_ for kind_, _, m_, _ in steps(A, b, kinds) if kind_ == "sn"][0]
                        need(pe, s.ring.dve if ms % 2 else s.ring.act, b * (per // 2) + ms // 2 + 1)
                        plain(pe)
                        for qt in range(2):
                            last = turn(ps[:, qt * 16:(qt + 1) * 16], sn16[:, qt * P:(qt + 1) * P])
                    elif kind == "outT" and A.dh == 64:
                        need(pe, s.norm, b * 8 + (2 * k + 2))
                        for c in range(2):
                            for qt in range(2):
                                at = (2 * (k % 4) + c) * P
                                last = turn(ps[:, c * S + qt * P:c * S + (qt + 1) * P], On[:, qt, at:at + P])
                    elif kind in ("outT", "outN"):
                        need(pe, s.norm, b * 8)
                        c = 8 if A.null else 0
                        for qt in range(2):
                            last = turn(ps[:, qt * P:(qt + 1) * P], On[:, qt, c * P:(c + 1) * P])
                    elif kind == "wo":
                        fills_read(b, m)
                        for qt in range(2):
                            for c in range(A.pieces):
                                last = mm(ps[:, qt * P:(qt + 1) * P], OT[:, c, qt * P:(qt + 1) * P],
                                          AWo[A.n][:, c, :], c == 0, c == A.pieces - 1)
                    elif kind == "turns":
                        last = turn(ps[:, 0:P], ident[:, :])
                    else:
                        bl = k if A.n == 2 else b - 1
                        need(pe, s.yn, bl + 1)
                        at = 2 * (k % 2) if A.n == 2 else 0
                        for t in range(2):
                            last = turn(ps[:, t * P:(t + 1) * P], yn[:, at + t, :])
                    last.then_inc(s.ring.filled.sem, 1)

                def body(b, kinds):
                    nh = A.nh
                    for kind, k, m, base in steps(A, b, kinds):
                        if kind == "scores":
                            if k == 0 and kinds in ("single", "first"):
                                fills_read(b, m)
                            if A.n == 1 and k % 4 == 0:
                                need(pe, s.qm, b * 4 + (k // 4 + 1))
                            need(pe, s.exp, b * nh + (k - 1))
                            for qt in range(2):
                                o = bank[k % 2][:, qt * S:(qt + 1) * S]
                                if A.mask == "full":
                                    mm(o, identb[:, :], mb0[:, qt, :], True, False)
                                elif A.mask == "key":
                                    mm(o, onesb[:, :], mb3[:, bass.ts(b, S)], True, False)
                                last = mm(o, Qz[:, k, qt * P:(qt + 1) * P], keys_of(A, b, k), A.mask is None, True)
                            last.then_inc(s.scores.sem, 1)
                        elif kind == "turn":
                            need(pe, s.exp, b * nh + (k + 1))
                            if A.n == 2:
                                need(pe, s.pt[k % 2], k // 2)
                            else:
                                need(pe, s.pt[1], b * nh + (k - 1))
                            for kt in range(2):
                                for qt in range(2):
                                    last = turn(bank[2 + k % 2][:, kt * S + qt * P:kt * S + (qt + 1) * P],
                                                Pm[:, k % 4, qt * S + kt * P:qt * S + (kt + 1) * P])
                            last.then_inc(s.turn.sem, 1)
                        elif kind == "av":
                            if A.n == 2:
                                need(pe, s.pt[k % 2], k // 2 + 1)
                                need(pe, s.norm, k - 1)
                                for qt in range(2):
                                    for kt in range(2):
                                        last = mm(bank[4 + k % 2][:, qt * S:qt * S + 129],
                                                  PTs[:, k % 4, kt * S + qt * P:kt * S + (qt + 1) * P],
                                                  Vx2[:, 2 * k + kt, :], kt == 0, kt == 1)
                            else:
                                need(pe, s.pt[1], b * nh + (k + 1))
                                p = k // 2
                                if k % 2 == 0:
                                    need(pe, s.norm, b * 8 + (p - 1))
                                for qt in range(2):
                                    r = (k % 2) * 2 + qt
                                    for kt in range(2):
                                        for n, (pp, vv) in enumerate(((PTh, VxH), (PTh, VxL), (PTl, VxH))):
                                            last = mm(bank[4 + p % 2][:, r * P:r * P + A.dh + 1],
                                                      pp[:, k % 4, kt * S + qt * P:kt * S + (qt + 1) * P],
                                                      Vhead(A, b if k >= 0 else b - 1, kt, k % 16, vv), kt == 0 and n == 0,
                                                      kt == 1 and n == 2)
                            last.then_inc(s.av.sem, 1)
                        elif kind in FILLS:
                            fill(kind, k, b, kinds, m, bank_of(m))
                if early:
                    body(0, "early")
                    return
                batches(pe, A, body)
                fills_read(0, all_fills(A))
                if A.n == 2:
                    need(pe, s.norm, A.nh)

            def turn_rows(F, c):
                s = ffn_s[F.n]
                need(pe, s.yn, c + 1)
                for t in range(4):
                    last = turn(bank[6][:, t * P:(t + 1) * P], yn[:, t, :])
                last.then_inc(s.lnf.sem, 1)

            def ffn_end(F):
                A = ATT[F.n + 1]
                if A.n not in prep:
                    need(pe, att_s[A.n].ring.act, (len(att_early(A)) + 1) // 2)
                    need(pe, att_s[A.n].ring.dve, len(att_early(A)) // 2)
                turn_rows(F, NCH - 1)

            def feed_forward(F):
                s = ffn_s[F.n]
                if F.n in (0, 1):
                    loaded(pe, f"l{F.n}f")
                    pe.wait_ge(up_low, blocks_before(F.n) + UP[F.n][2])
                gw = {0: gw0[:, :], 1: gw1[:, :], 2: vecT[:, V_GATE2:V_GATE2 + 8], 3: None}[F.n]

                def w_up(e, ft):
                    if F.n == 0:
                        if e == 8:
                            return block_parts(0, 8, ft * P, P), block_parts(0, 8, 256 + ft * P, P)
                        at = (e % 2) * 256 + ft * P
                        return block_parts(0, e // 2, at, P), block_parts(0, 4 + e // 2, at, P)
                    if F.n == 1:
                        return (block_parts(1, e, ft * P, P),)
                    if F.n == 2:
                        m = 96 if ft == 2 else P
                        return l2_parts("n1", e * 352 + ft * P, m), l2_parts("n3", e * 352 + ft * P, m)
                    return (fcT[:, ft * P:(ft + 1) * P],)

                def up(o, w, c):
                    if F.n == 3:
                        return mm(o, w, xnT[:, bass.ts(c, CH)])
                    mm(o, w[0], xH[:, bass.ts(c, CH)], True, False)
                    mm(o, w[0], xL[:, bass.ts(c, CH)], False, False)
                    return mm(o, w[1], xH[:, bass.ts(c, CH)], False, True)

                def w_down(e, ft):
                    if F.n == 0:
                        return L0s3[:, ft, :] if e == 8 else L0w3[:, e, ft, :]
                    if F.n == 1:
                        return L1w2[:, e, ft, :]
                    if F.n == 2:
                        return L2w2[0:96 if ft == 2 else P, e, ft, :]
                    return prT[:, ft, :]

                def body(c, first):
                    if F.n == 3 and not first:
                        need(pe, s.lne, 1)
                    xc = xnT[:, bass.ts(c, CH)]
                    for kind, k in ffn_schedule(F, first):
                        if kind == "gate" and k == 0:
                            need(pe, s.lne, 0 if first else c)
                            plain(pe)
                            mm(bank[6][0:8, :], gw, xc).then_inc(s.gt.sem, 1)
                        elif kind == "gate" and k == 1:
                            need(pe, s.gte, c + 1)
                            need(pe, s.gle, c)
                            if F.n == 1:
                                need(pe, s.wte, c)
                            plain(pe)
                            for t in range(4):
                                last = turn(bank[7][:, t * 8:(t + 1) * 8], gTs[:, t * P:(t + 1) * P])
                            last.then_inc(s.gl.sem, 1)
                        elif kind == "gate" and k == 3:
                            need(pe, s.w, c + 1)
                            need(pe, s.gle, c + 1)
                            for t in range(4):
                                last = turn(bank[7][:, t * P:(t + 1) * P], wpad[:, t, :])
                            last.then_inc(s.wt.sem, 1)
                        elif kind == "up":
                            e, ft = k
                            u = e * F.FT + ft
                            ws = w_up(e, ft)
                            M = F.last if ft == F.FT - 1 else P
                            if u == 0 and F.n < 3:
                                need(pe, x_split, c + (F.n * NCH + 1))
                            need(pe, s.g, c * F.U + (u - 1 if F.gated else u - 3))
                            if F.gated:
                                up(bank[u % 2][0:M, :], ws[0], c)
                                last = up(bank[2 + u % 2][0:M, :], ws[1], c)
                            else:
                                last = up(bank[u % 4][:, :], ws[0], c)
                            last.then_inc(s.h.sem, 1)
                        elif kind == "down":
                            e = k
                            need(pe, s.acc, c * F.E + (e - 1 if e >= 2 else 0))
                            if F.n == 1 and e == 8:
                                need(pe, s.wte, c + 1)
                                for t in range(4):
                                    last = mm(bank[4 + e % 2][:, t * P:(t + 1) * P], wTs[:, t * P:(t + 1) * P],
                                              b2pad[:, :])
                            else:
                                need(pe, s.g, c * F.U + (e + 1) * F.FT)
                                for t in range(4):
                                    for ft in range(F.FT):
                                        K = F.last if ft == F.FT - 1 else P
                                        slot = (e * F.FT + ft) % (2 * F.FT)
                                        last = mm(bank[4 + e % 2][:, t * P:(t + 1) * P],
                                                  G[0:K, slot, t * P:(t + 1) * P], w_down(e, ft),
                                                  ft == 0, ft == F.FT - 1)
                            last.then_inc(s.y.sem, 1)
                        elif kind == "ln":
                            need(pe, s.gte, c + 1)
                            turn_rows(F, c - 1)
                        elif kind == "attln":
                            need(pe, att_s[F.n].yn, B)
                            if F.k:
                                need(pe, s.gte, 1)
                            at = 2 * ((B - 1) % 2) if F.n == 2 else 0
                            for t in range(2):
                                last = turn(bank[6][:, t * P:(t + 1) * P], yn[:, at + t, :])
                            last.then_inc(s.lnf.sem, 1)
                chunks(pe, F, body)

            early(ATT[0])
            for n in range(4):
                attention(ATT[n])
                feed_forward(FFN[n])
                if n < 3:
                    early(ATT[n + 1])
                    ffn_end(FFN[n])
                    boundary(pe, "pe", n + 2)

        @block.vector
        def _(dve):
            count = [0]

            def link(ins):
                count[0] += 1
                ins.then_inc(dve_chain, 1)
                dve.wait_ge(dve_chain, count[0])

            def move(dst, src, gain=None, bias=None):
                if gain is None and bias is None:
                    return dve.tensor_copy(dst, src)
                if bias is None:
                    return dve.tensor_scalar(dst, src, gain, None, ALU.mult)
                if gain is None:
                    return dve.tensor_scalar(dst, src, bias, None, ALU.add)
                return dve.tensor_scalar(dst, src, gain, bias, ALU.mult, ALU.add)

            def stats(src, n, chain, done, to=None, at=0):
                for t in range(at, at + n):
                    last = dve.bn_stats(st6[:, t, :], src[:, t, :])
                chain(last)
                plain(dve)
                to = mv if to is None else to
                for t in range(at, at + n):
                    last = dve.bn_aggr(to[:, t, :], st6[:, t, :])
                last.then_inc(done, 1)

            def value_scale(lo, hi):
                link(dve.tensor_scalar(vscale[:, lo:hi], vmaxall[:, lo:hi] if lo == 3 else vmaxall[:, 1:3],
                                       vmaxall[:, 0:1], DC / 2.0 ** 14, ALU.mult, ALU.mult))
                link(dve.tensor_scalar(vscale[:, lo:hi], vscale[:, lo:hi], 2.0 ** -14, None, ALU.max))
                link(dve.reciprocal(vscale[:, lo:hi], vscale[:, lo:hi]))

            loaded(dve, "x")
            for t in range(NT):
                last = dve.bn_stats(st0[:, t, :], x[:, t, :])
            link(last)
            for t in range(NT):
                last = dve.bn_aggr(mv0[:, t, :], st0[:, t, :])
            last.then_inc(setup_stats, 1)

            def normalise0(k):
                need(dve, setup.filled, 0 if k < 2 else 5 + k)
                for t in range(4):
                    i = 4 * k + t
                    last = dve.tensor_scalar(normed0[k % 2][:, t, :], x[:, i, :], mv0[:, i, 0:1],
                                             rstd0[:, i:i + 1], ALU.subtract, ALU.mult)
                last.then_inc(setup_normed, 1)

            def masks_and_maxima():
                link(dve.memset(vmax[:, :], 0.0))
                loaded(dve, "ctx")
                loaded(dve, "l0a")
                dve.tensor_reduce(vmax[:, 0:1], ctok.rearrange("p t c -> p (t c)"), AX.X, ALU.max,
                                  apply_absolute_value=True)
                dve.tensor_reduce(vmax[0:DC, 1:2], L0Wkv[:, 1024:2048], AX.X, ALU.max, apply_absolute_value=True)
                dve.tensor_reduce(vmax[:, 2:3], w1nat[:, 224:320], AX.X, ALU.max,
                                  apply_absolute_value=True).then_inc(setup_vmax, 1)
                loaded(dve, "mask")
                dve.wait_ge(consts_ready, 3)
                dve.tensor_scalar(mb0[:, :, :], mask0[:, :, :], -1.0, -MASKED, ALU.add, ALU.mult)
                dve.tensor_reduce(seen[:, :], mask0[:, :, :], AX.X, ALU.max)
                link(dve.tensor_scalar(mb3[0:1, :], mask3[:, :], -1.0, -MASKED, ALU.add, ALU.mult))
                link(dve.tensor_scalar(pen[:, :], seen[:, :], -1.0, -MASKED, ALU.add, ALU.mult))
                link(dve.tensor_scalar(pen[:, :], pen[:, :], 10.0, None, ALU.mult))
                link(dve.tensor_tensor(pen[:, :], pen[:, :], pen[:, :], ALU.subtract))
                loaded(dve, "small")
                for qt in range(2):
                    dve.tensor_scalar(bopen[:, qt, :], bo_bc[:, :], pen[:, qt:qt + 1], None, ALU.add)

            dve.wait_ge(setup_rstd, 1)
            normalise0(0)
            normalise0(1)
            for n, (kind, k) in enumerate(SETUP):
                if kind == "vec":
                    loaded(dve, "l1a")
                    masks_and_maxima()
                if kind == "ln" and k in (1, 2):
                    normalise0(k + 1)
                if n % 2:
                    dve.wait_ge(setup.filled, n + 1)
                    setup_evac(move, kind, k, bank_of(n)).then_inc(setup.dve, 1)
            dve.wait_ge(setup.act, 3)
            dve.tensor_scalar(bqs[:, :], vecT[:, V_BQ:V_BQ + 1], ATT[2].scale, None,
                              ALU.mult).then_inc(consts_ready_dve, 1)
            dve.wait_ge(setup_vmaxall, 1)
            value_scale(0, 2)
            boundary(dve, "dve", 1)

            def prep3_operands():
                dve.wait_ge(prep3_zero, 1)
                dve.tensor_reduce(am[:, 0:1], fcn, AX.X, ALU.max, apply_absolute_value=True)
                dve.tensor_reduce(am[:, 1:2], prn, AX.X, ALU.max,
                                  apply_absolute_value=True).then_inc(prep3_rows, 1)
                dve.tensor_copy(NVflat[0:64, 0:128:18], nv_col[0:64, 0:1].to_broadcast([64, 8]))
                dve.tensor_copy(NVflat[64:128, 1:128:18],
                                nv_col[64:128, 0:1].to_broadcast([64, 8])).then_inc(prep3_done, 1)
                q3 = qtmp.rearrange("p (h e) -> p h e", e=64)
                link(dve.tensor_tensor(q3, L3Wq.rearrange("p (h e) -> p h e", e=64),
                                       nk_bc[:, :].unsqueeze(1).to_broadcast([P, 16, 64]), ALU.mult))
                link(dve.tensor_reduce(Wn, q3, AX.X, ALU.add))
                dve.wait_ge(prep3_max, 1)
                link(dve.tensor_scalar(qsc, amx, 1.0 / 127.0, None, ALU.mult))
                link(dve.reciprocal(rqs, qsc))
                for i, w in enumerate((fcn, prn)):
                    link(dve.tensor_scalar(w, w, rqs[:, i:i + 1], ROUND, ALU.mult, ALU.add))
                    link(dve.tensor_scalar(w, w, -ROUND, 127.0, ALU.add, ALU.min))
                    dve.tensor_scalar(w, w, -128.0, qsc[:, i:i + 1], ALU.max, ALU.mult).then_inc(prep3_done, 1)

            def block_maximum(n, i, src):
                return dve.tensor_reduce(upmax[:, n, i:i + 1], src, AX.X, ALU.max, apply_absolute_value=True)

            def scale_of(n):
                dve.wait_ge(up_max, n + 1)
                link(dve.tensor_scalar(upback[:, n:n + 1], uprowall[:, n:n + 1], 2.0 ** -13, 2.0 ** -100,
                                       ALU.mult, ALU.max))
                dve.reciprocal(upscale[:, n:n + 1], upback[:, n:n + 1]).then_inc(up_scale, 1)

            def early(A):
                if A.n == 3:
                    loaded(dve, "l3")
                    dve.tensor_reduce(vmax[0:DC, 3:4], L3Wkv[:, 1024:2048], AX.X, ALU.max,
                                      apply_absolute_value=True).then_inc(vmax3_rows, 1)
                attention(A, ("early",))
                if A.n == 3:
                    prep3_operands()
                if A.n in prep:
                    evacuate_prep(A)

            def values_scale_and_ones(A):
                if A.n == 3:
                    dve.wait_ge(vmax3_max, 1)
                    value_scale(3, 4)
                if A.n != 2:
                    for kt in range(2 if A.dh == 64 else 2 * B):
                        one = vscale[:, A.n:A.n + 1].to_broadcast([P, 16])
                        link(dve.tensor_copy(Vheads(A, kt, VxH)[:, :, A.dh], one))
                        last = dve.tensor_tensor(Vheads(A, kt, VxL)[:, :, A.dh], one,
                                                 Vheads(A, kt, VxH)[:, :, A.dh], ALU.subtract)
                    last.then_inc(ones_set, 1)

            def evacuate_prep(A):
                r = prep[A.n]
                before = 0
                if A.n == 2:
                    before = len(PREP2_UP)
                    for n, (kind, k) in enumerate(PREP2_UP):
                        dve.wait_ge(prep2_high, n + 1)
                        w = 512 if k < 5 else 256
                        high, low = l2_parts(kind, k * 512, w)
                        dve.scalar_tensor_tensor(low, bank_of(n)[:, 0:w], upscale[:, 2:3], high,
                                                 ALU.mult, ALU.subtract).then_inc(prep2_low, 1)
                for n, (kind, k) in enumerate(PREP2 if A.n == 2 else PREP3):
                    if n % 2:
                        dve.wait_ge(r.filled, before + n + 1)
                        prep_evac(move, kind, k, bank_of(n)).then_inc(r.dve, 1)

            def attention(A, early=None):
                s = att_s[A.n]
                per_links = {0: 10, 1: 9, 2: 0, 3: 51}[A.n]
                start = count[0]
                nh = A.nh

                def body(b, kinds):
                    n = [0]

                    def chain(ins):
                        if A.n == 2 or kinds == "early":
                            return link(ins)
                        n[0] += 1
                        ins.then_inc(dve_chain, 1)
                        dve.wait_ge(dve_chain, b * per_links + (first_off(kinds) + n[0]))

                    for kind, k, m, base in steps(A, b, kinds):
                        if kinds == "early" and (kind, k) == ("v", 0):
                            values_scale_and_ones(A)
                        if A.n < 2 and kinds == "first" and kind == "softmax" and k >= 4:
                            t, lo, blocks = UP[A.n]
                            if k == 4:
                                loaded(dve, f"l{A.n}f")
                            if k < 4 + blocks:
                                last = block_maximum(A.n, k - 4, cols(t, lo + 512 * (k - 3), 512))
                            if k == 3 + blocks:
                                chain(last)
                                dve.tensor_reduce(uprow[:, A.n:A.n + 1], upmax[:, A.n, 0:blocks], AX.X,
                                                  ALU.max).then_inc(up_rows, 1)
                            if k == 15:
                                dve.wait_ge(up_max, A.n + 1)
                                chain(dve.tensor_scalar(upback[:, A.n:A.n + 1], uprowall[:, A.n:A.n + 1],
                                                        2.0 ** -13, 2.0 ** -100, ALU.mult, ALU.max))
                                dve.reciprocal(upscale[:, A.n:A.n + 1], upback[:, A.n:A.n + 1]).then_inc(up_scale, 1)
                        if kind == "softmax":
                            need(dve, s.scores, b * nh + (k + 1))
                            v = bank[k % 2][:, :].rearrange("p (q s) -> p q s", s=S)
                            nm = negm[:, k % 4, :]
                            if A.null:
                                if k == 0:
                                    need(dve, s.ring.dve, b * (BATCH_FILLS[A.n] // 2) + m // 2)
                                chain(dve.tensor_reduce(nm, v, AX.X, ALU.max, negate=True))
                                chain(dve.tensor_tensor(nm, nm, nsn[:, :, k], ALU.min))
                                dve.tensor_tensor(dn[:, k % 4, :], nm, nsn[:, :, k],
                                                  ALU.subtract).then_inc(s.negmax.sem, 1)
                            else:
                                dve.tensor_reduce(nm, v, AX.X, ALU.max, negate=True).then_inc(s.negmax.sem, 1)
                        elif kind == "low":
                            need(dve, s.pt[0], b * nh + (k + 1))
                            dve.tensor_tensor(PTl[:, k % 4, :], bank[2 + k % 2][:, :], PTh[:, k % 4, :],
                                              ALU.subtract).then_inc(s.pt[1].sem, 1)
                            if A.n < 2 and kinds == "last" and 0 <= k - 2 < UP[A.n][2]:
                                t, lo, _ = UP[A.n]
                                i = k - 2
                                high, low = block_parts(A.n, i)
                                dve.wait_ge(up_high, blocks_before(A.n) + i + 1)
                                dve.scalar_tensor_tensor(low, cols(t, lo + 512 * (i + 1), 512),
                                                         upscale[:, A.n:A.n + 1], high,
                                                         ALU.mult, ALU.subtract).then_inc(up_low, 1)
                        elif kind == "v" and A.n != 2 and m % 2:
                            need(dve, s.vhigh, b * v_count(A, 1) + v_done(A, b, kinds, m, 1))
                            v_low(A, dve, k, bank_of(m)).then_inc(s.ring.dve.sem, 1)
                        elif kind == "v" and A.n != 2:
                            need(dve, s.ring.filled, b * BATCH_FILLS[A.n] + (m + 1))
                            chain(v_high(A, move, k, bank_of(m)))
                            v_low(A, dve, k, bank_of(m)).then_inc(s.vlow.sem, 1)
                        elif kind == "turn" and A.n == 2 and k % 2:
                            need(dve, s.turn, b * nh + (k + 1))
                            need(dve, s.av, b * nh + (k - 3))
                            move(PTs[:, k % 4, :], bank[3][:, :]).then_inc(s.pt[1].sem, 1)
                        elif kind == "norm" and A.n == 2:
                            need(dve, s.av, k + 1)
                            o = bank[4 + k % 2][:, :].rearrange("p (q s) -> p q s", s=S)
                            chain(dve.reciprocal(rden[:, 0, 0, :], o[:, :, 128]))
                            at = 2 * (k % 2)
                            need(dve, s.yn, k - 1)
                            for qt in range(2):
                                last = dve.scalar_tensor_tensor(rtmp[:, at + qt, :], o[:, qt, 0:128],
                                                                rden[:, 0, 0, qt:qt + 1], bv_bc[:, :],
                                                                ALU.mult, ALU.add)
                            last.then_inc(s.norm.sem, 1)
                            need(dve, s.norm, k + 1)
                            chain(dve.tensor_tensor(xnew[:, at:at + 2, :], rtmp[:, at:at + 2, :],
                                                    x[:, 2 * k:2 * k + 2, :], ALU.add))
                            stats(xnew, 2, chain, s.stats.sem, None, at)
                            dve.tensor_copy(x[:, 2 * k:2 * k + 2, :], xnew[:, at:at + 2, :])
                        elif kind == "norm":
                            p = k % 8
                            need(dve, s.av, b * nh + (2 * k + 2))
                            o = bank[4 + p % 2][:, :].rearrange("p (h q e) -> p h q e", h=2, q=2)
                            rd = rden[:, p % 2, :, :]
                            if A.null:
                                pnv = pn[:, :, 2 * p:2 * p + 2].rearrange("p q h -> p h q")
                                sc = vscale[:, A.n:A.n + 1]
                                chain(dve.scalar_tensor_tensor(den[:, p % 2, :, :], pnv, sc, o[:, :, :, A.dh],
                                                               ALU.mult, ALU.add))
                                chain(dve.reciprocal(rd, den[:, p % 2, :, :]))
                                dve.scalar_tensor_tensor(
                                    On[:, :, 1024 + 2 * p:1026 + 2 * p].rearrange("p q h -> p h q"), pnv, sc, rd,
                                    ALU.mult, ALU.mult)
                            else:
                                chain(dve.reciprocal(rd, o[:, :, :, A.dh]))
                            dst = On[:, :, 2 * p * A.dh:(2 * p + 2) * A.dh]
                            dve.tensor_tensor(dst.rearrange("p q (h e) -> p h q e", h=2), o[:, :, :, 0:A.dh],
                                              rd.unsqueeze(3).to_broadcast([P, 2, 2, A.dh]),
                                              ALU.mult).then_inc(s.norm.sem, 1)
                        elif kind == "resid":
                            mw, bl = m - 1, b - 1
                            need(dve, s.ring.filled, b * BATCH_FILLS[A.n] + (mw + 1))
                            ps = bank_of(mw)[:, 0:S].rearrange("p (t d) -> p t d", d=D)
                            if A.null:
                                dve.tensor_copy(osb[:, :, :], ps).then_inc(s.ring.dve.sem, 1)
                                need(dve, s.ring.dve, b * (BATCH_FILLS[A.n] // 2) + mw // 2 + 1)
                                stats(osb, 2, chain, s.ostats.sem, mvo)
                            else:
                                if A.n == 0:
                                    dve.tensor_tensor(rtmp[:, 0:2, :], ps, bopen[:, :, :],
                                                      ALU.add).then_inc(s.ring.dve.sem, 1)
                                    need(dve, s.ring.dve, b * (BATCH_FILLS[A.n] // 2) + mw // 2 + 1)
                                    chain(dve.tensor_tensor(xnew[:, 0:2, :], rtmp[:, 0:2, :],
                                                            x[:, bass.ds(bl * 2, 2), :], ALU.add))
                                else:
                                    dve.tensor_tensor(xnew[:, 0:2, :], ps, x[:, bass.ds(bl * 2, 2), :],
                                                      ALU.add).then_inc(s.ring.dve.sem, 1)
                                    need(dve, s.ring.dve, b * (BATCH_FILLS[A.n] // 2) + mw // 2 + 1)
                                stats(xnew, 2, chain, s.stats.sem)
                                dve.tensor_copy(x[:, bass.ds(bl * 2, 2), :], xnew[:, 0:2, :])
                        elif kind == "resid2":
                            bl = b - 1
                            need(dve, s.onorm, bl + 1)
                            chain(dve.tensor_tensor(xnew[:, 0:2, :], osb[:, :, :], x[:, bass.ds(bl * 2, 2), :],
                                                    ALU.add))
                            stats(xnew, 2, chain, s.stats.sem)
                            dve.tensor_copy(x[:, bass.ds(bl * 2, 2), :], xnew[:, 0:2, :])
                        elif kind in FILLS and m % 2 and kind != "wo":
                            need(dve, s.ring.filled, b * BATCH_FILLS.get(A.n, 0) + (m + 1))
                            att_evac(A, move, kind, k, b, kinds, bank_of(m)).then_inc(s.ring.dve.sem, 1)
                    used[kinds] = n[0]

                used = {}

                def first_off(kinds):
                    if kinds in ("early", "prologue"):
                        return start
                    if kinds == "first":
                        return start + used["prologue"]
                    before = used["prologue"] + used["first"] - per_links
                    return start + before + (used["last"] - per_links if kinds == "epilogue" else 0)
                if early:
                    body(0, "early")
                    return
                batches(dve, A, body)
                if A.n != 2:
                    assert used["mid"] == per_links, (A.n, used, per_links)
                    count[0] = start + used["prologue"] + used["first"] + (B - 2) * used["mid"] + used["last"] + used["epilogue"]

            def feed_forward(F):
                s = ffn_s[F.n]
                if F.n == 1:
                    loaded(dve, "l2f")
                    for i, src in enumerate((n1, n3)):
                        last = block_maximum(2, i, src)
                    link(last)
                    dve.tensor_reduce(uprow[:, 2:3], upmax[:, 2, 0:2], AX.X, ALU.max).then_inc(up_rows, 1)
                    scale_of(2)
                per_links = {0: 11, 1: 8, 2: 11, 3: 0}[F.n]
                start = count[0]
                used = []

                def body(c, first):
                    n = [0]

                    def chain(ins):
                        n[0] += 1
                        ins.then_inc(dve_chain, 1)
                        dve.wait_ge(dve_chain, c * per_links + (start + n[0]))

                    for kind, k in ffn_schedule(F, first):
                        if kind == "gate" and k == 1:
                            need(dve, s.gl, c + 1)
                            src = bank[7][:, 0:32].rearrange("p (t e) -> p t e", e=8)
                            if F.n == 1:
                                ins = dve.tensor_tensor(lg[:, :, :], src,
                                                        swb_bc[:, :].unsqueeze(1).to_broadcast([P, 4, 8]), ALU.add)
                            else:
                                ins = dve.tensor_copy(lg[:, :, :], src)
                            ins.then_inc(s.gle.sem, 1)
                            need(dve, s.gle, c + 1)
                            plain(dve)
                            for t in range(4):
                                last = dve.max(mx[:, t, :], lg[:, t, :])
                            chain(last)
                            if F.k == 1:
                                dve.tensor_tensor(gd[:, :, :], lg[:, :, :],
                                                  mx[:, :, 0:1].to_broadcast([P, 4, 8]),
                                                  ALU.subtract).then_inc(s.gd.sem, 1)
                            else:
                                dve.tensor_tensor(gd[:, :, 0], mx[:, :, 1], mx[:, :, 0],
                                                  ALU.subtract).then_inc(s.gd.sem, 1)
                            plain(dve)
                            for t in range(4):
                                last = dve.max_index(mi[:, t, :], mx[:, t, :], lg[:, t, :])
                            chain(last)
                            chain(dve.tensor_copy(mif[:, :, :], mi[:, :, :]))
                            io = iota[:, :].unsqueeze(1).to_broadcast([P, 4, 8])
                            dve.tensor_tensor(oh1[:, :, :], io, mif[:, :, 1:2].to_broadcast([P, 4, 8]),
                                              ALU.is_equal)
                            chain(dve.tensor_tensor(oh0[:, :, :], io, mif[:, :, 0:1].to_broadcast([P, 4, 8]),
                                                    ALU.is_equal))
                        elif kind == "gate" and k == 2:
                            need(dve, s.gx, c + 1)
                            if F.k == 1:
                                chain(dve.tensor_reduce(gs[:, :], ge[:, :, :], AX.X, ALU.add))
                                chain(dve.reciprocal(gr[:, :], gs[:, :]))
                                dve.tensor_tensor(wpad[:, :, 0:8], oh0[:, :, :],
                                                  gr[:, :].unsqueeze(2).to_broadcast([P, 4, 8]),
                                                  ALU.mult).then_inc(s.w.sem, 1)
                                need(dve, s.w, c + 1)
                            else:
                                chain(dve.tensor_scalar(gs[:, :], ge[:, :, 0], 1.0, None, ALU.add))
                                chain(dve.reciprocal(gr[:, :], gs[:, :]))
                                chain(dve.tensor_tensor(gp[:, :], ge[:, :, 0], gr[:, :], ALU.mult))
                                dve.tensor_tensor(oh0[:, :, :], oh0[:, :, :],
                                                  gr[:, :].unsqueeze(2).to_broadcast([P, 4, 8]), ALU.mult)
                                chain(dve.tensor_tensor(oh1[:, :, :], oh1[:, :, :],
                                                        gp[:, :].unsqueeze(2).to_broadcast([P, 4, 8]), ALU.mult))
                                chain(dve.tensor_tensor(wpad[:, :, 0:8], oh0[:, :, :], oh1[:, :, :], ALU.add))
                        elif kind == "gate" and k == 3:
                            need(dve, s.wt, c + 1)
                            dve.tensor_copy(wTs[:, :], bank[7][:, :]).then_inc(s.wte.sem, 1)
                        elif kind == "up" and F.gated:
                            e, ft = k
                            u = e * F.FT + ft
                            M = F.last if ft == F.FT - 1 else P
                            need(dve, s.silu, c * F.U + (u + 1))
                            need(dve, s.y, c * F.E + (e - 1 if e >= 2 else 0))
                            dve.scalar_tensor_tensor(G[0:M, u % (2 * F.FT), :], bank[2 + u % 2][0:M, :],
                                                     upback[0:M, F.n:F.n + 1], sg[0:M, u % 2, :],
                                                     ALU.mult, ALU.mult).then_inc(s.g.sem, 1)
                        elif kind == "down":
                            e = k
                            need(dve, s.y, c * F.E + (e + 1))
                            Y = bank[4 + e % 2][:, :].rearrange("p (t d) -> p t d", d=D)
                            need(dve, s.acc, c * F.E + e)
                            if F.n == 3:
                                need(dve, s.stats, c)
                                last = dve.tensor_tensor(acc[:, :, :], Y,
                                                         bproj_bc[:, :].unsqueeze(1).to_broadcast([P, 4, D]), ALU.add)
                            elif e >= F.routed:
                                last = dve.tensor_tensor(acc[:, :, :], Y, acc[:, :, :], ALU.add)
                            else:
                                for t in range(4):
                                    w = wpad[:, t, e:e + 1]
                                    if e == 0:
                                        last = dve.tensor_scalar(acc[:, t, :], Y[:, t, :], w, None, ALU.mult)
                                    else:
                                        last = dve.scalar_tensor_tensor(acc[:, t, :], Y[:, t, :], w, acc[:, t, :],
                                                                        ALU.mult, ALU.add)
                            last.then_inc(s.acc.sem, 1)
                        elif kind == "fin":
                            need(dve, s.acc, c * F.E + F.E)
                            if F.n == 3:
                                dve.tensor_tensor(x[:, bass.ds(c * 4, 4), :], acc[:, :, :],
                                                  x[:, bass.ds(c * 4, 4), :], ALU.add).then_inc(s.stats.sem, 1)
                            else:
                                need(dve, s.yn, c)
                                chain(dve.tensor_tensor(xnew[:, :, :], acc[:, :, :], x[:, bass.ds(c * 4, 4), :],
                                                        ALU.add))
                                stats(xnew, 4, chain, s.stats.sem)
                                dve.tensor_copy(x[:, bass.ds(c * 4, 4), :], xnew[:, :, :])
                    used.append(n[0])
                    assert F.n == 3 or n[0] == per_links, (F.n, n[0])
                chunks(dve, F, body)
                count[0] = start + used[0] * NCH

            early(ATT[0])
            for n in range(4):
                attention(ATT[n])
                feed_forward(FFN[n])
                if n < 3:
                    early(ATT[n + 1])
                    boundary(dve, "dve", n + 2)


def kernel(**inputs):
    import concourse.bacc as _bacc
    from concourse.bass_utils import run_bass_kernel_spmd as _run

    nc = _bacc.Bacc("TRN2", target_bir_lowering=False, num_devices=1)
    arrays, args = {}, {}
    for name in inputs:
        v = np.ascontiguousarray(inputs[name])
        arrays[f"in_{name}"] = v
        args[name] = nc.dram_tensor(f"in_{name}", v.shape, mybir.dt.from_np(v.dtype), kind="ExternalInput").ap()
    out = nc.dram_tensor("out", (B, S, D), F32, kind="ExternalOutput").ap()
    build(nc, args, out)
    r = _run(nc, [arrays], core_ids=[0])
    return r.results[0]["out"]
```
